# Optimizing a Trainium2 kernel written in Bass

```python
import numpy as np
import jax
import jax.numpy as jnp

def _softmax(x, axis=-1):
    return jax.nn.softmax(x, axis=axis)

def _gelu(x):
    return jax.nn.gelu(x, approximate=True)

def _silu(x):
    return jax.nn.silu(x)

def _sigmoid(x):
    return jax.nn.sigmoid(x)

def _layernorm(x, axis=-1, eps=1e-05):
    m = jnp.mean(x, axis=axis, keepdims=True)
    v = jnp.var(x, axis=axis, keepdims=True)
    return (x - m) / jnp.sqrt(v + eps)

def _scatter_add(tgt, idx, src, axis=0):
    return tgt.at[idx].add(src)

def _segment_sum(src, seg, n):
    return jax.ops.segment_sum(src, seg, n)
kernel_name = 'mk_early_fusion_d1_tok_img1024_r4_4472e3'

def setup_inputs(seed: int=0):
    np.random.seed(seed)
    _w = jnp.asarray

    def _rec_inputs():
        import jax
        import jax.numpy as jnp
        _rk = jax.random.key(seed)
        x = -0.000222058 + 0.999998 * jax.random.normal(jax.random.fold_in(_rk, 1), (128, 3, 64, 64), jnp.float32)
        txt = 0.000354947 + 1.41246 * jax.random.normal(jax.random.fold_in(_rk, 2), (128, 32, 256), jnp.float32)
        return (x, txt)
    x, txt = _rec_inputs()

    def _L0_tok_setup():
        import jax, jax.numpy as jnp
        import numpy as np
        IMG, PS, C, OUT = (64, 16, 3, 256)
        NP = IMG // PS
        IN_FEAT = C * PS * PS
        key = jax.random.key(seed)
        k1, k2, k3, k4 = jax.random.split(key, 4)
        x = jax.random.normal(k1, (128, C, IMG, IMG), dtype=jnp.float32)
        W = jax.random.normal(k2, (OUT, IN_FEAT), dtype=jnp.float32) / np.sqrt(IN_FEAT)
        b = jax.random.normal(k3, (OUT,), dtype=jnp.float32) * 0.01
        pos_emb = jax.random.normal(k4, (NP * NP, OUT), dtype=jnp.float32)
        return {'x': x, 'W': W, 'b': b, 'pos_emb': pos_emb}
    _L0_tok_all = _L0_tok_setup()
    _L0_tok_in = {k: v for k, v in _L0_tok_all.items() if k in ('W', 'b', 'pos_emb')}
    del _L0_tok_all

    def _L0_attn_setup():
        import jax, jax.numpy as jnp
        import numpy as np
        B, T, D, R = (4, 512, 256, 64)
        key = jax.random.key(seed)
        ks = jax.random.split(key, 13)
        x = jax.random.normal(ks[0], (B, T, D), jnp.float32)
        WQ = jax.random.normal(ks[1], (D, D), jnp.float32) * 0.02
        WK = jax.random.normal(ks[2], (D, D), jnp.float32) * 0.02
        WO = jax.random.normal(ks[3], (D, D), jnp.float32) * 0.02
        Winv = jnp.eye(D, dtype=jnp.float32) + 0.01 * jax.random.normal(ks[4], (D, D), jnp.float32)
        U_b = jax.random.normal(ks[5], (D, R), jnp.float32) * 0.02
        V_b = jax.random.normal(ks[6], (D, R), jnp.float32) * 0.02
        W_b = jax.random.normal(ks[7], (D, R), jnp.float32) * 0.02
        bias_b = jnp.zeros((D,), jnp.float32)
        U_t = jax.random.normal(ks[8], (D, R), jnp.float32) * 0.02
        V_t = jax.random.normal(ks[9], (D, R), jnp.float32) * 0.02
        W_t = jax.random.normal(ks[10], (D, R), jnp.float32) * 0.02
        X_t = jax.random.normal(ks[11], (D, R), jnp.float32) * 0.02
        bias_t = jnp.zeros((D,), jnp.float32)
        alpha_bi = jnp.float32(0.5)
        alpha_tri = jnp.float32(0.5)
        return {'x': x, 'WQ': WQ, 'WK': WK, 'WO': WO, 'Winv': Winv, 'U_b': U_b, 'V_b': V_b, 'W_b': W_b, 'bias_b': bias_b, 'U_t': U_t, 'V_t': V_t, 'W_t': W_t, 'X_t': X_t, 'bias_t': bias_t, 'alpha_bi': alpha_bi, 'alpha_tri': alpha_tri}
    _L0_attn_all = _L0_attn_setup()
    _L0_attn_in = {k: v for k, v in _L0_attn_all.items() if k in ('WQ', 'WK', 'WO', 'Winv', 'U_b', 'V_b', 'W_b', 'bias_b', 'U_t', 'V_t', 'W_t', 'X_t', 'bias_t', 'alpha_bi', 'alpha_tri')}
    del _L0_attn_all

    def _L0_ffn_setup():
        import jax, jax.numpy as jnp
        import numpy as np
        B, S, D, E, K = (2, 512, 256, 8, 2)
        H = 4 * D
        key = jax.random.key(seed)
        ks = jax.random.split(key, 6)
        x = jax.random.normal(ks[0], (B, S, D), dtype=jnp.float32)
        lim_g = np.sqrt(6.0 / (D + E)).astype(np.float32)
        W_gate = jax.random.uniform(ks[1], (D, E), minval=-lim_g, maxval=lim_g, dtype=jnp.float32)
        lim1 = np.sqrt(1.0 / D).astype(np.float32)
        lim2 = np.sqrt(1.0 / H).astype(np.float32)
        W1 = jax.random.uniform(ks[2], (E, D, H), minval=-lim1, maxval=lim1, dtype=jnp.float32)
        b1 = jax.random.uniform(ks[3], (E, H), minval=-lim1, maxval=lim1, dtype=jnp.float32)
        W2 = jax.random.uniform(ks[4], (E, H, D), minval=-lim2, maxval=lim2, dtype=jnp.float32)
        b2 = jax.random.uniform(ks[5], (E, D), minval=-lim2, maxval=lim2, dtype=jnp.float32)
        return {'x': x, 'W_gate': W_gate, 'W1': W1, 'b1': b1, 'W2': W2, 'b2': b2}
    _L0_ffn_all = _L0_ffn_setup()
    _L0_ffn_in = {k: v for k, v in _L0_ffn_all.items() if k in ('W_gate', 'W1', 'b1', 'W2', 'b2')}
    del _L0_ffn_all
    return {'x': x, 'txt': txt, 'L0_tok_W': _L0_tok_in['W'], 'L0_tok_b': _L0_tok_in['b'], 'L0_tok_pos_emb': _L0_tok_in['pos_emb'], 'L0_attn_WQ': _L0_attn_in['WQ'], 'L0_attn_WK': _L0_attn_in['WK'], 'L0_attn_WO': _L0_attn_in['WO'], 'L0_attn_Winv': _L0_attn_in['Winv'], 'L0_attn_U_b': _L0_attn_in['U_b'], 'L0_attn_V_b': _L0_attn_in['V_b'], 'L0_attn_W_b': _L0_attn_in['W_b'], 'L0_attn_bias_b': _L0_attn_in['bias_b'], 'L0_attn_U_t': _L0_attn_in['U_t'], 'L0_attn_V_t': _L0_attn_in['V_t'], 'L0_attn_W_t': _L0_attn_in['W_t'], 'L0_attn_X_t': _L0_attn_in['X_t'], 'L0_attn_bias_t': _L0_attn_in['bias_t'], 'L0_attn_alpha_bi': _L0_attn_in['alpha_bi'], 'L0_attn_alpha_tri': _L0_attn_in['alpha_tri'], 'L0_ffn_W_gate': _L0_ffn_in['W_gate'], 'L0_ffn_W1': _L0_ffn_in['W1'], 'L0_ffn_b1': _L0_ffn_in['b1'], 'L0_ffn_W2': _L0_ffn_in['W2'], 'L0_ffn_b2': _L0_ffn_in['b2']}

def reference(x, txt, L0_tok_W, L0_tok_b, L0_tok_pos_emb, L0_attn_WQ, L0_attn_WK, L0_attn_WO, L0_attn_Winv, L0_attn_U_b, L0_attn_V_b, L0_attn_W_b, L0_attn_bias_b, L0_attn_U_t, L0_attn_V_t, L0_attn_W_t, L0_attn_X_t, L0_attn_bias_t, L0_attn_alpha_bi, L0_attn_alpha_tri, L0_ffn_W_gate, L0_ffn_W1, L0_ffn_b1, L0_ffn_W2, L0_ffn_b2):
    import jax
    import jax.numpy as jnp

    def _L0_tok_ref(x, W, b, pos_emb):
        import jax, jax.numpy as jnp
        import numpy as np
        IMG, PS, C, OUT = (64, 16, 3, 256)
        NP = IMG // PS
        IN_FEAT = C * PS * PS
        B = x.shape[0]
        p = x.reshape(B, C, NP, PS, NP, PS).transpose(0, 1, 2, 4, 3, 5)
        p = p.transpose(0, 2, 3, 1, 4, 5)
        p = p.reshape(B, NP * NP, IN_FEAT)
        out = jnp.einsum('bnf,of->bno', p, W) + b + pos_emb
        return out

    def _L0_attn_ref(x, WQ, WK, WO, Winv, U_b, V_b, W_b, bias_b, U_t, V_t, W_t, X_t, bias_t, alpha_bi, alpha_tri):
        import jax, jax.numpy as jnp
        import numpy as np
        B, T, D, R = (4, 512, 256, 64)
        Tlen = x.shape[1]
        Q = x @ WQ.T
        K = x @ WK.T
        invQ = Q @ Winv.T
        invK = K @ Winv.T
        counts = jnp.arange(1, Tlen + 1, dtype=x.dtype)[None, :, None]
        z = jnp.cumsum(x, axis=1) / counts
        fwd_r = Q @ V_b * jnp.cumsum(K @ W_b, axis=1)
        inv_r = jnp.cumsum(invK @ V_b, axis=1) * (invQ @ W_b)
        tri_r = Q @ V_t * jnp.cumsum(K @ W_t, axis=1) * (z @ X_t)
        sum_fwd = fwd_r @ U_b.T + counts * bias_b
        sum_inv = inv_r @ U_b.T + counts * bias_b
        sum_tri = tri_r @ U_t.T + counts * bias_t
        out = (sum_fwd + alpha_bi * sum_inv + alpha_tri * sum_tri) / counts
        return out @ WO.T

    def _L0_ffn_ref(x, W_gate, W1, b1, W2, b2):
        import jax, jax.numpy as jnp
        import numpy as np
        B, S, D, E, K = (2, 512, 256, 8, 2)
        H = 4 * D
        gate = jnp.einsum('bsd,de->bse', x, W_gate)
        kth = jax.lax.top_k(gate, K)[0][..., -1:]
        mask = jax.nn.softmax(jnp.where(gate >= kth, gate, -jnp.inf), axis=-1)
        h = jax.nn.relu(jnp.einsum('bsd,edh->bseh', x, W1) + b1)
        y = jnp.einsum('bseh,ehd->bsed', h, W2) + b2
        return (y * mask[..., None]).mean(axis=-2)
    h = _L0_tok_ref(x, L0_tok_W, L0_tok_b, L0_tok_pos_emb)
    h = jnp.concatenate([h, txt], axis=1)
    h = h + _L0_attn_ref(_layernorm(h, axis=-1), L0_attn_WQ, L0_attn_WK, L0_attn_WO, L0_attn_Winv, L0_attn_U_b, L0_attn_V_b, L0_attn_W_b, L0_attn_bias_b, L0_attn_U_t, L0_attn_V_t, L0_attn_W_t, L0_attn_X_t, L0_attn_bias_t, L0_attn_alpha_bi, L0_attn_alpha_tri)
    h = h + _L0_ffn_ref(_layernorm(h, axis=-1), L0_ffn_W_gate, L0_ffn_W1, L0_ffn_b1, L0_ffn_W2, L0_ffn_b2)
    return h

_drawn_inputs = setup_inputs


def setup_inputs(seed=0):
    import zlib

    import numpy as np

    out = dict(_drawn_inputs(seed))
    spreads = {'L0_attn_bias_b': (0.0, 2.0), 'L0_attn_bias_t': (0.0, 2.0)}
    factors = {'L0_tok_b': 8.0,
     'L0_attn_WQ': 8.0,
     'L0_attn_WK': 8.0,
     'L0_attn_Winv': 8.0,
     'L0_attn_U_b': 8.0,
     'L0_attn_V_b': 8.0,
     'L0_attn_W_b': 8.0,
     'L0_attn_U_t': 8.0,
     'L0_attn_V_t': 8.0,
     'L0_attn_W_t': 8.0,
     'L0_attn_X_t': 8.0,
     'L0_ffn_W_gate': 31.904,
     'L0_ffn_W1': 34.288,
     'L0_ffn_b1': 182.813,
     'L0_ffn_W2': 28.256,
     'L0_ffn_b2': 200.0}
    for name, (base, spread) in spreads.items():
        noise = np.random.default_rng([zlib.crc32(name.encode()), seed]).standard_normal(out[name].shape)
        drawn = base * np.exp(spread * noise) if base else spread * noise
        out[name] = jnp.asarray(drawn.astype(out[name].dtype))
    for name, factor in factors.items():
        out[name] = (out[name] * factor).astype(out[name].dtype)
    return out
```

```python
from contextlib import ExitStack

import concourse.bass as bass
from concourse import mybir

F32 = mybir.dt.float32
F32R = mybir.dt.float32r
I32 = mybir.dt.int32
ALU = mybir.AluOpType
ACT = mybir.ActivationFunctionType
AX = mybir.AxisListType

P = 128
D = 256
DC = D // P
R = 64
T_IMG = 16
STEPS = 48
FEAT = 768
FC = FEAT // P
GS = 4
GROUPS = STEPS // GS
IMG_GROUPS = T_IMG // GS
TOKENS = P * STEPS
E = 8
H = 1024
HC = H // P
TILE = 256
SUB = TILE // P
MIN_TILES = 2
PAD = MIN_TILES * TILE
CAP = TOKENS + PAD
LIST_ROWS = E * CAP
ROW = D + 1 + E
DUMP = P
EPS = 1e-5

C_ID, C_TRI, C_INV, C_TOK, C_CAP, C_STEP, C_END = 0, 128, 256, 304, 353, 361, 409
M_Q, M_K, M_TQ, M_TK, M_TX, M_END = 0, 128, 256, 320, 384, 448
TB_TILE, TB_PAD, TB_TIE, TB_LAST, TB_END = 0, 9, 17, 18, 26

ds = bass.ds


def waited(eng, sem):
    eng.sem_inc(sem, 1)


def build(nc, xp, txt, tok_wt, tok_b, pos, wq, wk, wot, winv, u_b, v_b, w_b, bias_b,
          u_t, v_t, w_t, x_t, bias_t, alpha_bi, alpha_tri, w_gate, w1, b1t, w2, b2, consts, out):
    lists = nc.dram_tensor("expert_lists", (LIST_ROWS, ROW), F32, kind="Internal").ap()
    out_steps = out[0:TOKENS, :].rearrange("(b t) d -> b t d", t=STEPS)
    txt_steps = txt
    w1_v = w1.rearrange("e (c p) h -> e p c h", p=P)
    w2_v = w2.rearrange("e (c p) d -> e p c d", p=P)

    with ExitStack() as common:
        def sb(name, shape, dt=F32, stack=common):
            return stack.enter_context(nc.sbuf_tensor(name, shape, dt))

        def sems(stack, *names):
            return [stack.enter_context(nc.semaphore(n)) for n in names]

        ps = [common.enter_context(nc.psum_tensor(f"bank{i}", [P, 512], F32)) for i in range(8)]
        cst = sb("cst", [P, C_END])
        ident = cst[:, C_ID:C_ID + P]
        table = sb("table", [1, 32], I32)
        w1h, w1l, w2hl = [sb("w1h0", [P, DC, H], F32R)], [sb("w1l0", [P, DC, H], F32R)], [
            sb("w2hl0", [P, HC, 2 * D], F32R)]
        w1raw = sb("w1raw", [P, DC, H])
        w2raw = sb("w2raw", [P, HC, D])
        (w_raw, w_high, w_low) = sems(common, "w_raw", "w_high", "w_low")

        def split_low(k):
            nc.gpsimd.tensor_tensor(w1l[k][:], w1raw[:], w1h[k][:].bitcast(F32), ALU.subtract).then_inc(w_low, 1)
            nc.gpsimd.tensor_tensor(w2hl[k][:, :, D:2 * D], w2raw[:], w2hl[k][:, :, 0:D].bitcast(F32),
                                    ALU.subtract).then_inc(w_low, 1)

        attention(nc, sb, sems, ps, cst, ident, table, lists, out, out_steps, txt_steps, xp, tok_wt, tok_b, pos,
                  wq, wk, wot, winv, u_b, v_b, w_b, bias_b, u_t, v_t, w_t, x_t, bias_t, alpha_bi,
                  alpha_tri, w_gate, w1_v, w2_v, consts, w1h, w2hl, w1raw, w2raw, w_raw, w_high, split_low)
        experts(nc, sb, sems, ps, ident, table, lists, out, w1_v, b1t, w2_v, b2, w1h, w1l, w2hl,
                w1raw, w2raw, w_raw, w_high, w_low, split_low)


def attention(nc, sb_, sems, ps, cst, ident, table, lists, out, out_steps, txt_steps, xp, tok_wt, tok_b, pos,
              wq, wk, wot, winv, u_b, v_b, w_b, bias_b, u_t, v_t, w_t, x_t, bias_t, alpha_bi,
              alpha_tri, w_gate, w1_v, w2_v, consts, w1h, w2hl, w1raw, w2raw, w_raw, w_high, split_low):
    with ExitStack() as st:
        def sb(name, shape, dt=F32):
            return sb_(name, shape, dt, st)

        h_all = sb("h_all", [P, STEPS, D])
        posb = h_all[:, 0:T_IMG, :]
        tokb = sb("tokb", [P, D])
        tokw = sb("tokw", [P, FC, D])
        px = [sb(f"px{i}", [P, GS, FC, P]) for i in range(2)]
        wq_s, wk_s, wi_s, wo_s = (sb(n, [P, DC, D]) for n in ("wq_s", "wk_s", "wi_s", "wo_s"))
        vw = sb("vw", [P, DC, 2 * R])
        rhs_q = sb("rhs_q", [P, DC, 3 * R])
        rhs_k = sb("rhs_k", [P, DC, 3 * R])
        xt_s = sb("xt_s", [P, DC, R])
        ub_s, ut_s = sb("ub_s", [P, DC, R]), sb("ut_s", [P, DC, R])
        uu1 = sb("uu1", [P, DC, 2 * R])
        uu2 = sb("uu2", [P, DC, R + 1])
        bias_s = sb("bias_s", [P, 2, DC])
        bias_m = sb("bias_m", [P, 2, DC])
        alpha = sb("alpha", [P, 3])
        wg_s = sb("wg_s", [P, DC, E])
        a_h, a_l = sb("a_h", [P, DC, M_END], F32R), sb("a_l", [P, DC, M_END], F32R)
        g1, g2 = sb("g1", [P, D]), sb("g2", [R + 1, D])
        ones = sb("ones", [P, P])
        rsq, eps = sb("rsq", [P, GS]), sb("eps", [P, GS])
        stats, mv, veps, nmean, rstd, shift = ([[sb(f"{name}{i}_{k}", [P, GS] + w) for k in range(2)] for i in (1, 2)]
                                               for name, w in (("stats", [6]), ("mv", [2]), ("veps", []),
                                                               ("nmean", []), ("rstd", []), ("shift", [])))
        xn = sb("xn", [P, GS, D])
        xth, xtl = sb("xth", [P, DC, GS * P], F32R), sb("xtl", [P, DC, GS * P], F32R)
        c1 = sb("c1", [P, GS, P])
        c6, c7 = sb("c6", [R, GS, P]), sb("c7", [R, GS, P])
        z = sb("z", [R, GS, P])
        r1 = [sb(f"r1_{i}", [P, GS, P]) for i in range(2)]
        r2 = [sb(f"r2_{i}", [R + 1, GS, P]) for i in range(2)]
        rows = [sb(f"rows{i}", [P, GS, ROW]) for i in range(2)]
        x2t = sb("x2t", [P, DC, GS * P])
        gate = sb("gate", [P, GS, E])
        top8 = sb("top8", [P, GS, E])
        gsub = sb("gsub", [P, GS, E])
        ex = sb("ex", [P, GS, E])
        exs = sb("exs", [P, GS, E])
        exsum, exinv = sb("exsum", [P, GS]), sb("exinv", [P, GS])
        sel = [sb(f"sel{i}", [P, GS + 1, E]) for i in range(2)]
        carry = sb("carry", [P, E])
        dest1 = sb("place1", [P, GS, E])
        rev0, rev = sb("rev_0", [P, GS, E]), sb("rev", [P, GS, E])
        seldest = sb("seldest", [P, STEPS, E])
        last1, first1 = sb("last1", [P, STEPS]), sb("first1", [P, STEPS])
        revmax = sb("revmax", [P, GS])
        dest = [sb(f"dest_{i}", [P, GS, 2], I32) for i in range(2)]
        pad = sb("pad", [P, PAD // P, ROW])
        cnt = sb("cnt", [1, 4, E + 1])
        cnti = sb("cnti", [1, 2, E], I32)
        tie_a, tie_b, tie_dest = (w[:].rearrange("p c n -> p (c n)")[:, 0:STEPS * E] for w in (wq_s, wk_s, wi_s))
        tie_a, tie_b, tie_dest = (v.rearrange("p (t e) -> p t e", e=E) for v in (tie_a, tie_b, tie_dest.bitcast(I32)))
        tie_first = sb("tie_first", [P, STEPS], I32)
        tie_row = sb("tie_row", [P, ROW])
        tie_idx = sb("tie_idx", [P, E + 1], I32)
        inv_t = cst[:, C_INV:C_INV + STEPS]

        bank_w, bank_p, bank_o, bank_g = ps[0:2], ps[2:5], ps[5:7], ps[7]

        (consts_in, setup_in, tok_in, pos_in, txt_in, px_in0, px_in1, stored, pads_out, zero_out) = sems(
            st, "consts_in", "setup_in", "tok_in", "pos_in", "txt_in", "px_in0", "px_in1", "stored",
            "pads_out", "zero_out")
        px_in = [px_in0, px_in1]
        (setup_dve, setup_pe, posb_ready, pool_const, pad_ready) = sems(
            st, "setup_dve", "setup_pe", "posb_ready", "pool_const", "pad_ready")
        (tok_done, h_sum, xn_ready, t1_done, xth_ready, xtl_ready, proj_done) = sems(
            st, "tok_done", "h_sum", "xn_ready", "t1_done", "xth_ready", "xtl_ready", "proj_done")
        stat_ready = sems(st, "stat1_ready", "stat2_ready")
        mv_ready = sems(st, "mv1_ready", "mv2_ready")
        ln_half = sems(st, "ln1_half", "ln2_half")
        rstd_ready = sems(st, "rstd1_ready", "rstd2_ready")
        ln_ready = sems(st, "ln1_ready", "ln2_ready")
        (c1_sum, c6_sum, c7_sum, z_ready, r1_ready, r2_ready, count_row, out_done, h2_ready) = sems(
            st, "c1_sum", "c6_sum", "c7_sum", "z_ready", "r1_ready", "r2_ready", "count_row", "out_done",
            "h2_ready")
        (x2_ready, t2_done, x2t_ready, gate_done, gate_copied, top_ready, sel_ready, gsub_ready) = sems(
            st, "x2_ready", "t2_done", "x2t_ready", "gate_done", "gate_copied", "top_ready", "sel_ready",
            "gsub_ready")
        (ex_ready, exs_ready, exsum_ready, exinv_ready, weight_ready) = sems(
            st, "ex_ready", "exs_ready", "exsum_ready", "exinv_ready", "weight_ready")
        (rank_done, dest1_ready, carry_ready, seldest_ready, rev0_ready, rev_ready, revmax_ready,
         last_ready, dest_ready, id_ready) = sems(
            st, "rank_done", "dest1_ready", "carry_ready", "seldest_ready", "rev0_ready", "rev_ready",
            "revmax_ready", "last_ready", "dest_ready", "id_ready")
        scattered = sems(st, "scattered0", "scattered1")
        (cnt_step, table_ready, tie_step, tie_ready, tie_copied, tie_moved) = sems(
            st, "cnt_step", "table_ready", "tie_step", "tie_ready", "tie_copied", "tie_moved")
        (pool_waited, dve_waited) = sems(st, "pool_waited", "dve_waited")
        N_SETUP = 19

        block = st.enter_context(nc.Block())

        @block.sync
        def _(sp):
            sp.dma_start(cst[:], consts).then_inc(consts_in, 16)
            sp.dma_start(px[0][:], xp[:, 0:GS]).then_inc(px_in[0], 16)
            sp.dma_start(tokw[:], tok_wt).then_inc(tok_in, 16)
            sp.dma_start(posb, pos.partition_broadcast(P)).then_inc(pos_in, 16)
            sp.dma_start(tokb[:], tok_b.partition_broadcast(P)).then_inc(pos_in, 16)
            sp.dma_start(px[1][:], xp[:, GS:2 * GS]).then_inc(px_in[1], 16)
            for g in range(2, IMG_GROUPS):
                sp.wait_ge(tok_done, 2 * (g - 1))
                sp.dma_start(px[g % 2][:], xp[:, GS * g:GS * g + GS]).then_inc(px_in[g % 2], 16)
            sp.dma_start(h_all[:, T_IMG:STEPS, :], txt_steps).then_inc(txt_in, 16)
            sp.dma_start(w1raw[:], w1_v[0]).then_inc(w_raw, 16)
            sp.dma_start(w2raw[:], w2_v[0]).then_inc(w_raw, 16)
            sp.wait_ge(pad_ready, 3)
            sp.dma_start(out[TOKENS:TOKENS + DUMP, :], pad[:, 0, 0:D]).then_inc(zero_out, 16)
            with sp.Fori(0, GROUPS) as g:
                sp.wait_ge(h2_ready, GS * g + GS)
                sp.dma_start(out_steps[:, ds(GS * g, GS), :], h_all[:, ds(GS * g, GS), :]).then_inc(stored, 16)
            sp.wait_ge(table_ready, 1)
            for e in range(E):
                row = sp.value_load(table[0:1, TB_PAD + e:TB_PAD + e + 1], min_val=e * CAP,
                                    max_val=e * CAP + TOKENS)
                sp.dma_start(lists[ds(row, PAD), :].rearrange("(k p) c -> p k c", p=P),
                             pad[:]).then_inc(pads_out, 16)
            sp.wait_ge(pads_out, 16 * E)
            sp.wait_ge(stored, 16 * GROUPS)
            sp.wait_ge(zero_out, 16)

        def pool_ln(pool, n, g, par):
            pool.wait_ge(mv_ready[n], GS * g + GS)
            nc.gpsimd.tensor_tensor(veps[n][par][:], mv[n][par][:, :, 1], eps[:], ALU.add).then_inc(ln_half[n], 1)
            nc.gpsimd.tensor_scalar(nmean[n][par][:], mv[n][par][:, :, 0], -1.0, None, ALU.mult).then_inc(ln_half[n], 1)
            pool.wait_ge(ln_half[n], 2 * g + 2)
            nc.gpsimd.tensor_tensor(rstd[n][par][:], veps[n][par][:], rsq[:], ALU.pow).then_inc(rstd_ready[n], 1)
            pool.wait_ge(rstd_ready[n], g + 1)
            nc.gpsimd.tensor_tensor(shift[n][par][:], nmean[n][par][:], rstd[n][par][:], ALU.mult).then_inc(ln_ready[n], 1)

        def pool_scatter(pool, g, par):
            if not isinstance(g, int) or g >= 2:
                pool.wait_ge(scattered[par], 64 * (g - par))
            nc.gpsimd.tensor_copy(rows[par][:, :, D], cst[:, ds(C_TOK + GS * g, GS)]).then_inc(id_ready, 1)
            pool.wait_ge(id_ready, g + 1)
            pool.wait_ge(x2_ready, GS * g + GS)
            pool.wait_ge(weight_ready, g + 1)
            pool.wait_ge(dest_ready, g + 1)
            waited(pool, pool_waited)
            for j in range(GS):
                for c in range(2):
                    nc.gpsimd.indirect_dma_start(
                        out=lists, out_offset=bass.IndirectOffsetOnAxis(ap=dest[par][:, j, c:c + 1], axis=0),
                        in_=rows[par][:, j, :], in_offset=None, bounds_check=LIST_ROWS - 1,
                        oob_is_err=False).then_inc(scattered[par], 16)

        @block.gpsimd
        def _(pool):
            nc.gpsimd.dma_start(w1h[0][:], w1_v[0]).then_inc(w_high, 16)
            nc.gpsimd.dma_start(w2hl[0][:, :, 0:D], w2_v[0]).then_inc(w_high, 16)
            nc.gpsimd.memset(ones[:], 1.0).then_inc(pool_const, 1)
            nc.gpsimd.memset(rsq[:], -0.5).then_inc(pool_const, 1)
            nc.gpsimd.memset(eps[:], EPS).then_inc(pool_const, 1)
            nc.gpsimd.memset(sel[0][:, GS, :], 0.0).then_inc(pool_const, 1)
            nc.gpsimd.memset(sel[1][:, GS, :], 0.0).then_inc(pool_const, 1)
            nc.gpsimd.memset(pad[:], 0.0).then_inc(pad_ready, 1)
            pool.wait_ge(pad_ready, 1)
            pool.wait_ge(consts_in, 16)
            for k in range(0, PAD // P, 2):
                nc.gpsimd.tensor_copy(pad[:, k:k + 2, D], cst[:, C_TOK + STEPS:C_TOK + STEPS + 1]
                                      .to_broadcast([P, 2])).then_inc(pad_ready, 1)
            pool.wait_ge(pos_in, 32)
            pool.wait_ge(pool_const, 5)
            for k in range(4):
                v = posb[:, GS * k:GS * k + GS, :]
                nc.gpsimd.tensor_tensor(v, v, tokb[:].unsqueeze(1).to_broadcast([P, GS, D]),
                                        ALU.add).then_inc(posb_ready, 1)
            pool_ln(pool, 0, 0, 0)
            pool_ln(pool, 0, 1, 1)

            def tick(g, par):
                if not isinstance(g, int) or 1 <= g <= GROUPS:
                    pool_ln(pool, 1, g - 1, 1 - par)
                if not isinstance(g, int) or 2 <= g:
                    pool_scatter(pool, g - 2, par)
                if not isinstance(g, int) or g + 2 < GROUPS:
                    pool_ln(pool, 0, g + 2, par)

            for g in range(IMG_GROUPS):
                tick(g, g % 2)
            with pool.Fori(IMG_GROUPS // 2, GROUPS // 2 - 1) as i:
                tick(2 * i, 0)
                tick(2 * i + 1, 1)
            pool.wait_ge(w_high, 32)
            pool.wait_ge(w_raw, 32)
            split_low(0)
            for g in range(GROUPS - 2, GROUPS + 2):
                tick(g, g % 2)
            for par in range(2):
                pool.wait_ge(scattered[par], 64 * GROUPS)
            pool.wait_ge(table_ready, 1)
            tie = pool.value_load(table[0:1, TB_TIE:TB_TIE + 1], min_val=0, max_val=1)
            with pool.If(tie > 0):
                pool.wait_ge(tie_ready, 2)
                with pool.Fori(0, STEPS) as t:
                    nc.gpsimd.tensor_copy(tie_idx[:, E:E + 1], tie_first[:, ds(t, 1)]).then_inc(tie_copied, 1)
                    nc.gpsimd.tensor_copy(tie_idx[:, 0:E], tie_dest[:, ds(t, 1), :].squeeze(1)
                                          ).then_inc(tie_copied, 1)
                    pool.wait_ge(tie_copied, 2 * t + 2)
                    waited(pool, pool_waited)
                    nc.gpsimd.indirect_dma_start(
                        out=tie_row[:], out_offset=None, in_=lists,
                        in_offset=bass.IndirectOffsetOnAxis(ap=tie_idx[:, E:E + 1], axis=0),
                        bounds_check=LIST_ROWS - 1, oob_is_err=False).then_inc(tie_moved, 16)
                    pool.wait_ge(tie_moved, 16 * (E + 1) * t + 16)
                    waited(pool, pool_waited)
                    for e in range(E):
                        nc.gpsimd.indirect_dma_start(
                            out=lists, out_offset=bass.IndirectOffsetOnAxis(ap=tie_idx[:, e:e + 1], axis=0),
                            in_=tie_row[:], in_offset=None, bounds_check=LIST_ROWS - 1,
                            oob_is_err=False).then_inc(tie_moved, 16)
                    pool.wait_ge(tie_moved, 16 * (E + 1) * t + 16 * (E + 1))

        def act_ln1(act, g, par):
            act.wait_ge(ln_ready[0], g + 1)
            if not isinstance(g, int) or g >= 1:
                act.wait_ge(t1_done, 2 * g)
            for j in range(GS):
                t = ds(GS * g + j, 1)
                nc.scalar.activation(xn[:, j, :], h_all[:, t, :].squeeze(1), ACT.Identity,
                                     bias=shift[0][par][:, j:j + 1], scale=rstd[0][par][:, j:j + 1]).then_inc(xn_ready, 1)

        def act_xt(act, g):
            for k in range(2):
                act.wait_ge(t1_done, 2 * g + k + 1)
                nc.scalar.copy(xth[:, :, 256 * k:256 * k + 256],
                               bank_w[k][:].rearrange("p (c n) -> p c n", c=DC)).then_inc(xth_ready, 1)

        def act_tail(act, g, par):
            act.wait_ge(ln_ready[1], g + 1)
            if not isinstance(g, int) or g >= 2:
                act.wait_ge(scattered[par], 64 * (g - par))
            for j in range(GS):
                t = ds(GS * g + j, 1)
                nc.scalar.activation(rows[par][:, j, 0:D], h_all[:, t, :].squeeze(1), ACT.Identity,
                                     bias=shift[1][par][:, j:j + 1], scale=rstd[1][par][:, j:j + 1]).then_inc(x2_ready, 1)
            for k in range(2):
                act.wait_ge(t2_done, 2 * g + k + 1)
                nc.scalar.copy(x2t[:, :, 256 * k:256 * k + 256],
                               bank_w[k][:].rearrange("p (c n) -> p c n", c=DC)).then_inc(x2t_ready, 1)

        @block.scalar
        def _(act):
            act.dma_start(wi_s[:], winv.rearrange("(c p) n -> p c n", p=P)).then_inc(setup_in, 16)
            act.dma_start(vw[:, :, 0:R], v_b.rearrange("(c p) n -> p c n", p=P)).then_inc(setup_in, 16)
            act.dma_start(vw[:, :, R:2 * R], w_b.rearrange("(c p) n -> p c n", p=P)).then_inc(setup_in, 16)
            act.dma_start(wq_s[:], wq.rearrange("(c p) n -> p c n", p=P)).then_inc(setup_in, 16)
            act.dma_start(wk_s[:], wk.rearrange("(c p) n -> p c n", p=P)).then_inc(setup_in, 16)
            for dst, c0, src in ((rhs_q, 0, v_b), (rhs_q, 2 * R, v_t), (rhs_k, 0, w_b), (rhs_k, 2 * R, w_t),
                                 (xt_s, 0, x_t), (ub_s, 0, u_b), (ut_s, 0, u_t)):
                act.dma_start(dst[:, :, c0:c0 + R], src.rearrange("(c p) n -> p c n", p=P)).then_inc(setup_in, 16)
            act.dma_start(wo_s[:], wot.rearrange("(c p) n -> p c n", p=P)).then_inc(setup_in, 16)
            act.dma_start(wg_s[:], w_gate.rearrange("(c p) n -> p c n", p=P)).then_inc(setup_in, 16)
            act.dma_start(bias_s[:, 0, :], bias_b).then_inc(setup_in, 16)
            act.dma_start(bias_s[:, 1, :], bias_t).then_inc(setup_in, 16)
            act.dma_start(alpha[:, 0:1], alpha_bi.partition_broadcast(P)).then_inc(setup_in, 16)
            act.dma_start(alpha[:, 1:2], alpha_tri.partition_broadcast(P)).then_inc(setup_in, 16)
            act.dma_start(alpha[:, 2:3], alpha_bi.partition_broadcast(P)).then_inc(setup_in, 16)
            act_ln1(act, 0, 0)
            act_xt(act, 0)
            act_ln1(act, 1, 1)

            def tick(g, par):
                if not isinstance(g, int) or 1 <= g <= GROUPS:
                    act_tail(act, g - 1, 1 - par)
                if not isinstance(g, int) or g + 1 < GROUPS:
                    act_xt(act, g + 1)
                if not isinstance(g, int) or g < GROUPS:
                    if not isinstance(g, int) or g >= 2:
                        act.wait_ge(out_done, 2 * (g - 1))
                    act.wait_ge(consts_in, 16)
                    nc.scalar.copy(r2[par][R:R + 1, :, :],
                                   cst[R:R + 1, ds(C_STEP + GS * g, GS)].unsqueeze(2).to_broadcast([1, GS, P])
                                   ).then_inc(count_row, 1)
                if not isinstance(g, int) or 1 <= g <= GROUPS:
                    act.wait_ge(gsub_ready, g)
                    if not isinstance(g, int) or g >= 2:
                        act.wait_ge(exs_ready, g - 1)
                    nc.scalar.activation(ex[:], gsub[:], ACT.Exp).then_inc(ex_ready, 1)
                if not isinstance(g, int) or g + 2 < GROUPS:
                    act_ln1(act, g + 2, par)

            for g in range(IMG_GROUPS):
                tick(g, g % 2)
            with act.Fori(IMG_GROUPS // 2, GROUPS // 2 - 1) as i:
                tick(2 * i, 0)
                tick(2 * i + 1, 1)
            for g in range(GROUPS - 2, GROUPS + 1):
                tick(g, g % 2)

        def dve_stats(dve, n, g, par):
            for j in range(GS):
                t = GS * g + j
                nc.vector.bn_stats(stats[n][par][:, j, :], h_all[:, ds(t, 1), :].squeeze(1)
                                   ).then_inc(stat_ready[n], 1)
            dve.wait_ge(stat_ready[n], GS * g + GS)
            waited(dve, dve_waited)
            for j in range(GS):
                nc.vector.bn_aggr(mv[n][par][:, j, :], stats[n][par][:, j, :]
                                  ).then_inc(mv_ready[n], 1)

        def dve_tok(dve, g):
            dve.wait_ge(posb_ready, g + 1)
            for k in range(2):
                dve.wait_ge(tok_done, 2 * g + k + 1)
                s = slice(GS * g + 2 * k, GS * g + 2 * k + 2)
                nc.vector.tensor_tensor(h_all[:, s, :], bank_w[k][:].rearrange("p (s d) -> p s d", s=2),
                                        posb[:, s, :], ALU.add).then_inc(h_sum, 1)
            dve.wait_ge(h_sum, 2 * g + 2)

        def dve_xt(dve, g):
            for k in range(2):
                dve.wait_ge(xth_ready, 2 * g + k + 1)
                s = slice(256 * k, 256 * k + 256)
                nc.vector.tensor_tensor(xtl[:, :, s], bank_w[k][:].rearrange("p (c n) -> p c n", c=DC),
                                        xth[:, :, s].bitcast(F32), ALU.subtract).then_inc(xtl_ready, 1)

        def dve_h2(dve, g, par):
            for j in range(GS):
                t = GS * g + j
                dve.wait_ge(out_done, 2 * g + j // 2 + 1)
                v = h_all[:, ds(t, 1), :].squeeze(1)
                nc.vector.scalar_tensor_tensor(v, bank_o[j // 2][:, D * (j % 2):D * (j % 2) + D],
                                               cst[:, ds(C_INV + t, 1)], v, ALU.mult, ALU.add).then_inc(h2_ready, 1)
            dve.wait_ge(h2_ready, GS * g + GS)
            waited(dve, dve_waited)
            dve_stats(dve, 1, g, par)

        def dve_factors(dve, g, par):
            def psum(n, rows_=P):
                return bank_p[n][0:rows_, :].rearrange("p (s b) -> p s b", s=GS)

            dve.wait_ge(proj_done, 5 * g + 1)
            for j in range(GS):
                dve.wait_ge(c1_sum, GS * g + j + 1)
                nc.vector.tensor_tensor(c1[:, j, :], psum(0)[:, j, :], c1[:, (j - 1) % GS, :],
                                        ALU.add).then_inc(c1_sum, 1)
            dve.wait_ge(proj_done, 5 * g + 2)
            dve.wait_ge(c1_sum, GS * g + GS + 1)
            nc.vector.tensor_tensor(r1[par][:], psum(1), c1[:], ALU.mult).then_inc(r1_ready, 1)
            for j in range(GS):
                dve.wait_ge(proj_done, 5 * g + 3)
                dve.wait_ge(c6_sum, GS * g + j + 1)
                nc.vector.tensor_tensor(c6[:, j, :], psum(2, R)[:, j, :], c6[:, (j - 1) % GS, :],
                                        ALU.add).then_inc(c6_sum, 1)
                dve.wait_ge(proj_done, 5 * g + 4)
                dve.wait_ge(c7_sum, GS * g + j + 1)
                nc.vector.tensor_tensor(c7[:, j, :], psum(0, R)[:, j, :], c7[:, (j - 1) % GS, :],
                                        ALU.add).then_inc(c7_sum, 1)
            for j in range(GS):
                dve.wait_ge(c6_sum, GS * g + j + 2)
                dve.wait_ge(c7_sum, GS * g + j + 2)
                nc.vector.scalar_tensor_tensor(z[:, j, :], c7[:, j, :], cst[0:R, ds(C_INV + GS * g + j, 1)],
                                               c6[:, j, :], ALU.mult, ALU.mult).then_inc(z_ready, 1)
            dve.wait_ge(proj_done, 5 * g + 5)
            dve.wait_ge(z_ready, GS * g + GS)
            nc.vector.tensor_tensor(r2[par][0:R, :, :], psum(1, R), z[:], ALU.mult).then_inc(r2_ready, 1)

        def dve_choose(dve, g, par):
            dve.wait_ge(gate_done, g + 1)
            nc.vector.tensor_copy(gate[:], bank_g[:, 0:GS * E].rearrange("p (s e) -> p s e", s=GS)
                                  ).then_inc(gate_copied, 1)
            dve.wait_ge(gate_copied, g + 1)
            waited(dve, dve_waited)
            for j in range(GS):
                nc.vector.max(top8[:, j, :], gate[:, j, :]).then_inc(top_ready, 1)
            dve.wait_ge(top_ready, GS * g + GS)
            nc.vector.tensor_tensor(sel[par][:, 0:GS, :], gate[:], top8[:, :, 1:2].to_broadcast([P, GS, E]),
                                    ALU.is_ge).then_inc(sel_ready, 1)
            if not isinstance(g, int) or g >= 1:
                dve.wait_ge(ex_ready, g)
            nc.vector.tensor_tensor(gsub[:], gate[:], top8[:, :, 0:1].to_broadcast([P, GS, E]),
                                    ALU.subtract).then_inc(gsub_ready, 1)

        def dve_route(dve, g, par):
            s = ds(GS * g, GS)
            dve.wait_ge(ex_ready, g + 1)
            nc.vector.tensor_tensor(exs[:], ex[:], sel[par][:, 0:GS, :], ALU.mult).then_inc(exs_ready, 1)
            dve.wait_ge(rank_done, g + 1)
            ranks = bank_g[:, 64:64 + (GS + 1) * E].rearrange("p (s e) -> p s e", s=GS + 1)
            dve.wait_ge(carry_ready, g + 1)
            nc.vector.tensor_tensor(dest1[:], ranks[:, 0:GS, :], carry[:].unsqueeze(1).to_broadcast([P, GS, E]),
                                    ALU.add).then_inc(dest1_ready, 1)
            dve.wait_ge(exs_ready, g + 1)
            nc.vector.reduce_sum(exsum[:], exs[:], AX.X).then_inc(exsum_ready, 1)
            dve.wait_ge(dest1_ready, g + 1)
            nc.vector.tensor_tensor(carry[:], ranks[:, GS, :], carry[:], ALU.add).then_inc(carry_ready, 1)
            nc.vector.tensor_tensor(seldest[:, s, :], dest1[:], sel[par][:, 0:GS, :], ALU.mult
                                    ).then_inc(seldest_ready, 1)
            nc.vector.tensor_scalar(rev0[:], dest1[:], -1.0, float(LIST_ROWS + 1), ALU.mult, ALU.add
                                    ).then_inc(rev0_ready, 1)
            dve.wait_ge(exsum_ready, g + 1)
            nc.vector.reciprocal(exinv[:], exsum[:]).then_inc(exinv_ready, 1)
            dve.wait_ge(rev0_ready, g + 1)
            nc.vector.tensor_tensor(rev[:], rev0[:], sel[par][:, 0:GS, :], ALU.mult).then_inc(rev_ready, 1)
            dve.wait_ge(seldest_ready, g + 1)
            nc.vector.reduce_max(last1[:, s], seldest[:, s, :], AX.X).then_inc(last_ready, 1)
            dve.wait_ge(exinv_ready, g + 1)
            if not isinstance(g, int) or g >= 2:
                dve.wait_ge(scattered[par], 64 * (g - par))
            nc.vector.scalar_tensor_tensor(rows[par][:, :, D + 1:ROW], exs[:], 1.0 / E,
                                           exinv[:].unsqueeze(2).to_broadcast([P, GS, E]), ALU.mult,
                                           ALU.mult).then_inc(weight_ready, 1)
            dve.wait_ge(rev_ready, g + 1)
            nc.vector.reduce_max(revmax[:], rev[:], AX.X).then_inc(revmax_ready, 1)
            dve.wait_ge(last_ready, g + 1)
            nc.vector.tensor_scalar(dest[par][:, :, 1], last1[:, s], -1.0, None, ALU.add)
            dve.wait_ge(revmax_ready, g + 1)
            nc.vector.tensor_scalar(first1[:, s], revmax[:], -1.0, float(LIST_ROWS + 1), ALU.mult, ALU.add)
            nc.vector.tensor_scalar(dest[par][:, :, 0], revmax[:], -1.0, float(LIST_ROWS), ALU.mult, ALU.add
                                    ).then_inc(dest_ready, 1)

        @block.vector
        def _(dve):
            n = [0]

            def step(ins):
                n[0] += 1
                ins.then_inc(setup_dve, 1)

            nc.vector.memset(c1[:, GS - 1, :], 0.0).then_inc(c1_sum, 1)
            nc.vector.memset(c6[:, GS - 1, :], 0.0).then_inc(c6_sum, 1)
            nc.vector.memset(c7[:, GS - 1, :], 0.0).then_inc(c7_sum, 1)
            dve.wait_ge(consts_in, 16)
            nc.vector.tensor_copy(carry[:], cst[:, C_CAP:C_CAP + E]).then_inc(carry_ready, 1)
            dve_tok(dve, 0)
            dve_stats(dve, 0, 0, 0)
            dve.wait_ge(setup_in, 16 * N_SETUP)
            step(nc.vector.tensor_copy(uu1[:, :, 0:R], ub_s[:]))
            step(nc.vector.tensor_scalar(uu1[:, :, R:2 * R], ub_s[:], alpha[:, 0:1], None, ALU.mult))
            step(nc.vector.tensor_scalar(uu2[:, :, 0:R], ut_s[:], alpha[:, 1:2], None, ALU.mult))
            step(nc.vector.tensor_scalar(bias_m[:, 0, :], bias_s[:, 1, :], alpha[:, 1:2], None, ALU.mult))
            dve.wait_ge(setup_dve, n[0])
            step(nc.vector.tensor_tensor(bias_m[:, 1, :], bias_s[:, 0, :], bias_m[:, 0, :], ALU.add))
            dve.wait_ge(setup_dve, n[0])
            step(nc.vector.scalar_tensor_tensor(uu2[:, :, R], bias_s[:, 0, :], alpha[:, 2:3],
                                                bias_m[:, 1, :], ALU.mult, ALU.add))
            step(nc.vector.tensor_copy(a_h[:, :, M_TX:M_END], xt_s[:]))
            dve.wait_ge(setup_dve, n[0])
            step(nc.vector.tensor_tensor(a_l[:, :, M_TX:M_END], xt_s[:], a_h[:, :, M_TX:M_END].bitcast(F32),
                                         ALU.subtract))
            dve.wait_ge(setup_pe, 1)
            iv = bank_p[0][:, 0:256].rearrange("p (c n) -> p c n", c=DC)
            step(nc.vector.tensor_copy(rhs_k[:, :, R:2 * R], iv[:, :, 0:R]))
            step(nc.vector.tensor_copy(rhs_q[:, :, R:2 * R], iv[:, :, R:2 * R]))
            for m in range(DC):
                dve.wait_ge(setup_pe, 2 + m)
                q, k = bank_p[1 + m][:, 0:192], bank_p[1 + m][:, 192:384]
                for dst, src in ((M_Q, q[:, 0:128]), (M_K, k[:, 0:128]), (M_TQ, q[:, 128:192]),
                                 (M_TK, k[:, 128:192])):
                    w = src.shape[1]
                    step(nc.vector.tensor_copy(a_h[:, m, dst:dst + w], src))
                    dve.wait_ge(setup_dve, n[0])
                    step(nc.vector.tensor_tensor(a_l[:, m, dst:dst + w], src, a_h[:, m, dst:dst + w].bitcast(F32),
                                                 ALU.subtract))
            dve.wait_ge(setup_pe, 4)
            step(nc.vector.tensor_copy(g1[:], bank_o[0][:, 0:D]))
            step(nc.vector.tensor_copy(g2[:], bank_o[1][0:R + 1, 0:D]))
            dve_xt(dve, 0)
            dve_tok(dve, 1)
            dve_stats(dve, 0, 1, 1)

            def tick(g, par):
                if not isinstance(g, int) or 1 <= g <= GROUPS:
                    dve_h2(dve, g - 1, 1 - par)
                if not isinstance(g, int) or g >= 2:
                    dve_route(dve, g - 2, par)
                if not isinstance(g, int) or g < GROUPS:
                    dve_factors(dve, g, par)
                if not isinstance(g, int) or g + 1 < GROUPS:
                    dve_xt(dve, g + 1)
                if not isinstance(g, int) or 1 <= g <= GROUPS:
                    dve_choose(dve, g - 1, 1 - par)
                if isinstance(g, int) and g + 2 < IMG_GROUPS:
                    dve_tok(dve, g + 2)
                if not isinstance(g, int) or g + 2 < GROUPS:
                    if not isinstance(g, int) or g + 2 >= IMG_GROUPS:
                        dve.wait_ge(txt_in, 16)
                    dve_stats(dve, 0, g + 2, par)

            for g in range(IMG_GROUPS):
                tick(g, g % 2)
            with dve.Fori(IMG_GROUPS // 2, GROUPS // 2 - 1) as i:
                tick(2 * i, 0)
                tick(2 * i + 1, 1)
            for g in range(GROUPS - 2, GROUPS + 2):
                tick(g, g % 2)

            m = [0]

            def count(ins):
                m[0] += 1
                ins.then_inc(cnt_step, 1)
                dve.wait_ge(cnt_step, m[0])

            dve.wait_ge(carry_ready, GROUPS + 1)
            nf, nt, tile0 = cnt[:, 0, 0:E], cnt[:, 1, 0:E], cnt[:, 2, :]
            count(nc.vector.tensor_tensor(nf, carry[0:1, :], cst[0:1, C_CAP:C_CAP + E], ALU.subtract))
            count(nc.vector.tensor_scalar(cnti[:, 0, :], nf, float(TILE - 1), None, ALU.add))
            count(nc.vector.tensor_scalar(cnti[:, 1, :], cnti[:, 0, :], TILE.bit_length() - 1, None,
                                          ALU.arith_shift_right))
            count(nc.vector.tensor_scalar(nt, cnti[:, 1, :], float(MIN_TILES), None, ALU.max))
            count(nc.vector.memset(tile0[:, 0:1], 0.0))
            for e in range(E):
                count(nc.vector.tensor_tensor(tile0[:, e + 1:e + 2], tile0[:, e:e + 1], nt[:, e:e + 1], ALU.add))
            count(nc.vector.reduce_sum(cnt[:, 3, 0:1], nf, AX.X))
            count(nc.vector.tensor_copy(table[:, TB_TILE:TB_TILE + E + 1], tile0))
            count(nc.vector.tensor_scalar(table[:, TB_LAST:TB_LAST + E], tile0[:, 1:E + 1], -1.0, None, ALU.add))
            count(nc.vector.tensor_scalar(table[:, TB_PAD:TB_PAD + E], carry[0:1, :], -1.0, None, ALU.add))
            nc.vector.tensor_scalar(table[:, TB_TIE:TB_TIE + 1], cnt[:, 3, 0:1], float(2 * TOKENS), None,
                                    ALU.is_gt).then_inc(table_ready, 1)
            dve.wait_ge(table_ready, 1)
            tie = dve.value_load(table[0:1, TB_TIE:TB_TIE + 1], min_val=0, max_val=1)
            with dve.If(tie > 0):
                for a, edge in ((tie_a, first1), (tie_b, last1)):
                    nc.vector.tensor_tensor(a, seldest[:], edge[:].unsqueeze(2).to_broadcast([P, STEPS, E]),
                                            ALU.not_equal).then_inc(tie_step, 1)
                dve.wait_ge(tie_step, 2)
                nc.vector.tensor_tensor(tie_a, tie_a, tie_b, ALU.mult).then_inc(tie_step, 1)
                dve.wait_ge(tie_step, 3)
                nc.vector.tensor_tensor(tie_b, tie_a, seldest[:], ALU.mult).then_inc(tie_step, 1)
                dve.wait_ge(tie_step, 4)
                nc.vector.tensor_scalar(tie_a, tie_b, 0.0, float(LIST_ROWS + 2), ALU.is_equal,
                                        ALU.mult).then_inc(tie_step, 1)
                dve.wait_ge(tie_step, 5)
                nc.vector.scalar_tensor_tensor(tie_dest, tie_b, -1.0, tie_a, ALU.add, ALU.add
                                               ).then_inc(tie_ready, 1)
                nc.vector.tensor_scalar(tie_first[:], first1[:], -1.0, None, ALU.add).then_inc(tie_ready, 1)

        def pe_tok(pe, g):
            pe.wait_ge(px_in[g % 2], 16 * (g // 2 + 1))
            pe.wait_ge(tok_in, 16)
            for k in range(2):
                if g >= 1:
                    pe.wait_ge(xtl_ready, 2 * (g - 1) + k + 1)
                for jj in range(2):
                    for c in range(FC):
                        last = nc.tensor.matmul(bank_w[k][:, D * jj:D * jj + D], px[g % 2][:, 2 * k + jj, c, :],
                                                tokw[:, c, :], start=(c == 0), stop=(c == FC - 1))
                last.then_inc(tok_done, 1)

        def pe_t1(pe, g):
            for k in range(2):
                pe.wait_ge(xn_ready, GS * g + 2 * k + 2)
                if isinstance(g, int) and g < 2:
                    pe.wait_ge(h_sum, 2 * g + k + 1)
                if not isinstance(g, int) or g >= 2:
                    pe.wait_ge(x2t_ready, 2 * (g - 2) + k + 1)
                for jj in range(2):
                    for c in range(DC):
                        last = nc.tensor.transpose(bank_w[k][:, 256 * c + P * jj:256 * c + P * jj + P],
                                                   xn[:, 2 * k + jj, P * c:P * c + P], ident)
                last.then_inc(t1_done, 1)

        def pe_t2(pe, g, par):
            for k in range(2):
                pe.wait_ge(x2_ready, GS * g + 2 * k + 2)
                pe.wait_ge(xtl_ready, 2 * (g + 1) + k + 1 if not isinstance(g, int) or g + 1 < GROUPS
                           else 2 * GROUPS)
                if isinstance(g, int) and g + 2 < IMG_GROUPS:
                    pe.wait_ge(h_sum, 2 * (g + 2) + k + 1)
                for jj in range(2):
                    for c in range(DC):
                        last = nc.tensor.transpose(bank_w[k][:, 256 * c + P * jj:256 * c + P * jj + P],
                                                   rows[par][:, 2 * k + jj, P * c:P * c + P], ident)
                last.then_inc(t2_done, 1)

        def pe_proj(pe, g):
            pe.wait_ge(xth_ready, 2 * g + 2)
            pe.wait_ge(xtl_ready, 2 * g + 2)
            chunks = ((0, M_K, P), (1, M_Q, P), (2, M_TK, R), (0, M_TX, R), (1, M_TQ, R))
            freed = ((c7_sum, GS * g + 1), (r2_ready, g), (c6_sum, GS * g + 1), (c1_sum, GS * g + GS + 1),
                     (r1_ready, g + 1))
            for n, (bank, col, m) in enumerate(chunks):
                if not (isinstance(g, int) and g == 0 and n < 3):
                    pe.wait_ge(*freed[n])
                for c in range(DC):
                    for i, (a, x) in enumerate(((a_h, xth), (a_h, xtl), (a_l, xth))):
                        last = nc.tensor.matmul(bank_p[bank][0:m, :], a[:, c, col:col + m], x[:, c, :],
                                                start=(c == 0 and i == 0), stop=(c == DC - 1 and i == 2))
                last.then_inc(proj_done, 1)

        def pe_out(pe, g, par):
            pe.wait_ge(r1_ready, g + 1)
            pe.wait_ge(r2_ready, g + 1)
            pe.wait_ge(count_row, g + 1)
            for k in range(2):
                if not isinstance(g, int) or g >= 1:
                    pe.wait_ge(h2_ready, GS * (g - 1) + 2 * k + 2)
                for jj in range(2):
                    o = bank_o[k][:, D * jj:D * jj + D]
                    nc.tensor.matmul(o, r1[par][:, 2 * k + jj, :], g1[:], start=True, stop=False)
                    last = nc.tensor.matmul(o, r2[par][:, 2 * k + jj, :], g2[:], start=False, stop=True)
                last.then_inc(out_done, 1)

        def pe_gate(pe, g):
            pe.wait_ge(x2t_ready, 2 * g + 2)
            if not isinstance(g, int) or g >= 1:
                pe.wait_ge(gate_copied, g)
                pe.wait_ge(carry_ready, g + 1)
            for j in range(GS):
                for c in range(DC):
                    last = nc.tensor.matmul(bank_g[:, E * j:E * j + E], x2t[:, c, P * j:P * j + P], wg_s[:, c, :],
                                            start=(c == 0), stop=(c == DC - 1))
            last.then_inc(gate_done, 1)

        def pe_rank(pe, g, par):
            pe.wait_ge(sel_ready, g + 1)
            if not isinstance(g, int) or g >= 1:
                pe.wait_ge(carry_ready, g + 1)
            nc.tensor.matmul(bank_g[:, 64:64 + (GS + 1) * E], cst[:, C_TRI:C_TRI + P],
                             sel[par][:].rearrange("p s e -> p (s e)"), start=True, stop=False)
            for j in range(GS):
                later = GS - j
                last = nc.tensor.matmul(
                    bank_g[:, 64 + (j + 1) * E:64 + (GS + 1) * E].rearrange("p (s e) -> p s e", e=E), ones[:],
                    sel[par][:, j:j + 1, :].to_broadcast([P, later, E]), start=False, stop=(j == GS - 1))
            last.then_inc(rank_done, 1)

        @block.tensor
        def _(pe):
            pe.wait_ge(consts_in, 16)
            pe.wait_ge(pool_const, 5)
            pe_tok(pe, 0)
            pe.wait_ge(setup_in, 16 * N_SETUP)
            for m in range(DC):
                for c in range(DC):
                    last = nc.tensor.matmul(bank_p[0][:, P * m:P * m + P], wi_s[:, c, P * m:P * m + P], vw[:, c, :],
                                            start=(c == 0), stop=(c == DC - 1))
            last.then_inc(setup_pe, 1)
            pe_t1(pe, 0)
            pe.wait_ge(setup_dve, 10)
            for m in range(DC):
                for o, w, rhs in ((0, wq_s, rhs_q), (192, wk_s, rhs_k)):
                    for c in range(DC):
                        last = nc.tensor.matmul(bank_p[1 + m][:, o:o + 192], w[:, c, P * m:P * m + P], rhs[:, c, :],
                                                start=(c == 0), stop=(c == DC - 1))
                last.then_inc(setup_pe, 1)
            for o, m, u in ((bank_o[0], P, uu1), (bank_o[1], R + 1, uu2)):
                for c in range(DC):
                    last = nc.tensor.matmul(o[0:m, 0:D], u[:, c, :], wo_s[:, c, :], start=(c == 0),
                                            stop=(c == DC - 1))
            last.then_inc(setup_pe, 1)
            pe_tok(pe, 1)
            pe.wait_ge(setup_dve, 28)

            def tick(g, par):
                if not isinstance(g, int) or 1 <= g <= GROUPS:
                    pe_out(pe, g - 1, 1 - par)
                if not isinstance(g, int) or g >= 2:
                    pe_rank(pe, g - 2, par)
                if not isinstance(g, int) or g < GROUPS:
                    pe_proj(pe, g)
                if not isinstance(g, int) or 1 <= g <= GROUPS:
                    pe_t2(pe, g - 1, 1 - par)
                if not isinstance(g, int) or g + 1 < GROUPS:
                    pe_t1(pe, g + 1)
                if not isinstance(g, int) or 1 <= g <= GROUPS:
                    pe_gate(pe, g - 1)
                if isinstance(g, int) and g + 2 < IMG_GROUPS:
                    pe_tok(pe, g + 2)

            for g in range(IMG_GROUPS):
                tick(g, g % 2)
            with pe.Fori(IMG_GROUPS // 2, GROUPS // 2 - 1) as i:
                tick(2 * i, 0)
                tick(2 * i + 1, 1)
            for g in range(GROUPS - 2, GROUPS + 2):
                tick(g, g % 2)


def experts(nc, sb_, sems, ps, ident, table, lists, out, w1_v, b1t, w2_v, b2, w1h, w1l, w2hl,
            w1raw, w2raw, w_raw, w_high, w_low, split_low):
    with ExitStack() as st:
        def sb(name, shape, dt=F32):
            return sb_(name, shape, dt, st)

        w1h.append(sb("w1h1", [P, DC, H], F32R))
        w1l.append(sb("w1l1", [P, DC, H], F32R))
        w2hl.append(sb("w2hl1", [P, HC, 2 * D], F32R))
        b1_s = sb("b1_s", [P, E * HC])
        b2_s = sb("b2_s", [P, E, D])
        xe = sb("xe", [P, SUB, ROW])
        xh, xl = sb("xh", [P, DC, TILE], F32R), sb("xl", [P, DC, TILE], F32R)
        hid = sb("hid", [P, 4, TILE])
        hh, hl = sb("hh", [P, HC, TILE], F32R), sb("hl", [P, HC, TILE], F32R)
        meta_n = sb("meta_n", [P, SUB, 1 + E])
        meta_w = sb("meta_w", [P, SUB, 1 + E])
        meta_i = sb("meta_i", [P, SUB], I32)
        y1 = sb("y1", [P, SUB, D])
        y2 = sb("y2", [P, SUB, D])
        y = sb("y", [P, SUB, D])
        bank_s, bank_y, bank_x = ps[0:4], ps[4:6], ps[6]

        (bias_in, xe_in, transposed, xh_ready, xl_ready, s1_done, hh_ready, hid_ready, hl_ready) = sems(
            st, "bias_in", "xe_in", "transposed", "xh_ready", "xl_ready", "s1_done", "hh_ready", "hid_ready",
            "hl_ready")
        (y_done, y1_ready, y2_ready, y_ready, added, y_free, meta_next, meta_ready) = sems(
            st, "y_done", "y1_ready", "y2_ready", "y_ready", "added", "y_free", "meta_next", "meta_ready")

        (sp_waited, pool_waited, pe_waited) = sems(st, "sp_waited", "pool_waited_2", "pe_waited")
        block = st.enter_context(nc.Block())
        MAX_TILES = E * (TOKENS // TILE) + E

        def tile_of(eng, e):
            return eng.value_load(table[0:1, ds(TB_TILE + e, 1)], min_val=0, max_val=MAX_TILES)

        def each_expert(eng, head, tile, before_last=None):
            with eng.Fori(0, E // 2) as i:
                for k in range(2):
                    e = 2 * i + k
                    t0 = tile_of(eng, e)
                    t1 = tile_of(eng, e + 1)
                    head(e, k)
                    if before_last is None:
                        with eng.Fori(t0, t1) as t:
                            tile(t, e, k, t0)
                    else:
                        last = eng.value_load(table[0:1, ds(TB_LAST + e, 1)], min_val=1, max_val=MAX_TILES)
                        with eng.Fori(t0, last) as t:
                            tile(t, e, k, t0)
                        before_last(e, k)
                        tile(last, e, k, t0)

        def following(i2):
            return (i2 + 1) % E

        @block.sync
        def _(sp):
            sp.dma_start(b1_s[:], b1t).then_inc(bias_in, 16)
            sp.dma_start(b2_s[:], b2.partition_broadcast(P)).then_inc(bias_in, 16)

            def head(e, k):
                sp.wait_ge(w_low, 2 * e + 2)
                n = following(e)
                sp.dma_start(w1raw[:], w1_v[ds(n, 1)].squeeze(0)).then_inc(w_raw, 16)
                sp.dma_start(w2raw[:], w2_v[ds(n, 1)].squeeze(0)).then_inc(w_raw, 16)

            def tile(t, e, k, t0):
                sp.wait_ge(transposed, t + 1)
                sp.wait_ge(meta_next, t + 1)
                row = nc.s_assert_within(
                    e * CAP + (t - t0) * TILE, 0, LIST_ROWS - TILE,
                    skip_runtime_bounds_check_because="an expert has at most CAP // TILE tiles")
                sp.dma_start(xe[:], lists[ds(row, TILE), :].rearrange("(s p) c -> p s c", p=P)
                             ).then_inc(xe_in, 16)

            each_expert(sp, head, tile)
            total = tile_of(sp, E)
            sp.wait_ge(transposed, total + 1)
            sp.wait_ge(meta_next, total + 1)
            sp.dma_start(xe[:], lists[0:TILE, :].rearrange("(s p) c -> p s c", p=P)).then_inc(xe_in, 16)
            sp.wait_ge(xe_in, 16 * total + 16)
            sp.wait_ge(bias_in, 32)
            waited(sp, sp_waited)

        @block.gpsimd
        def _(pool):
            def take_next(t1):
                pool.wait_ge(xe_in, 16 * t1)
                waited(pool, pool_waited)
                nc.gpsimd.tensor_copy(meta_n[:], xe[:, :, D:ROW]).then_inc(meta_next, 1)
                pool.wait_ge(meta_next, t1 + 1)

            def use_next():
                nc.gpsimd.tensor_copy(meta_w[:], meta_n[:]).then_inc(meta_ready, 1)
                nc.gpsimd.tensor_copy(meta_i[:], meta_n[:, :, 0]).then_inc(meta_ready, 1)

            pool.sem_inc(meta_next, 1)
            pool.sem_inc(y_free, SUB)
            take_next(1)
            use_next()

            def head(e, k):
                n = following(e)
                nc.gpsimd.dma_start(w1h[1 - k][:], w1_v[ds(n, 1)].squeeze(0)).then_inc(w_high, 16)
                nc.gpsimd.dma_start(w2hl[1 - k][:, :, 0:D], w2_v[ds(n, 1)].squeeze(0)).then_inc(w_high, 16)

            def before_last(e, k):
                pool.wait_ge(w_high, 32 * e + 64)
                pool.wait_ge(w_raw, 32 * e + 64)
                split_low(1 - k)

            def tile(t, e, k, t0):
                pool.wait_ge(meta_ready, 2 * t + 2)
                take_next(t + 2)
                for s in range(SUB):
                    pool.wait_ge(y_ready, SUB * t + s + 1)
                    waited(pool, pool_waited)
                    nc.gpsimd.indirect_dma_start(
                        out=out, out_offset=bass.IndirectOffsetOnAxis(ap=meta_i[:, s:s + 1], axis=0),
                        in_=y[:, s, :], in_offset=None, bounds_check=TOKENS + DUMP - 1, oob_is_err=True,
                        compute_op=ALU.add).then_inc(added, 16)
                    pool.wait_ge(added, 16 * (SUB * t + s + 1))
                    pool.sem_inc(y_free, 1)
                use_next()

            each_expert(pool, head, tile, before_last)

        @block.scalar
        def _(act):
            act.sem_inc(hh_ready, HC)
            def high_x(t1):
                act.wait_ge(transposed, t1 + 1)
                nc.scalar.copy(xh[:], bank_x[:].rearrange("p (c n) -> p c n", c=DC)).then_inc(xh_ready, 1)

            high_x(1)
            act.wait_ge(bias_in, 32)

            def tile(t, e, k, t0):
                for c in range(HC):
                    if c % 2 == 0:
                        act.wait_ge(s1_done, HC // 2 * t + c // 2 + 1)
                    nc.scalar.activation(hh[:, c, :], bank_s[c // 2][:, TILE * (c % 2):TILE * (c % 2) + TILE],
                                         ACT.Relu, bias=b1_s[:, ds(e * HC + c, 1)]).then_inc(hh_ready, 1)
                high_x(t + 2)
                act.wait_ge(meta_ready, 2 * t + 2)
                for s in range(SUB):
                    act.wait_ge(y_done, SUB * t + s + 1)
                    nc.scalar.activation(y1[:, s, :], bank_y[s][:, D:2 * D], ACT.Copy,
                                         scale=meta_w[:, s, ds(1 + e, 1)]).then_inc(y1_ready, 1)

            each_expert(act, lambda e, k: None, tile)

        @block.vector
        def _(dve):
            dve.sem_inc(hid_ready, HC)
            dve.sem_inc(y2_ready, SUB)

            def low_x(t1):
                dve.wait_ge(xh_ready, t1)
                nc.vector.tensor_tensor(xl[:], bank_x[:].rearrange("p (c n) -> p c n", c=DC),
                                        xh[:].bitcast(F32), ALU.subtract).then_inc(xl_ready, 1)

            low_x(1)
            dve.wait_ge(bias_in, 32)

            def tile(t, e, k, t0):
                def hidden(c):
                    if c % 2 == 0:
                        dve.wait_ge(hh_ready, HC * (t + 1) + c + 2)
                    nc.vector.tensor_scalar(hid[:, c % 4, :], bank_s[c // 2][:, TILE * (c % 2):TILE * (c % 2) + TILE],
                                            b1_s[:, ds(e * HC + c, 1)], 0.0, ALU.add, ALU.max).then_inc(hid_ready, 1)

                def low_hidden(c):
                    dve.wait_ge(hid_ready, HC * (t + 1) + c + 1)
                    nc.vector.tensor_tensor(hl[:, c, :], hid[:, c % 4, :], hh[:, c, :].bitcast(F32),
                                            ALU.subtract).then_inc(hl_ready, 1)

                hidden(0)
                for c in range(1, HC):
                    hidden(c)
                    low_hidden(c - 1)
                low_hidden(HC - 1)
                low_x(t + 2)
                for s in range(SUB):
                    w = meta_w[:, s, ds(1 + e, 1)]
                    dve.wait_ge(y1_ready, SUB * t + s + 1)
                    nc.vector.scalar_tensor_tensor(y2[:, s, :], bank_y[s][:, 0:D], w, y1[:, s, :], ALU.mult,
                                                   ALU.add).then_inc(y2_ready, 1)
                for s in range(SUB):
                    w = meta_w[:, s, ds(1 + e, 1)]
                    dve.wait_ge(y2_ready, SUB * (t + 1) + s + 1)
                    dve.wait_ge(y_free, SUB * t + s + 1)
                    nc.vector.scalar_tensor_tensor(y[:, s, :], b2_s[:, ds(e, 1), :].squeeze(1), w, y2[:, s, :],
                                                   ALU.mult, ALU.add).then_inc(y_ready, 1)

            each_expert(dve, lambda e, k: None, tile)

        @block.tensor
        def _(pe):
            pe.sem_inc(transposed, 1)

            def transpose(t1):
                pe.wait_ge(xe_in, 16 * t1)
                for c in range(DC):
                    for s in range(SUB):
                        last = nc.tensor.transpose(bank_x[:, TILE * c + P * s:TILE * c + P * s + P],
                                                   xe[:, s, P * c:P * c + P], ident)
                last.then_inc(transposed, 1)

            transpose(1)

            def head(e, k):
                pe.wait_ge(w_low, 2 * e + 2)
                waited(pe, pe_waited)

            def tile(t, e, k, t0):
                pe.wait_ge(xh_ready, t + 1)
                pe.wait_ge(xl_ready, t + 1)
                for c in range(HC):
                    if c % 2 == 0:
                        pe.wait_ge(hid_ready, HC * t + c + 2)
                    for d in range(DC):
                        for i, (w, x) in enumerate(((w1h[k], xh), (w1h[k], xl), (w1l[k], xh))):
                            last = nc.tensor.matmul(bank_s[c // 2][:, TILE * (c % 2):TILE * (c % 2) + TILE],
                                                    w[:, d, P * c:P * c + P], x[:, d, :],
                                                    start=(d == 0 and i == 0), stop=(d == DC - 1 and i == 2))
                    if c % 2 == 1:
                        last.then_inc(s1_done, 1)
                transpose(t + 2)
                for s in range(SUB):
                    pe.wait_ge(y2_ready, SUB * t + s + 1)
                    for c in range(HC):
                        if s == 0:
                            pe.wait_ge(hl_ready, HC * t + c + 1)
                        nc.tensor.matmul(bank_y[s][:], hh[:, c, P * s:P * s + P], w2hl[k][:, c, :],
                                         start=(c == 0), stop=False)
                        last = nc.tensor.matmul(bank_y[s][:, 0:D], hl[:, c, P * s:P * s + P], w2hl[k][:, c, 0:D],
                                                start=False, stop=(c == HC - 1))
                    last.then_inc(y_done, 1)

            each_expert(pe, head, tile)


def kernel(**inputs):
    import numpy as np
    import concourse.bacc as bacc
    from concourse.bass_utils import run_bass_kernel_spmd

    def a(name):
        return np.ascontiguousarray(inputs[name])

    x = a("x").reshape(P, 3, 4, 16, 4, 16).transpose(2, 4, 1, 3, 5, 0)
    x = x.reshape(T_IMG, FC, P, P).transpose(2, 0, 1, 3)
    consts = np.zeros((P, C_END), np.float32)
    consts[:, C_ID:C_ID + P] = np.eye(P)
    consts[:, C_TRI:C_TRI + P] = np.triu(np.ones((P, P)), 1)
    consts[:, C_INV:C_INV + STEPS] = 1.0 / np.arange(1, STEPS + 1)
    consts[:, C_TOK:C_TOK + STEPS] = np.arange(TOKENS).reshape(P, STEPS)
    consts[:, C_TOK + STEPS] = TOKENS + np.arange(P)
    consts[:, C_CAP:C_CAP + E] = np.arange(E) * CAP + 1
    consts[:, C_STEP:C_STEP + STEPS] = np.arange(1, STEPS + 1)
    L, A, M = "L0_tok_", "L0_attn_", "L0_ffn_"
    data = {
        "xp": x, "txt": a("txt"),
        "tok_wt": a(L + "W").T.reshape(FC, P, D).transpose(1, 0, 2),
        "tok_b": a(L + "b"), "pos": a(L + "pos_emb"),
        "wq": a(A + "WQ"), "wk": a(A + "WK"), "wot": a(A + "WO").T, "winv": a(A + "Winv"),
        "u_b": a(A + "U_b"), "v_b": a(A + "V_b"), "w_b": a(A + "W_b"),
        "bias_b": a(A + "bias_b").reshape(DC, P).T,
        "u_t": a(A + "U_t"), "v_t": a(A + "V_t"), "w_t": a(A + "W_t"), "x_t": a(A + "X_t"),
        "bias_t": a(A + "bias_t").reshape(DC, P).T,
        "alpha_bi": a(A + "alpha_bi").reshape(1), "alpha_tri": a(A + "alpha_tri").reshape(1),
        "w_gate": a(M + "W_gate"), "w1": a(M + "W1"),
        "b1t": a(M + "b1").reshape(E, HC, P).transpose(2, 0, 1).reshape(P, E * HC),
        "w2": a(M + "W2"), "b2": a(M + "b2"), "consts": consts,
    }
    data = {k: np.ascontiguousarray(v) for k, v in data.items()}
    nc = bacc.Bacc("TRN2", target_bir_lowering=False, num_devices=1)
    args = [nc.dram_tensor(f"in_{k}", v.shape, mybir.dt.from_np(v.dtype), kind="ExternalInput").ap()
            for k, v in data.items()]
    out = nc.dram_tensor("out", (TOKENS + DUMP, D), F32, kind="ExternalOutput").ap()
    build(nc, *args, out)
    got = run_bass_kernel_spmd(nc, [{f"in_{k}": v for k, v in data.items()}], core_ids=[0])
    return got.results[0]["out"][0:TOKENS].reshape(P, STEPS, D)
```

```python
from contextlib import ExitStack

import concourse.bass as bass
from concourse import mybir

F32 = mybir.dt.float32
F32R = mybir.dt.float32r
I32 = mybir.dt.int32
ALU = mybir.AluOpType
ACT = mybir.ActivationFunctionType
AX = mybir.AxisListType

P = 128
D = 256
DC = D // P
R = 64
T_IMG = 16
STEPS = 48
FEAT = 768
FC = FEAT // P
GS = 4
GROUPS = STEPS // GS
IMG_GROUPS = T_IMG // GS
TOKENS = P * STEPS
E = 8
H = 1024
HC = H // P
TILE = 256
SUB = TILE // P
PAD = TILE
CAP = TOKENS + PAD
LIST_ROWS = E * CAP
ROW = D + 1 + E
DUMP = P
EPS = 1e-5

C_ID, C_TRI, C_INV, C_TOK, C_CAP, C_STEP, C_END = 0, 128, 256, 304, 353, 361, 409
M_Q1, M_K1, M_K2, M_Q2, M_END = 0, 128, 256, 384, 448
TB_TILE, TB_PAD, TB_TIE, TB_FULL, TB_END = 0, 9, 17, 18, 26

ds = bass.ds


def waited(eng, sem):
    eng.sem_inc(sem, 1)


def build(nc, xp, txt, tok_wt, tok_b, pos, wq, wk, wot, winv, u_b, v_b, w_b, bias_b,
          u_t, v_t, w_t, x_t, bias_t, alpha_bi, alpha_tri, w_gate, w1, b1t, w2, b2, consts, out):
    lists = nc.dram_tensor("expert_lists", (LIST_ROWS, ROW), F32, kind="Internal").ap()
    out_steps = out[0:TOKENS, :].rearrange("(b t) d -> b t d", t=STEPS)
    txt_steps = txt
    w1_v = w1.rearrange("e (c p) h -> e p c h", p=P)
    w2_v = w2.rearrange("e (c p) d -> e p c d", p=P)

    with ExitStack() as common:
        def sb(name, shape, dt=F32, stack=common):
            return stack.enter_context(nc.sbuf_tensor(name, shape, dt))

        def sems(stack, *names):
            return [stack.enter_context(nc.semaphore(n)) for n in names]

        ps = [common.enter_context(nc.psum_tensor(f"bank{i}", [P, 512], F32)) for i in range(8)]
        cst = sb("cst", [P, C_END])
        ident = cst[:, C_ID:C_ID + P]
        table = sb("table", [1, 32], I32)
        w1h, w1l, w2hl = [sb("w1h0", [P, DC, H], F32R)], [sb("w1l0", [P, DC, H], F32R)], [
            sb("w2hl0", [P, HC, 2 * D], F32R)]
        w1raw = sb("w1raw", [P, DC, H])
        w2raw = sb("w2raw", [P, HC, D])
        b1_s = sb("b1_s", [P, E * HC])
        b2_s = sb("b2_s", [P, 2, D])
        (w_raw, w_high, w_low, b1_in, b2_in) = sems(common, "w_raw", "w_high", "w_low", "b1_in", "b2_in")

        def split_low(eng, k):
            eng.tensor_tensor(w1l[k][:], w1raw[:], w1h[k][:].bitcast(F32), ALU.subtract).then_inc(w_low, 1)
            eng.tensor_tensor(w2hl[k][:, :, D:2 * D], w2raw[:], w2hl[k][:, :, 0:D].bitcast(F32),
                              ALU.subtract).then_inc(w_low, 1)

        attention(nc, sb, sems, ps, cst, ident, table, lists, out, out_steps, txt_steps, xp, tok_wt, tok_b, pos,
                  wq, wk, wot, winv, u_b, v_b, w_b, bias_b, u_t, v_t, w_t, x_t, bias_t, alpha_bi,
                  alpha_tri, w_gate, w1_v, w2_v, b1t, b2, consts, w1h, w2hl, w1raw, w2raw, b1_s, b2_s, w_raw, w_high,
                  b1_in, b2_in, split_low)
        experts(nc, sb, sems, ps, ident, table, lists, out, w1_v, w2_v, b2, w1h, w1l, w2hl,
                w1raw, w2raw, b1_s, b2_s, w_raw, w_high, w_low, b1_in, b2_in, split_low)


def attention(nc, sb_, sems, ps, cst, ident, table, lists, out, out_steps, txt_steps, xp, tok_wt, tok_b, pos,
              wq, wk, wot, winv, u_b, v_b, w_b, bias_b, u_t, v_t, w_t, x_t, bias_t, alpha_bi,
              alpha_tri, w_gate, w1_v, w2_v, b1t, b2, consts, w1h, w2hl, w1raw, w2raw, b1_s, b2_s, w_raw, w_high,
                  b1_in, b2_in, split_low):
    with ExitStack() as st:
        def sb(name, shape, dt=F32):
            return sb_(name, shape, dt, st)

        h_all = sb("h_all", [P, STEPS, D])
        posb = h_all[:, 0:T_IMG, :]
        tokb = sb("tokb", [P, D])
        tokw = sb("tokw", [P, FC, D])
        px = [sb(f"px{i}", [P, GS, FC, P]) for i in range(2)]
        wq_s, wk_s, wi_s, wo_s = (sb(n, [P, DC, D]) for n in ("wq_s", "wk_s", "wi_s", "wo_s"))
        vw = sb("vw", [P, DC, 2 * R])
        rhs_q = sb("rhs_q", [P, DC, 3 * R])
        rhs_k = sb("rhs_k", [P, DC, 3 * R])
        xt_s = sb("xt_s", [P, DC, R])
        ub_s, ut_s = sb("ub_s", [P, DC, R]), sb("ut_s", [P, DC, R])
        uu = sb("uu", [P, DC, 2 * R])
        bias_col = sb("bias_col", [P, DC])
        bias_s = sb("bias_s", [P, 2, DC])
        bias_m = sb("bias_m", [P, 2, DC])
        alpha = sb("alpha", [P, 2])
        wg_s = sb("wg_s", [P, DC, E])
        a_h, a_l = sb("a_h", [P, DC, M_END], F32R), sb("a_l", [P, DC, M_END], F32R)
        g_out = sb("g_out", [P, D])
        g_bias = sb("g_bias", [1, 2, D], F32R)
        ones = sb("ones", [P, P])
        rsq, eps = sb("rsq", [P, GS]), sb("eps", [P, GS])
        rstd2, shift2 = sb("rstd2", [P, STEPS]), sb("shift2", [P, STEPS])
        weights = sb("weights", [P, STEPS, E])
        stats, mv, veps, nmean, rstd, shift = ([[sb(f"{name}{i}_{k}", [P, GS] + w) for k in range(2)] for i in (1, 2)]
                                               for name, w in (("stats", [6]), ("mv", [2]), ("veps", []),
                                                               ("nmean", []), ("rstd", []), ("shift", [])))
        xn = sb("xn", [P, GS, D])
        xth, xtl = sb("xth", [P, DC, GS * P], F32R), sb("xtl", [P, DC, GS * P], F32R)
        c1 = sb("c1", [P, GS, P])
        c2 = sb("c2", [P, GS, P])
        inverse = sb("inverse", [R, GS, P])
        factors = [sb(f"factors{i}", [P, GS, P]) for i in range(2)]
        count_row = [sb(f"count_row{i}", [1, GS, P], F32R) for i in range(2)]
        rows = [sb(f"rows{i}", [P, GS, ROW]) for i in range(2)]
        x2t = sb("x2t", [P, DC, GS * P])
        gate = sb("gate", [P, GS, E])
        top8 = sb("top8", [P, GS, E])
        gsub = sb("gsub", [P, GS, E])
        ex = sb("ex", [P, GS, E])
        exs = sb("exs", [P, GS, E])
        exsum, exinv = sb("exsum", [P, GS]), sb("exinv", [P, GS])
        sel = [sb(f"sel{i}", [P, GS + 1, E]) for i in range(2)]
        carry = sb("carry", [P, E])
        dest1 = sb("place1", [P, GS, E])
        rev0, rev = sb("rev_0", [P, GS, E]), sb("rev", [P, GS, E])
        seldest = sb("seldest", [P, STEPS, E])
        last1, first1 = sb("last1", [P, STEPS]), sb("first1", [P, STEPS])
        revmax = sb("revmax", [P, GS])
        dest = [sb(f"dest_{i}", [P, GS, 2], I32) for i in range(2)]
        pad = sb("pad", [P, PAD // P, ROW])
        cnt = sb("cnt", [1, 6, E + 1])
        cnti = sb("cnti", [1, 4, E], I32)
        tie_a, tie_b, tie_dest = (w[:].rearrange("p c n -> p (c n)")[:, 0:STEPS * E] for w in (wq_s, wk_s, wi_s))
        tie_a, tie_b, tie_dest = (v.rearrange("p (t e) -> p t e", e=E) for v in (tie_a, tie_b, tie_dest.bitcast(I32)))
        tie_row = sb("tie_row", [P, ROW])
        tie_idx = sb("tie_idx", [P, E], I32)
        inv_t = cst[:, C_INV:C_INV + STEPS]

        bank_w, bank_p, bank_o, bank_g = ps[0:2], ps[2:5], ps[5:7], ps[7]

        (consts_in, setup_in, tok_in, pos_in, txt_in, px_in0, px_in1, stored, pads_out, zero_out) = sems(
            st, "consts_in", "setup_in", "tok_in", "pos_in", "txt_in", "px_in0", "px_in1", "stored",
            "pads_out", "zero_out")
        px_in = [px_in0, px_in1]
        (setup_dve, setup_pe, posb_ready, pool_const, pad_ready) = sems(
            st, "setup_dve", "setup_pe", "posb_ready", "pool_const", "pad_ready")
        (tok_done, h_sum, xn_ready, t1_done, xth_ready, xtl_ready, proj_done) = sems(
            st, "tok_done", "h_sum", "xn_ready", "t1_done", "xth_ready", "xtl_ready", "proj_done")
        stat_ready = sems(st, "stat1_ready", "stat2_ready")
        mv_ready = sems(st, "mv1_ready", "mv2_ready")
        ln_half = sems(st, "ln1_half", "ln2_half")
        rstd_ready = sems(st, "rstd1_ready", "rstd2_ready")
        ln_ready = sems(st, "ln1_ready", "ln2_ready")
        (c1_sum, c2_sum, q1_used, q2_used, factors_ready, counts_ready, out_done, h2_ready) = sems(
            st, "c1_sum", "c2_sum", "q1_used", "q2_used", "factors_ready", "counts_ready", "out_done", "h2_ready")
        (x2_ready, t2_done, x2t_ready, gate_done, gate_copied, top_ready, sel_ready, gsub_ready) = sems(
            st, "x2_ready", "t2_done", "x2t_ready", "gate_done", "gate_copied", "top_ready", "sel_ready",
            "gsub_ready")
        (ex_ready, exs_ready, exsum_ready, exinv_ready, weight_ready) = sems(
            st, "ex_ready", "exs_ready", "exsum_ready", "exinv_ready", "weight_ready")
        (rank_done, dest1_ready, carry_ready, seldest_ready, rev0_ready, rev_ready, revmax_ready,
         last_ready, dest_ready, id_ready) = sems(
            st, "rank_done", "dest1_ready", "carry_ready", "seldest_ready", "rev0_ready", "rev_ready",
            "revmax_ready", "last_ready", "dest_ready", "id_ready")
        scattered = sems(st, "scattered0", "scattered1")
        (cnt_step, table_ready, tie_step, tie_ready, tie_copied, tie_moved, tie_free) = sems(
            st, "cnt_step", "table_ready", "tie_step", "tie_ready", "tie_copied", "tie_moved", "tie_free")
        (pool_waited, dve_waited) = sems(st, "pool_waited", "dve_waited")
        N_SETUP = 18
        INNER_READY, COMBINED_READY = 9, 28

        block = st.enter_context(nc.Block())

        @block.sync
        def _(sp):
            sp.dma_start(cst[:], consts).then_inc(consts_in, 16)
            sp.dma_start(px[0][:], xp[:, 0:GS]).then_inc(px_in[0], 16)
            sp.dma_start(tokw[:], tok_wt).then_inc(tok_in, 16)
            sp.dma_start(posb, pos.partition_broadcast(P)).then_inc(pos_in, 16)
            sp.dma_start(tokb[:], tok_b.partition_broadcast(P)).then_inc(pos_in, 16)
            sp.dma_start(px[1][:], xp[:, GS:2 * GS]).then_inc(px_in[1], 16)
            for g in range(2, IMG_GROUPS):
                sp.wait_ge(tok_done, 2 * (g - 1))
                sp.dma_start(px[g % 2][:], xp[:, GS * g:GS * g + GS]).then_inc(px_in[g % 2], 16)
            sp.dma_start(h_all[:, T_IMG:STEPS, :], txt_steps).then_inc(txt_in, 16)
            sp.dma_start(w1raw[:], w1_v[0]).then_inc(w_raw, 16)
            sp.dma_start(w2raw[:], w2_v[0]).then_inc(w_raw, 16)
            sp.dma_start(b2_s[:, 0, :], b2[0].partition_broadcast(P)).then_inc(b2_in, 16)
            sp.dma_start(b1_s[:], b1t).then_inc(b1_in, 16)
            sp.wait_ge(pad_ready, 2)
            sp.dma_start(out[TOKENS:TOKENS + DUMP, :], pad[:, 0, 0:D]).then_inc(zero_out, 16)
            with sp.Fori(0, GROUPS) as g:
                sp.wait_ge(h2_ready, GS * g + GS)
                sp.dma_start(out_steps[:, ds(GS * g, GS), :], h_all[:, ds(GS * g, GS), :]).then_inc(stored, 16)
            sp.wait_ge(table_ready, 1)
            for e in range(E):
                row = sp.value_load(table[0:1, TB_PAD + e:TB_PAD + e + 1], min_val=e * CAP,
                                    max_val=e * CAP + TOKENS)
                sp.dma_start(lists[ds(row, PAD), :].rearrange("(k p) c -> p k c", p=P),
                             pad[:]).then_inc(pads_out, 16)
            sp.wait_ge(pads_out, 16 * E)
            sp.wait_ge(stored, 16 * GROUPS)
            sp.wait_ge(zero_out, 16)

        def pool_ln(pool, n, g, par):
            pool.wait_ge(mv_ready[n], GS * g + GS)
            nc.gpsimd.tensor_tensor(veps[n][par][:], mv[n][par][:, :, 1], eps[:], ALU.add).then_inc(ln_half[n], 1)
            nc.gpsimd.tensor_scalar(nmean[n][par][:], mv[n][par][:, :, 0], -1.0, None, ALU.mult).then_inc(ln_half[n], 1)
            pool.wait_ge(ln_half[n], 2 * g + 2)
            s = ds(GS * g, GS)
            r, m = (rstd[0][par][:], shift[0][par][:]) if n == 0 else (rstd2[:, s], shift2[:, s])
            nc.gpsimd.tensor_tensor(r, veps[n][par][:], rsq[:], ALU.pow).then_inc(rstd_ready[n], 1)
            pool.wait_ge(rstd_ready[n], g + 1)
            nc.gpsimd.tensor_tensor(m, nmean[n][par][:], r, ALU.mult).then_inc(ln_ready[n], 1)

        def pool_scatter(pool, g, par):
            if not isinstance(g, int) or g >= 2:
                pool.wait_ge(scattered[par], 64 * (g - par))
            nc.gpsimd.tensor_copy(rows[par][:, :, D], cst[:, ds(C_TOK + GS * g, GS)]).then_inc(id_ready, 1)
            pool.wait_ge(weight_ready, g + 1)
            waited(pool, pool_waited)
            nc.gpsimd.tensor_copy(rows[par][:, :, D + 1:ROW], weights[:, ds(GS * g, GS), :]).then_inc(id_ready, 1)
            pool.wait_ge(id_ready, 2 * g + 2)
            pool.wait_ge(x2_ready, GS * g + GS)
            pool.wait_ge(dest_ready, g + 1)
            waited(pool, pool_waited)
            for j in range(GS):
                for c in range(2):
                    nc.gpsimd.indirect_dma_start(
                        out=lists, out_offset=bass.IndirectOffsetOnAxis(ap=dest[par][:, j, c:c + 1], axis=0),
                        in_=rows[par][:, j, :], in_offset=None, bounds_check=LIST_ROWS - 1,
                        oob_is_err=False).then_inc(scattered[par], 16)

        @block.gpsimd
        def _(pool):
            nc.gpsimd.memset(ones[:], 1.0).then_inc(pool_const, 1)
            nc.gpsimd.memset(rsq[:], -0.5).then_inc(pool_const, 1)
            nc.gpsimd.memset(eps[:], EPS).then_inc(pool_const, 1)
            nc.gpsimd.memset(sel[0][:, GS, :], 0.0).then_inc(pool_const, 1)
            nc.gpsimd.memset(sel[1][:, GS, :], 0.0).then_inc(pool_const, 1)
            nc.gpsimd.memset(pad[:], 0.0).then_inc(pad_ready, 1)
            pool.wait_ge(pad_ready, 1)
            pool.wait_ge(consts_in, 16)
            nc.gpsimd.tensor_copy(pad[:, :, D], cst[:, C_TOK + STEPS:C_TOK + STEPS + 1]
                                  .to_broadcast([P, PAD // P])).then_inc(pad_ready, 1)
            pool.wait_ge(pos_in, 32)
            pool.wait_ge(pool_const, 5)
            for k in range(4):
                v = posb[:, GS * k:GS * k + GS, :]
                nc.gpsimd.tensor_tensor(v, v, tokb[:].unsqueeze(1).to_broadcast([P, GS, D]),
                                        ALU.add).then_inc(posb_ready, 1)
            pool_ln(pool, 0, 0, 0)
            pool_ln(pool, 0, 1, 1)

            def tick(g, par):
                if not isinstance(g, int) or 1 <= g <= GROUPS:
                    pool_ln(pool, 1, g - 1, 1 - par)
                if not isinstance(g, int) or 2 <= g:
                    pool_scatter(pool, g - 2, par)
                if not isinstance(g, int) or g + 2 < GROUPS:
                    pool_ln(pool, 0, g + 2, par)

            for g in range(IMG_GROUPS):
                tick(g, g % 2)
            with pool.Fori(IMG_GROUPS // 2, GROUPS // 2 - 1) as i:
                tick(2 * i, 0)
                tick(2 * i + 1, 1)
            for g in range(GROUPS - 2, GROUPS + 2):
                tick(g, g % 2)
            for par in range(2):
                pool.wait_ge(scattered[par], 64 * GROUPS)
            pool.wait_ge(table_ready, 1)
            tie = pool.value_load(table[0:1, TB_TIE:TB_TIE + 1], min_val=0, max_val=1)
            with pool.If(tie > 0):
                with pool.Fori(0, STEPS) as t:
                    pool.wait_ge(tie_copied, 4 * t + 4)
                    waited(pool, pool_waited)
                    for e in range(E):
                        nc.gpsimd.indirect_dma_start(
                            out=lists, out_offset=bass.IndirectOffsetOnAxis(ap=tie_idx[:, e:e + 1], axis=0),
                            in_=tie_row[:], in_offset=None, bounds_check=LIST_ROWS - 1,
                            oob_is_err=False).then_inc(tie_moved, 16)
                    pool.wait_ge(tie_moved, 16 * E * t + 16 * E)
                    pool.sem_inc(tie_free, 1)

        def act_ln1(act, g, par):
            act.wait_ge(ln_ready[0], g + 1)
            if not isinstance(g, int) or g >= 1:
                act.wait_ge(t1_done, 2 * g)
            for j in range(GS):
                t = ds(GS * g + j, 1)
                nc.scalar.activation(xn[:, j, :], h_all[:, t, :].squeeze(1), ACT.Identity,
                                     bias=shift[0][par][:, j:j + 1], scale=rstd[0][par][:, j:j + 1]).then_inc(xn_ready, 1)

        def act_xt(act, g):
            for k in range(2):
                act.wait_ge(t1_done, 2 * g + k + 1)
                nc.scalar.copy(xth[:, :, 256 * k:256 * k + 256],
                               bank_w[k][:].rearrange("p (c n) -> p c n", c=DC)).then_inc(xth_ready, 1)

        def act_tail(act, g, par):
            act.wait_ge(ln_ready[1], g + 1)
            if not isinstance(g, int) or g >= 2:
                act.wait_ge(scattered[par], 64 * (g - par))
            for j in range(GS):
                t = ds(GS * g + j, 1)
                nc.scalar.activation(rows[par][:, j, 0:D], h_all[:, t, :].squeeze(1), ACT.Identity,
                                     bias=shift2[:, t], scale=rstd2[:, t]).then_inc(x2_ready, 1)
            for k in range(2):
                act.wait_ge(t2_done, 2 * g + k + 1)
                nc.scalar.copy(x2t[:, :, 256 * k:256 * k + 256],
                               bank_w[k][:].rearrange("p (c n) -> p c n", c=DC)).then_inc(x2t_ready, 1)

        @block.scalar
        def _(act):
            act.dma_start(wi_s[:], winv.rearrange("(c p) n -> p c n", p=P)).then_inc(setup_in, 16)
            act.dma_start(vw[:, :, 0:R], v_b.rearrange("(c p) n -> p c n", p=P)).then_inc(setup_in, 16)
            act.dma_start(vw[:, :, R:2 * R], w_b.rearrange("(c p) n -> p c n", p=P)).then_inc(setup_in, 16)
            act.dma_start(wq_s[:], wq.rearrange("(c p) n -> p c n", p=P)).then_inc(setup_in, 16)
            act.dma_start(wk_s[:], wk.rearrange("(c p) n -> p c n", p=P)).then_inc(setup_in, 16)
            for dst, c0, src in ((rhs_q, 0, v_b), (rhs_q, R, v_t), (rhs_k, 0, w_b), (rhs_k, R, w_t),
                                 (xt_s, 0, x_t), (ub_s, 0, u_b), (ut_s, 0, u_t)):
                act.dma_start(dst[:, :, c0:c0 + R], src.rearrange("(c p) n -> p c n", p=P)).then_inc(setup_in, 16)
            act.dma_start(wo_s[:], wot.rearrange("(c p) n -> p c n", p=P)).then_inc(setup_in, 16)
            act.dma_start(wg_s[:], w_gate.rearrange("(c p) n -> p c n", p=P)).then_inc(setup_in, 16)
            act.dma_start(bias_s[:, 0, :], bias_b).then_inc(setup_in, 16)
            act.dma_start(bias_s[:, 1, :], bias_t).then_inc(setup_in, 16)
            act.dma_start(alpha[:, 0:1], alpha_bi.partition_broadcast(P)).then_inc(setup_in, 16)
            act.dma_start(alpha[:, 1:2], alpha_tri.partition_broadcast(P)).then_inc(setup_in, 16)
            act_ln1(act, 0, 0)
            act_xt(act, 0)
            act_ln1(act, 1, 1)

            def tick(g, par):
                if not isinstance(g, int) or 1 <= g <= GROUPS:
                    act_tail(act, g - 1, 1 - par)
                if not isinstance(g, int) or g + 1 < GROUPS:
                    act_xt(act, g + 1)
                if not isinstance(g, int) or g < GROUPS:
                    if not isinstance(g, int) or g >= 2:
                        act.wait_ge(out_done, 2 * (g - 1))
                    nc.scalar.copy(count_row[par][:], cst[0:1, ds(C_STEP + GS * g, GS)].unsqueeze(2)
                                   .to_broadcast([1, GS, P])).then_inc(counts_ready, 1)
                if not isinstance(g, int) or 1 <= g <= GROUPS:
                    act.wait_ge(gsub_ready, g)
                    if not isinstance(g, int) or g >= 2:
                        act.wait_ge(exs_ready, g - 1)
                    nc.scalar.activation(ex[:], gsub[:], ACT.Exp).then_inc(ex_ready, 1)
                if not isinstance(g, int) or g + 2 < GROUPS:
                    act_ln1(act, g + 2, par)

            for g in range(IMG_GROUPS):
                tick(g, g % 2)
            with act.Fori(IMG_GROUPS // 2, GROUPS // 2 - 1) as i:
                tick(2 * i, 0)
                tick(2 * i + 1, 1)
            for g in range(GROUPS - 2, GROUPS + 1):
                tick(g, g % 2)
            act.wait_ge(w_raw, 32)
            nc.scalar.copy(w1h[0][:], w1raw[:]).then_inc(w_high, 1)
            nc.scalar.copy(w2hl[0][:, :, 0:D], w2raw[:]).then_inc(w_high, 1)

        def dve_stats(dve, n, g, par):
            for j in range(GS):
                t = GS * g + j
                nc.vector.bn_stats(stats[n][par][:, j, :], h_all[:, ds(t, 1), :].squeeze(1)
                                   ).then_inc(stat_ready[n], 1)
            dve.wait_ge(stat_ready[n], GS * g + GS)
            waited(dve, dve_waited)
            for j in range(GS):
                nc.vector.bn_aggr(mv[n][par][:, j, :], stats[n][par][:, j, :]
                                  ).then_inc(mv_ready[n], 1)

        def dve_tok(dve, g):
            dve.wait_ge(posb_ready, g + 1)
            for k in range(2):
                dve.wait_ge(tok_done, 2 * g + k + 1)
                s = slice(GS * g + 2 * k, GS * g + 2 * k + 2)
                nc.vector.tensor_tensor(h_all[:, s, :], bank_w[k][:].rearrange("p (s d) -> p s d", s=2),
                                        posb[:, s, :], ALU.add).then_inc(h_sum, 1)
            dve.wait_ge(h_sum, 2 * g + 2)

        def dve_xt(dve, g):
            for k in range(2):
                dve.wait_ge(xth_ready, 2 * g + k + 1)
                s = slice(256 * k, 256 * k + 256)
                nc.vector.tensor_tensor(xtl[:, :, s], bank_w[k][:].rearrange("p (c n) -> p c n", c=DC),
                                        xth[:, :, s].bitcast(F32), ALU.subtract).then_inc(xtl_ready, 1)

        def dve_h2(dve, g, par):
            for j in range(GS):
                t = GS * g + j
                dve.wait_ge(out_done, 2 * g + j // 2 + 1)
                v = h_all[:, ds(t, 1), :].squeeze(1)
                nc.vector.scalar_tensor_tensor(v, bank_o[j // 2][:, D * (j % 2):D * (j % 2) + D],
                                               cst[:, ds(C_INV + t, 1)], v, ALU.mult, ALU.add).then_inc(h2_ready, 1)
            dve.wait_ge(h2_ready, GS * g + GS)
            waited(dve, dve_waited)
            dve_stats(dve, 1, g, par)

        def dve_factors(dve, g, par):
            def psum(n, rows_=P):
                return bank_p[n][0:rows_, :].rearrange("p (s b) -> p s b", s=GS)

            f = factors[par]
            dve.wait_ge(proj_done, 4 * g + 1)
            for j in range(GS):
                dve.wait_ge(c1_sum, GS * g + j + 1)
                nc.vector.tensor_tensor(c1[:, j, :], psum(0)[:, j, :], c1[:, (j - 1) % GS, :],
                                        ALU.add).then_inc(c1_sum, 1)
            dve.wait_ge(proj_done, 4 * g + 2)
            dve.wait_ge(c1_sum, GS * g + GS + 1)
            nc.vector.tensor_tensor(f[:], psum(1), c1[:], ALU.mult).then_inc(q1_used, 1)
            dve.wait_ge(proj_done, 4 * g + 3)
            for j in range(GS):
                dve.wait_ge(c2_sum, GS * g + j + 1)
                nc.vector.tensor_tensor(c2[:, j, :], psum(2)[:, j, :], c2[:, (j - 1) % GS, :],
                                        ALU.add).then_inc(c2_sum, 1)
            dve.wait_ge(proj_done, 4 * g + 4)
            dve.wait_ge(c2_sum, GS * g + GS + 1)
            nc.vector.tensor_tensor(inverse[:], psum(0, R), c2[0:R, :, :], ALU.mult).then_inc(q2_used, 1)
            dve.wait_ge(q1_used, g + 1)
            for j in range(GS):
                nc.vector.scalar_tensor_tensor(f[R:P, j, :], c2[R:P, j, :], cst[R:P, ds(C_INV + GS * g + j, 1)],
                                               f[R:P, j, :], ALU.mult, ALU.mult).then_inc(factors_ready, 1)
            dve.wait_ge(q2_used, g + 1)
            nc.vector.tensor_tensor(f[0:R, :, :], f[0:R, :, :], inverse[:], ALU.add).then_inc(factors_ready, 1)

        def dve_choose(dve, g, par):
            dve.wait_ge(gate_done, g + 1)
            nc.vector.tensor_copy(gate[:], bank_g[:, 0:GS * E].rearrange("p (s e) -> p s e", s=GS)
                                  ).then_inc(gate_copied, 1)
            dve.wait_ge(gate_copied, g + 1)
            waited(dve, dve_waited)
            for j in range(GS):
                nc.vector.max(top8[:, j, :], gate[:, j, :]).then_inc(top_ready, 1)
            dve.wait_ge(top_ready, GS * g + GS)
            nc.vector.tensor_tensor(sel[par][:, 0:GS, :], gate[:], top8[:, :, 1:2].to_broadcast([P, GS, E]),
                                    ALU.is_ge).then_inc(sel_ready, 1)
            if not isinstance(g, int) or g >= 1:
                dve.wait_ge(ex_ready, g)
            nc.vector.tensor_tensor(gsub[:], gate[:], top8[:, :, 0:1].to_broadcast([P, GS, E]),
                                    ALU.subtract).then_inc(gsub_ready, 1)

        def dve_route(dve, g, par):
            s = ds(GS * g, GS)
            dve.wait_ge(ex_ready, g + 1)
            nc.vector.tensor_tensor(exs[:], ex[:], sel[par][:, 0:GS, :], ALU.mult).then_inc(exs_ready, 1)
            dve.wait_ge(rank_done, g + 1)
            ranks = bank_g[:, 64:64 + (GS + 1) * E].rearrange("p (s e) -> p s e", s=GS + 1)
            dve.wait_ge(carry_ready, g + 1)
            nc.vector.tensor_tensor(dest1[:], ranks[:, 0:GS, :], carry[:].unsqueeze(1).to_broadcast([P, GS, E]),
                                    ALU.add).then_inc(dest1_ready, 1)
            dve.wait_ge(exs_ready, g + 1)
            nc.vector.reduce_sum(exsum[:], exs[:], AX.X).then_inc(exsum_ready, 1)
            dve.wait_ge(dest1_ready, g + 1)
            nc.vector.tensor_tensor(carry[:], ranks[:, GS, :], carry[:], ALU.add).then_inc(carry_ready, 1)
            nc.vector.tensor_tensor(seldest[:, s, :], dest1[:], sel[par][:, 0:GS, :], ALU.mult
                                    ).then_inc(seldest_ready, 1)
            nc.vector.tensor_scalar(rev0[:], dest1[:], -1.0, float(LIST_ROWS + 1), ALU.mult, ALU.add
                                    ).then_inc(rev0_ready, 1)
            dve.wait_ge(exsum_ready, g + 1)
            nc.vector.reciprocal(exinv[:], exsum[:]).then_inc(exinv_ready, 1)
            dve.wait_ge(rev0_ready, g + 1)
            nc.vector.tensor_tensor(rev[:], rev0[:], sel[par][:, 0:GS, :], ALU.mult).then_inc(rev_ready, 1)
            dve.wait_ge(seldest_ready, g + 1)
            nc.vector.reduce_max(last1[:, s], seldest[:, s, :], AX.X).then_inc(last_ready, 1)
            dve.wait_ge(exinv_ready, g + 1)
            nc.vector.scalar_tensor_tensor(weights[:, s, :], exs[:], 1.0 / E,
                                           exinv[:].unsqueeze(2).to_broadcast([P, GS, E]), ALU.mult,
                                           ALU.mult).then_inc(weight_ready, 1)
            dve.wait_ge(rev_ready, g + 1)
            nc.vector.reduce_max(revmax[:], rev[:], AX.X).then_inc(revmax_ready, 1)
            dve.wait_ge(last_ready, g + 1)
            if not isinstance(g, int) or g >= 2:
                dve.wait_ge(scattered[par], 64 * (g - par))
            nc.vector.tensor_scalar(dest[par][:, :, 1], last1[:, s], -1.0, None, ALU.add)
            dve.wait_ge(revmax_ready, g + 1)
            nc.vector.tensor_scalar(first1[:, s], revmax[:], -1.0, float(LIST_ROWS + 1), ALU.mult, ALU.add)
            nc.vector.tensor_scalar(dest[par][:, :, 0], revmax[:], -1.0, float(LIST_ROWS), ALU.mult, ALU.add
                                    ).then_inc(dest_ready, 1)

        @block.vector
        def _(dve):
            n = [0]

            def step(ins):
                n[0] += 1
                ins.then_inc(setup_dve, 1)

            nc.vector.memset(c1[:, GS - 1, :], 0.0).then_inc(c1_sum, 1)
            nc.vector.memset(c2[:, GS - 1, :], 0.0).then_inc(c2_sum, 1)
            dve.wait_ge(consts_in, 16)
            nc.vector.tensor_copy(carry[:], cst[:, C_CAP:C_CAP + E]).then_inc(carry_ready, 1)
            dve_tok(dve, 0)
            dve_stats(dve, 0, 0, 0)
            dve.wait_ge(setup_in, 16 * N_SETUP)
            step(nc.vector.tensor_copy(uu[:, :, 0:R], ub_s[:]))
            step(nc.vector.tensor_scalar(uu[:, :, R:2 * R], ut_s[:], alpha[:, 1:2], None, ALU.mult))
            step(nc.vector.tensor_scalar(bias_m[:, 0, :], bias_s[:, 1, :], alpha[:, 1:2], None, ALU.mult))
            dve.wait_ge(setup_dve, n[0])
            step(nc.vector.tensor_tensor(bias_m[:, 1, :], bias_s[:, 0, :], bias_m[:, 0, :], ALU.add))
            dve.wait_ge(setup_dve, n[0])
            step(nc.vector.scalar_tensor_tensor(bias_col[:], bias_s[:, 0, :], alpha[:, 0:1],
                                                bias_m[:, 1, :], ALU.mult, ALU.add))
            step(nc.vector.tensor_copy(a_h[:, :, M_K2 + R:M_Q2], xt_s[:]))
            dve.wait_ge(setup_dve, n[0])
            step(nc.vector.tensor_tensor(a_l[:, :, M_K2 + R:M_Q2], xt_s[:], a_h[:, :, M_K2 + R:M_Q2].bitcast(F32),
                                         ALU.subtract))
            dve.wait_ge(setup_pe, 1)
            iv = bank_p[0][:, 0:256].rearrange("p (c n) -> p c n", c=DC)
            step(nc.vector.tensor_copy(rhs_k[:, :, 2 * R:3 * R], iv[:, :, 0:R]))
            step(nc.vector.tensor_copy(rhs_q[:, :, 2 * R:3 * R], iv[:, :, R:2 * R]))
            assert n[0] == INNER_READY
            for m in range(DC):
                dve.wait_ge(setup_pe, 2 + m)
                q, k = bank_p[1 + m][:, 0:192], bank_p[1 + m][:, 192:384]
                for dst, src in ((M_Q1, q[:, 0:128]), (M_K1, k[:, 0:128]), (M_K2, k[:, 128:192])):
                    w = src.shape[1]
                    step(nc.vector.tensor_copy(a_h[:, m, dst:dst + w], src))
                    dve.wait_ge(setup_dve, n[0])
                    step(nc.vector.tensor_tensor(a_l[:, m, dst:dst + w], src, a_h[:, m, dst:dst + w].bitcast(F32),
                                                 ALU.subtract))
                step(nc.vector.tensor_scalar(a_h[:, m, M_Q2:M_END], q[:, 128:192], alpha[:, 0:1], None, ALU.mult))
                dve.wait_ge(setup_dve, n[0])
                step(nc.vector.scalar_tensor_tensor(a_l[:, m, M_Q2:M_END], q[:, 128:192], alpha[:, 0:1],
                                                    a_h[:, m, M_Q2:M_END].bitcast(F32), ALU.mult, ALU.subtract))
            dve.wait_ge(setup_pe, 4)
            step(nc.vector.tensor_copy(g_out[:], bank_o[0][:, 0:D]))
            step(nc.vector.tensor_copy(g_bias[:, 0, :], bank_o[1][0:1, 0:D]))
            dve.wait_ge(setup_dve, n[0])
            step(nc.vector.tensor_tensor(g_bias[:, 1, :], bank_o[1][0:1, 0:D], g_bias[:, 0, :].bitcast(F32),
                                         ALU.subtract))
            assert n[0] == COMBINED_READY
            dve_xt(dve, 0)
            dve_tok(dve, 1)
            dve_stats(dve, 0, 1, 1)

            def tick(g, par):
                if not isinstance(g, int) or 1 <= g <= GROUPS:
                    dve_h2(dve, g - 1, 1 - par)
                if not isinstance(g, int) or g >= 2:
                    dve_route(dve, g - 2, par)
                if not isinstance(g, int) or g < GROUPS:
                    dve_factors(dve, g, par)
                if not isinstance(g, int) or g + 1 < GROUPS:
                    dve_xt(dve, g + 1)
                if not isinstance(g, int) or 1 <= g <= GROUPS:
                    dve_choose(dve, g - 1, 1 - par)
                if isinstance(g, int) and g + 2 < IMG_GROUPS:
                    dve_tok(dve, g + 2)
                if not isinstance(g, int) or g + 2 < GROUPS:
                    if not isinstance(g, int) or g + 2 >= IMG_GROUPS:
                        dve.wait_ge(txt_in, 16)
                    dve_stats(dve, 0, g + 2, par)

            for g in range(IMG_GROUPS):
                tick(g, g % 2)
            with dve.Fori(IMG_GROUPS // 2, GROUPS // 2 - 1) as i:
                tick(2 * i, 0)
                tick(2 * i + 1, 1)
            for g in range(GROUPS - 2, GROUPS + 2):
                tick(g, g % 2)

            m = [0]

            def count(ins):
                m[0] += 1
                ins.then_inc(cnt_step, 1)
                dve.wait_ge(cnt_step, m[0])

            dve.wait_ge(carry_ready, GROUPS + 1)
            nf, nt, tile0, n_half = cnt[:, 0, 0:E], cnt[:, 1, 0:E], cnt[:, 2, :], cnt[:, 3, 0:E]
            count(nc.vector.tensor_tensor(nf, carry[0:1, :], cst[0:1, C_CAP:C_CAP + E], ALU.subtract))
            nc.vector.tensor_scalar(cnti[:, 1, :], nf, float(P - 1), None, ALU.add)
            count(nc.vector.tensor_scalar(cnti[:, 0, :], nf, float(TILE - 1), None, ALU.add))
            nc.vector.tensor_scalar(cnti[:, 3, :], cnti[:, 1, :], P.bit_length() - 1, None, ALU.arith_shift_right)
            count(nc.vector.tensor_scalar(cnti[:, 2, :], cnti[:, 0, :], TILE.bit_length() - 1, None,
                                          ALU.arith_shift_right))
            nc.vector.tensor_copy(n_half, cnti[:, 3, :])
            nc.vector.memset(tile0[:, 0:1], 0.0)
            count(nc.vector.tensor_scalar(nt, cnti[:, 2, :], 1.0, None, ALU.max))
            for e in range(E):
                count(nc.vector.tensor_tensor(tile0[:, e + 1:e + 2], tile0[:, e:e + 1], nt[:, e:e + 1], ALU.add))
            nc.vector.tensor_copy(table[:, TB_TILE:TB_TILE + E + 1], tile0)
            nc.vector.tensor_scalar(table[:, TB_PAD:TB_PAD + E], carry[0:1, :], -1.0, None, ALU.add)
            count(nc.vector.reduce_sum(cnt[:, 4, 0:1], nf, AX.X))
            count(nc.vector.tensor_tensor(cnt[:, 5, 0:E], n_half, nt, ALU.subtract))
            count(nc.vector.tensor_tensor(cnt[:, 5, 0:E], cnt[:, 5, 0:E], tile0[:, 0:E], ALU.add))
            count(nc.vector.scalar_tensor_tensor(table[:, TB_FULL:TB_FULL + E], tile0[:, 0:E], 1.0,
                                                 cnt[:, 5, 0:E], ALU.add, ALU.max))
            nc.vector.tensor_scalar(table[:, TB_TIE:TB_TIE + 1], cnt[:, 4, 0:1], float(2 * TOKENS), None,
                                    ALU.is_gt).then_inc(table_ready, 1)
            dve.wait_ge(w_high, 2)
            split_low(nc.vector, 0)
            dve.wait_ge(table_ready, 1)
            tie = dve.value_load(table[0:1, TB_TIE:TB_TIE + 1], min_val=0, max_val=1)
            with dve.If(tie > 0):
                for a, edge in ((tie_a, first1), (tie_b, last1)):
                    nc.vector.tensor_tensor(a, seldest[:], edge[:].unsqueeze(2).to_broadcast([P, STEPS, E]),
                                            ALU.not_equal).then_inc(tie_step, 1)
                dve.wait_ge(tie_step, 2)
                nc.vector.tensor_tensor(tie_a, tie_a, tie_b, ALU.mult).then_inc(tie_step, 1)
                dve.wait_ge(tie_step, 3)
                nc.vector.tensor_tensor(tie_b, tie_a, seldest[:], ALU.mult).then_inc(tie_step, 1)
                dve.wait_ge(tie_step, 4)
                nc.vector.tensor_scalar(tie_a, tie_b, 0.0, float(LIST_ROWS + 2), ALU.is_equal,
                                        ALU.mult).then_inc(tie_step, 1)
                dve.wait_ge(tie_step, 5)
                nc.vector.scalar_tensor_tensor(tie_dest, tie_b, -1.0, tie_a, ALU.add, ALU.add
                                               ).then_inc(tie_ready, 1)
                dve.wait_ge(tie_ready, 1)
                dve.sem_inc(tie_free, 1)
                with dve.Fori(0, STEPS) as t:
                    dve.wait_ge(tie_free, t + 1)
                    waited(dve, dve_waited)
                    v = ds(t, 1)
                    nc.vector.tensor_scalar(tie_row[:, 0:D], h_all[:, v, :].squeeze(1), rstd2[:, v], shift2[:, v],
                                            ALU.mult, ALU.add).then_inc(tie_copied, 1)
                    nc.vector.tensor_copy(tie_row[:, D:D + 1], cst[:, ds(C_TOK + t, 1)]).then_inc(tie_copied, 1)
                    nc.vector.tensor_copy(tie_row[:, D + 1:ROW], weights[:, v, :].squeeze(1)).then_inc(tie_copied, 1)
                    nc.vector.tensor_copy(tie_idx[:], tie_dest[:, v, :].squeeze(1)).then_inc(tie_copied, 1)

        def pe_tok(pe, g):
            pe.wait_ge(px_in[g % 2], 16 * (g // 2 + 1))
            pe.wait_ge(tok_in, 16)
            for k in range(2):
                if g >= 1:
                    pe.wait_ge(xtl_ready, 2 * (g - 1) + k + 1)
                for jj in range(2):
                    for c in range(FC):
                        last = nc.tensor.matmul(bank_w[k][:, D * jj:D * jj + D], px[g % 2][:, 2 * k + jj, c, :],
                                                tokw[:, c, :], start=(c == 0), stop=(c == FC - 1))
                last.then_inc(tok_done, 1)

        def pe_t1(pe, g):
            for k in range(2):
                pe.wait_ge(xn_ready, GS * g + 2 * k + 2)
                if isinstance(g, int) and g < 2:
                    pe.wait_ge(h_sum, 2 * g + k + 1)
                if not isinstance(g, int) or g >= 2:
                    pe.wait_ge(x2t_ready, 2 * (g - 2) + k + 1)
                for jj in range(2):
                    for c in range(DC):
                        last = nc.tensor.transpose(bank_w[k][:, 256 * c + P * jj:256 * c + P * jj + P],
                                                   xn[:, 2 * k + jj, P * c:P * c + P], ident)
                last.then_inc(t1_done, 1)

        def pe_t2(pe, g, par):
            for k in range(2):
                pe.wait_ge(x2_ready, GS * g + 2 * k + 2)
                pe.wait_ge(xtl_ready, 2 * (g + 1) + k + 1 if not isinstance(g, int) or g + 1 < GROUPS
                           else 2 * GROUPS)
                if isinstance(g, int) and g + 2 < IMG_GROUPS:
                    pe.wait_ge(h_sum, 2 * (g + 2) + k + 1)
                for jj in range(2):
                    for c in range(DC):
                        last = nc.tensor.transpose(bank_w[k][:, 256 * c + P * jj:256 * c + P * jj + P],
                                                   rows[par][:, 2 * k + jj, P * c:P * c + P], ident)
                last.then_inc(t2_done, 1)

        def pe_proj(pe, g):
            pe.wait_ge(xth_ready, 2 * g + 2)
            pe.wait_ge(xtl_ready, 2 * g + 2)
            chunks = ((0, M_K1, P), (1, M_Q1, P), (2, M_K2, P), (0, M_Q2, R))
            freed = ((q2_used, g), (q1_used, g), (c2_sum, GS * g + 1), (c1_sum, GS * g + GS + 1))
            for n, (bank, col, m) in enumerate(chunks):
                if not (isinstance(g, int) and g == 0 and n < 3):
                    pe.wait_ge(*freed[n])
                for c in range(DC):
                    for i, (a, x) in enumerate(((a_h, xth), (a_h, xtl), (a_l, xth))):
                        last = nc.tensor.matmul(bank_p[bank][0:m, :], a[:, c, col:col + m], x[:, c, :],
                                                start=(c == 0 and i == 0), stop=(c == DC - 1 and i == 2))
                last.then_inc(proj_done, 1)

        def pe_out(pe, g, par):
            pe.wait_ge(factors_ready, 5 * g + 5)
            pe.wait_ge(counts_ready, g + 1)
            for k in range(2):
                if not isinstance(g, int) or g >= 1:
                    pe.wait_ge(h2_ready, GS * (g - 1) + 2 * k + 2)
                for jj in range(2):
                    o = bank_o[k][:, D * jj:D * jj + D]
                    nc.tensor.matmul(o, factors[par][:, 2 * k + jj, :], g_out[:], start=True, stop=False)
                    for part in range(2):
                        last = nc.tensor.matmul(o, count_row[par][:, 2 * k + jj, :], g_bias[:, part, :],
                                                start=False, stop=(part == 1))
                last.then_inc(out_done, 1)

        def pe_gate(pe, g):
            pe.wait_ge(x2t_ready, 2 * g + 2)
            if not isinstance(g, int) or g >= 1:
                pe.wait_ge(gate_copied, g)
                pe.wait_ge(carry_ready, g + 1)
            for j in range(GS):
                for c in range(DC):
                    last = nc.tensor.matmul(bank_g[:, E * j:E * j + E], x2t[:, c, P * j:P * j + P], wg_s[:, c, :],
                                            start=(c == 0), stop=(c == DC - 1))
            last.then_inc(gate_done, 1)

        def pe_rank(pe, g, par):
            pe.wait_ge(sel_ready, g + 1)
            if not isinstance(g, int) or g >= 1:
                pe.wait_ge(carry_ready, g + 1)
            nc.tensor.matmul(bank_g[:, 64:64 + (GS + 1) * E], cst[:, C_TRI:C_TRI + P],
                             sel[par][:].rearrange("p s e -> p (s e)"), start=True, stop=False)
            for j in range(GS):
                later = GS - j
                last = nc.tensor.matmul(
                    bank_g[:, 64 + (j + 1) * E:64 + (GS + 1) * E].rearrange("p (s e) -> p s e", e=E), ones[:],
                    sel[par][:, j:j + 1, :].to_broadcast([P, later, E]), start=False, stop=(j == GS - 1))
            last.then_inc(rank_done, 1)

        @block.tensor
        def _(pe):
            pe.wait_ge(consts_in, 16)
            pe.wait_ge(pool_const, 5)
            pe_tok(pe, 0)
            pe.wait_ge(setup_in, 16 * N_SETUP)
            for m in range(DC):
                for c in range(DC):
                    last = nc.tensor.matmul(bank_p[0][:, P * m:P * m + P], wi_s[:, c, P * m:P * m + P], vw[:, c, :],
                                            start=(c == 0), stop=(c == DC - 1))
            last.then_inc(setup_pe, 1)
            pe_t1(pe, 0)
            pe.wait_ge(setup_dve, INNER_READY)
            for m in range(DC):
                for o, w, rhs in ((0, wq_s, rhs_q), (192, wk_s, rhs_k)):
                    for c in range(DC):
                        last = nc.tensor.matmul(bank_p[1 + m][:, o:o + 192], w[:, c, P * m:P * m + P], rhs[:, c, :],
                                                start=(c == 0), stop=(c == DC - 1))
                last.then_inc(setup_pe, 1)
            for c in range(DC):
                nc.tensor.matmul(bank_o[0][:, 0:D], uu[:, c, :], wo_s[:, c, :], start=(c == 0), stop=(c == DC - 1))
            for c in range(DC):
                last = nc.tensor.matmul(bank_o[1][0:1, 0:D], bias_col[:, c:c + 1], wo_s[:, c, :], start=(c == 0),
                                        stop=(c == DC - 1))
            last.then_inc(setup_pe, 1)
            pe_tok(pe, 1)
            pe.wait_ge(setup_dve, COMBINED_READY)

            def tick(g, par):
                if not isinstance(g, int) or 1 <= g <= GROUPS:
                    pe_out(pe, g - 1, 1 - par)
                if not isinstance(g, int) or g >= 2:
                    pe_rank(pe, g - 2, par)
                if not isinstance(g, int) or g < GROUPS:
                    pe_proj(pe, g)
                if not isinstance(g, int) or 1 <= g <= GROUPS:
                    pe_t2(pe, g - 1, 1 - par)
                if not isinstance(g, int) or g + 1 < GROUPS:
                    pe_t1(pe, g + 1)
                if not isinstance(g, int) or 1 <= g <= GROUPS:
                    pe_gate(pe, g - 1)
                if isinstance(g, int) and g + 2 < IMG_GROUPS:
                    pe_tok(pe, g + 2)

            for g in range(IMG_GROUPS):
                tick(g, g % 2)
            with pe.Fori(IMG_GROUPS // 2, GROUPS // 2 - 1) as i:
                tick(2 * i, 0)
                tick(2 * i + 1, 1)
            for g in range(GROUPS - 2, GROUPS + 2):
                tick(g, g % 2)


def experts(nc, sb_, sems, ps, ident, table, lists, out, w1_v, w2_v, b2, w1h, w1l, w2hl,
            w1raw, w2raw, b1_s, b2_s, w_raw, w_high, w_low, b1_in, b2_in, split_low):
    with ExitStack() as st:
        def sb(name, shape, dt=F32):
            return sb_(name, shape, dt, st)

        w1h.append(sb("w1h1", [P, DC, H], F32R))
        w1l.append(sb("w1l1", [P, DC, H], F32R))
        w2hl.append(sb("w2hl1", [P, HC, 2 * D], F32R))
        xe = sb("xe", [P, SUB, ROW])
        xh, xl = sb("xh", [P, DC, TILE], F32R), sb("xl", [P, DC, TILE], F32R)
        hid = sb("hid", [P, HC, TILE])
        hh, hl = sb("hh", [P, HC, TILE], F32R), sb("hl", [P, HC, TILE], F32R)
        meta_n = sb("meta_n", [P, SUB, 1 + E])
        meta_w = sb("meta_w", [P, SUB, 1 + E])
        meta_i = sb("meta_i", [P, SUB], I32)
        y1 = sb("y1", [P, SUB, D])
        y2 = sb("y2", [P, SUB, D])
        y = sb("y", [P, SUB, D])
        bank_s, bank_y, bank_x = ps[0:4], ps[4:6], ps[6]

        (xe_in, transposed, xh_ready, xl_ready, s1_done, hh_ready, hid_ready, hl_ready) = sems(
            st, "xe_in", "transposed", "xh_ready", "xl_ready", "s1_done", "hh_ready", "hid_ready",
            "hl_ready")
        (y_done, y1_ready, y2_ready, y_ready, added, y_free, meta_next, meta_ready) = sems(
            st, "y_done", "y1_ready", "y2_ready", "y_ready", "added", "y_free", "meta_next", "meta_ready")

        (sp_waited, pool_waited, pe_waited, act_waited, dve_waited) = sems(
            st, "sp_waited", "pool_waited_2", "pe_waited", "act_waited", "dve_waited_2")
        block = st.enter_context(nc.Block())
        MAX_TILES = E * (TOKENS // TILE) + E

        def tile_of(eng, e):
            return eng.value_load(table[0:1, ds(TB_TILE + e, 1)], min_val=0, max_val=MAX_TILES)

        def each_expert(eng, tile, head=None, behind_first=None, behind_all=None, halves=False):
            with eng.Fori(0, E // 2) as i:
                for k in range(2):
                    e = 2 * i + k
                    t0 = tile_of(eng, e)
                    t1 = tile_of(eng, e + 1)
                    if head is not None:
                        head(e, k)
                    tile(t0, e, k, t0)
                    if behind_first is not None:
                        behind_first(e, k, t0)
                    full = t1
                    if halves:
                        full = eng.value_load(table[0:1, ds(TB_FULL + e, 1)], min_val=1, max_val=MAX_TILES)
                    with eng.If(full > t0 + 1):
                        with eng.Fori(t0 + 1, full) as t:
                            tile(t, e, k, t0)
                    if halves:
                        with eng.If(t1 > full):
                            tile(full, e, k, t0, subs=1)
                    if behind_all is not None:
                        behind_all(e, k, t0)

        def following(i2):
            return (i2 + 1) % E

        @block.sync
        def _(sp):
            def weights_of_next(e, k, t0):
                sp.wait_ge(w_low, 2 * e + 2)
                n = following(e)
                sp.dma_start(w1raw[:], w1_v[ds(n, 1)].squeeze(0)).then_inc(w_raw, 16)
                sp.dma_start(w2raw[:], w2_v[ds(n, 1)].squeeze(0)).then_inc(w_raw, 16)

            def bias_of_next(e, k, t0):
                sp.wait_ge(b2_in, 16 * e + 16)
                sp.wait_ge(y_free, SUB * t0 + SUB)
                sp.dma_start(b2_s[:, 1 - k, :], b2[ds(following(e), 1)].squeeze(0).partition_broadcast(P)
                             ).then_inc(b2_in, 16)

            def tile(t, e, k, t0):
                sp.wait_ge(transposed, t + 1)
                sp.wait_ge(meta_next, t + 1)
                row = nc.s_assert_within(
                    e * CAP + (t - t0) * TILE, 0, LIST_ROWS - TILE,
                    skip_runtime_bounds_check_because="an expert has at most CAP // TILE tiles")
                sp.dma_start(xe[:], lists[ds(row, TILE), :].rearrange("(s p) c -> p s c", p=P)
                             ).then_inc(xe_in, 16)

            each_expert(sp, tile, behind_first=weights_of_next, behind_all=bias_of_next)
            total = tile_of(sp, E)
            sp.wait_ge(transposed, total + 1)
            sp.wait_ge(meta_next, total + 1)
            sp.dma_start(xe[:], lists[0:TILE, :].rearrange("(s p) c -> p s c", p=P)).then_inc(xe_in, 16)
            sp.wait_ge(xe_in, 16 * total + 16)
            sp.wait_ge(w_raw, 32 * E + 32)
            sp.wait_ge(b2_in, 16 * E + 16)
            waited(sp, sp_waited)

        @block.gpsimd
        def _(pool):
            def use_next(t1):
                pool.wait_ge(meta_next, t1 + 1)
                waited(pool, pool_waited)
                nc.gpsimd.tensor_copy(meta_w[:], meta_n[:]).then_inc(meta_ready, 1)
                nc.gpsimd.tensor_copy(meta_i[:], meta_n[:, :, 0]).then_inc(meta_ready, 1)

            pool.sem_inc(y_free, SUB)
            use_next(1)

            def split_next(e, k, t0):
                pool.wait_ge(w_high, 2 * e + 4)
                split_low(nc.gpsimd, 1 - k)

            def tile(t, e, k, t0):
                pool.wait_ge(meta_ready, 2 * t + 2)
                for s in range(SUB):
                    pool.wait_ge(y_ready, SUB * t + s + 1)
                    waited(pool, pool_waited)
                    nc.gpsimd.indirect_dma_start(
                        out=out, out_offset=bass.IndirectOffsetOnAxis(ap=meta_i[:, s:s + 1], axis=0),
                        in_=y[:, s, :], in_offset=None, bounds_check=TOKENS + DUMP - 1, oob_is_err=True,
                        compute_op=ALU.add).then_inc(added, 16)
                    pool.wait_ge(added, 16 * (SUB * t + s + 1))
                    pool.sem_inc(y_free, 1)
                use_next(t + 2)

            each_expert(pool, tile, behind_first=split_next)

        @block.scalar
        def _(act):
            act.sem_inc(hid_ready, HC)
            def high_x(t1):
                act.wait_ge(transposed, t1 + 1)
                nc.scalar.copy(xh[:], bank_x[:].rearrange("p (c n) -> p c n", c=DC)).then_inc(xh_ready, 1)

            def take_next(t1):
                nc.scalar.copy(meta_n[:], xe[:, :, D:ROW]).then_inc(meta_next, 1)

            act.sem_inc(meta_next, 1)
            high_x(1)
            act.wait_ge(xe_in, 16)
            take_next(1)
            act.wait_ge(b1_in, 16)

            def tile(t, e, k, t0, subs=SUB):
                n = P * subs
                for c in range(HC):
                    if c % 2 == 0:
                        act.wait_ge(s1_done, HC // 2 * t + c // 2 + 1)
                        act.wait_ge(hl_ready, HC // 2 * t + c // 2 + 1)
                        waited(act, act_waited)
                    nc.scalar.activation(hid[:, c, 0:n], bank_s[c // 2][:, TILE * (c % 2):TILE * (c % 2) + n],
                                         ACT.Relu, bias=b1_s[:, ds(e * HC + c, 1)]).then_inc(hid_ready, 1)
                high_x(t + 2)
                act.wait_ge(meta_ready, 2 * t + 2)
                act.wait_ge(xe_in, 16 * (t + 2))
                take_next(t + 2)
                for s in range(subs):
                    act.wait_ge(y_done, SUB * t + s + 1)
                    waited(act, act_waited)
                    nc.scalar.activation(y1[:, s, :], bank_y[s][:, D:2 * D], ACT.Copy,
                                         scale=meta_w[:, s, ds(1 + e, 1)]).then_inc(y1_ready, SUB // subs)

            each_expert(act, tile, halves=True)

        @block.vector
        def _(dve):
            dve.sem_inc(hl_ready, HC // 2)
            dve.sem_inc(y2_ready, SUB)

            def low_x(t1):
                dve.wait_ge(xh_ready, t1)
                nc.vector.tensor_tensor(xl[:], bank_x[:].rearrange("p (c n) -> p c n", c=DC),
                                        xh[:].bitcast(F32), ALU.subtract).then_inc(xl_ready, 1)

            low_x(1)

            def head(e, k):
                dve.wait_ge(b2_in, 16 * e + 16)
                waited(dve, dve_waited)

            def tile(t, e, k, t0, subs=SUB):
                n = P * subs

                def high_hidden(q):
                    v = slice(2 * q, 2 * q + 2)
                    dve.wait_ge(hid_ready, HC * (t + 1) + 2 * q + 2)
                    nc.vector.tensor_copy(hh[:, v, 0:n], hid[:, v, 0:n]).then_inc(hh_ready, 1)

                def low_hidden(q):
                    v = slice(2 * q, 2 * q + 2)
                    dve.wait_ge(hh_ready, HC // 2 * t + q + 1)
                    nc.vector.tensor_tensor(hl[:, v, 0:n], hid[:, v, 0:n], hh[:, v, 0:n].bitcast(F32),
                                            ALU.subtract).then_inc(hl_ready, 1)

                for q in range(HC // 2):
                    high_hidden(q)
                    low_hidden(q)
                low_x(t + 2)
                for s in range(subs):
                    w = meta_w[:, s, ds(1 + e, 1)]
                    dve.wait_ge(y1_ready, SUB * t + s + 1)
                    nc.vector.scalar_tensor_tensor(y2[:, s, :], bank_y[s][:, 0:D], w, y1[:, s, :], ALU.mult,
                                                   ALU.add).then_inc(y2_ready, SUB // subs)
                for s in range(subs):
                    w = meta_w[:, s, ds(1 + e, 1)]
                    dve.wait_ge(y2_ready, SUB * (t + 1) + s + 1)
                    dve.wait_ge(y_free, SUB * t + s + 1)
                    nc.vector.scalar_tensor_tensor(y[:, s, :], b2_s[:, k, :], w, y2[:, s, :], ALU.mult,
                                                   ALU.add).then_inc(y_ready, SUB // subs)

            def raise_next(e, k, t0):
                dve.wait_ge(w_raw, 32 * e + 64)
                nc.vector.tensor_copy(w1h[1 - k][:], w1raw[:]).then_inc(w_high, 1)
                nc.vector.tensor_copy(w2hl[1 - k][:, :, 0:D], w2raw[:]).then_inc(w_high, 1)

            each_expert(dve, tile, head=head, behind_first=raise_next, halves=True)

        @block.tensor
        def _(pe):
            pe.sem_inc(transposed, 1)

            def transpose(t1):
                pe.wait_ge(xe_in, 16 * t1)
                for c in range(DC):
                    for s in range(SUB):
                        last = nc.tensor.transpose(bank_x[:, TILE * c + P * s:TILE * c + P * s + P],
                                                   xe[:, s, P * c:P * c + P], ident)
                last.then_inc(transposed, 1)

            transpose(1)

            def head(e, k):
                pe.wait_ge(w_low, 2 * e + 2)
                waited(pe, pe_waited)

            def tile(t, e, k, t0, subs=SUB):
                n = P * subs
                pe.wait_ge(xh_ready, t + 1)
                pe.wait_ge(xl_ready, t + 1)
                for c in range(HC):
                    if c % 2 == 0:
                        pe.wait_ge(hid_ready, HC * t + c + 2)
                    for d in range(DC):
                        for i, (w, x) in enumerate(((w1h[k], xh), (w1h[k], xl), (w1l[k], xh))):
                            last = nc.tensor.matmul(bank_s[c // 2][:, TILE * (c % 2):TILE * (c % 2) + n],
                                                    w[:, d, P * c:P * c + P], x[:, d, 0:n],
                                                    start=(d == 0 and i == 0), stop=(d == DC - 1 and i == 2))
                    if c % 2 == 1:
                        last.then_inc(s1_done, 1)
                transpose(t + 2)
                for s in range(subs):
                    pe.wait_ge(y2_ready, SUB * t + s + 1)
                    for c in range(HC):
                        if s == 0 and c % 2 == 0:
                            pe.wait_ge(hl_ready, HC // 2 * (t + 1) + c // 2 + 1)
                        nc.tensor.matmul(bank_y[s][:], hh[:, c, P * s:P * s + P], w2hl[k][:, c, :],
                                         start=(c == 0), stop=False)
                        last = nc.tensor.matmul(bank_y[s][:, 0:D], hl[:, c, P * s:P * s + P], w2hl[k][:, c, 0:D],
                                                start=False, stop=(c == HC - 1))
                    last.then_inc(y_done, SUB // subs)

            each_expert(pe, tile, head=head, halves=True)


def kernel(**inputs):
    import numpy as np
    import concourse.bacc as bacc
    from concourse.bass_utils import run_bass_kernel_spmd

    def a(name):
        return np.ascontiguousarray(inputs[name])

    x = a("x").reshape(P, 3, 4, 16, 4, 16).transpose(2, 4, 1, 3, 5, 0)
    x = x.reshape(T_IMG, FC, P, P).transpose(2, 0, 1, 3)
    consts = np.zeros((P, C_END), np.float32)
    consts[:, C_ID:C_ID + P] = np.eye(P)
    consts[:, C_TRI:C_TRI + P] = np.triu(np.ones((P, P)), 1)
    consts[:, C_INV:C_INV + STEPS] = 1.0 / np.arange(1, STEPS + 1)
    consts[:, C_TOK:C_TOK + STEPS] = np.arange(TOKENS).reshape(P, STEPS)
    consts[:, C_TOK + STEPS] = TOKENS + np.arange(P)
    consts[:, C_CAP:C_CAP + E] = np.arange(E) * CAP + 1
    consts[:, C_STEP:C_STEP + STEPS] = np.arange(1, STEPS + 1)
    L, A, M = "L0_tok_", "L0_attn_", "L0_ffn_"
    data = {
        "xp": x, "txt": a("txt"),
        "tok_wt": a(L + "W").T.reshape(FC, P, D).transpose(1, 0, 2),
        "tok_b": a(L + "b"), "pos": a(L + "pos_emb"),
        "wq": a(A + "WQ"), "wk": a(A + "WK"), "wot": a(A + "WO").T, "winv": a(A + "Winv"),
        "u_b": a(A + "U_b"), "v_b": a(A + "V_b"), "w_b": a(A + "W_b"),
        "bias_b": a(A + "bias_b").reshape(DC, P).T,
        "u_t": a(A + "U_t"), "v_t": a(A + "V_t"), "w_t": a(A + "W_t"), "x_t": a(A + "X_t"),
        "bias_t": a(A + "bias_t").reshape(DC, P).T,
        "alpha_bi": a(A + "alpha_bi").reshape(1), "alpha_tri": a(A + "alpha_tri").reshape(1),
        "w_gate": a(M + "W_gate"), "w1": a(M + "W1"),
        "b1t": a(M + "b1").reshape(E, HC, P).transpose(2, 0, 1).reshape(P, E * HC),
        "w2": a(M + "W2"), "b2": a(M + "b2"), "consts": consts,
    }
    data = {k: np.ascontiguousarray(v) for k, v in data.items()}
    nc = bacc.Bacc("TRN2", target_bir_lowering=False, num_devices=1)
    args = [nc.dram_tensor(f"in_{k}", v.shape, mybir.dt.from_np(v.dtype), kind="ExternalInput").ap()
            for k, v in data.items()]
    out = nc.dram_tensor("out", (TOKENS + DUMP, D), F32, kind="ExternalOutput").ap()
    build(nc, *args, out)
    got = run_bass_kernel_spmd(nc, [{f"in_{k}": v for k, v in data.items()}], core_ids=[0])
    return got.results[0]["out"][0:TOKENS].reshape(P, STEPS, D)
```

```python
from contextlib import ExitStack

import concourse.bass as bass
from concourse import mybir

F32 = mybir.dt.float32
F32R = mybir.dt.float32r
I32 = mybir.dt.int32
ALU = mybir.AluOpType
ACT = mybir.ActivationFunctionType
AX = mybir.AxisListType

P = 128
D = 256
DC = D // P
R = 64
T_IMG = 16
STEPS = 48
FEAT = 768
FC = FEAT // P
GS = 4
GROUPS = STEPS // GS
IMG_GROUPS = T_IMG // GS
TOKENS = P * STEPS
E = 8
H = 1024
HC = H // P
TILE = 256
SUB = TILE // P
PAD = TILE
CAP = TOKENS + PAD
LIST_ROWS = E * CAP
ROW = D + 1 + E
DUMP = P
EPS = 1e-5

C_ID, C_TRI, C_INV, C_TOK, C_CAP, C_END = 0, 128, 256, 304, 353, 361
M_Q1, M_K1, M_K2, M_Q2, M_END = 0, 128, 256, 384, 448
W_INV, W_V, W_W, W_A_END = 0, D, D + 2 * R, D + 4 * R
W_Q, W_K, W_QK_END = 0, D, 2 * D
W_O, W_XT, W_UB, W_UT, W_G = 0, D, D + R, D + 2 * R, D + 3 * R
W_BB, W_BT, W_B_END = W_G + E, W_G + E + 1, W_G + E + 2
TB_TILE, TB_PAD, TB_TIE, TB_FULL, TB_END = 0, 9, 17, 18, 26

ds = bass.ds


def waited(eng, sem):
    eng.sem_inc(sem, 1)


def build(nc, xp, txt, tok_wt, tok_b, pos, pack_a, pack_qk, pack_b, alphas, w1, b1t, w2, b2, consts, out):
    lists = nc.dram_tensor("expert_lists", (LIST_ROWS, ROW), F32, kind="Internal").ap()
    out_steps = out[0:TOKENS, :].rearrange("(b t) d -> b t d", t=STEPS)
    w1_v = w1.rearrange("e (c p) h -> e p c h", p=P)
    w2_v = w2.rearrange("e (c p) d -> e p c d", p=P)

    with ExitStack() as common:
        def sb(name, shape, dt=F32, stack=common):
            return stack.enter_context(nc.sbuf_tensor(name, shape, dt))

        def sems(stack, *names):
            return [stack.enter_context(nc.semaphore(n)) for n in names]

        ps = [common.enter_context(nc.psum_tensor(f"bank{i}", [P, 512], F32)) for i in range(8)]
        cst = sb("cst", [P, C_END])
        ident = cst[:, C_ID:C_ID + P]
        table = sb("table", [1, 32], I32)
        w1h, w1l, w2hl = [sb("w1h0", [P, DC, H], F32R)], [sb("w1l0", [P, DC, H], F32R)], [
            sb("w2hl0", [P, HC, 2 * D], F32R)]
        w1raw = sb("w1raw", [P, DC, H])
        w2raw = sb("w2raw", [P, HC, D])
        b1_s = sb("b1_s", [P, E * HC])
        b2_s = sb("b2_s", [P, 2, D])
        (w_raw, w_high, w_low, b1_in, b2_in) = sems(common, "w_raw", "w_high", "w_low", "b1_in", "b2_in")

        def split_low(eng, k):
            eng.tensor_tensor(w1l[k][:], w1raw[:], w1h[k][:].bitcast(F32), ALU.subtract).then_inc(w_low, 1)
            eng.tensor_tensor(w2hl[k][:, :, D:2 * D], w2raw[:], w2hl[k][:, :, 0:D].bitcast(F32),
                              ALU.subtract).then_inc(w_low, 1)

        attention(nc, sb, sems, ps, cst, ident, table, lists, out, out_steps, txt, xp, tok_wt, tok_b, pos,
                  pack_a, pack_qk, pack_b, alphas, w1_v, w2_v, b1t, b2, consts, w1h, w1l, w2hl, w1raw, w2raw,
                  b1_s, b2_s, w_raw, w_high, b1_in, b2_in, split_low)
        experts(nc, sb, sems, ps, ident, table, lists, out, w1_v, w2_v, b2, w1h, w1l, w2hl,
                w1raw, w2raw, b1_s, b2_s, w_raw, w_high, w_low, b1_in, b2_in, split_low)


def attention(nc, sb_, sems, ps, cst, ident, table, lists, out, out_steps, txt, xp, tok_wt, tok_b, pos,
              pack_a, pack_qk, pack_b, alphas, w1_v, w2_v, b1t, b2, consts, w1h, w1l, w2hl, w1raw, w2raw,
              b1_s, b2_s, w_raw, w_high, b1_in, b2_in, split_low):
    with ExitStack() as st:
        def sb(name, shape, dt=F32):
            return sb_(name, shape, dt, st)

        h_all = sb("h_all", [P, STEPS, D])
        posb = h_all[:, 0:T_IMG, :]
        tokb = sb("tokb", [P, D])
        tokwh, tokwl = sb("tokwh", [P, FC, D], F32R), sb("tokwl", [P, FC, D], F32R)
        tokw = w1raw[:].rearrange("p c n -> p (c n)")[:, 0:FC * D].rearrange("p (c n) -> p c n", c=FC)
        w2_flat = w2hl[0][:].rearrange("p c n -> p (c n)")
        n_half = GS // 2 * FC * P
        pxh, pxl = ([v.rearrange("p (s c b) -> p s c b", s=GS // 2, c=FC) for v in (
            w2_flat[:, n_half * i:n_half * i + n_half], w[0][:].rearrange("p c n -> p (c n)")[:, 0:n_half])]
                    for i, w in enumerate((w1h, w1l)))
        px = [sb(f"px{i}", [P, GS, FC, P]) for i in range(2)]
        pa, pqk, pb = (sb(name, [P, DC, n]) for name, n in (("pa", W_A_END), ("pqk", W_QK_END), ("pb", W_B_END)))
        bias_col = sb("bias_col", [P, DC])
        bias_m = sb("bias_m", [P, 2, DC])
        alpha = sb("alpha", [P, 2])
        a_h, a_l = sb("a_h", [P, DC, M_END], F32R), sb("a_l", [P, DC, M_END], F32R)
        g_out = sb("g_out", [P, D])
        g_bias = sb("g_bias", [1, 2, D], F32R)
        ones = sb("ones", [P, P])
        rsq, eps = sb("rsq", [P, 3 * GS]), sb("eps", [P, 3 * GS])
        rstd, shift = ([sb(f"{name}{i}", [P, STEPS]) for i in (1, 2)] for name in ("rstd", "shift"))
        weights = sb("weights", [P, STEPS, E])
        mv1, veps1, nmean1 = sb("mv1", [P, STEPS, 2]), sb("veps1", [P, STEPS]), sb("nmean1", [P, STEPS])
        stats1 = [sb(f"stats1_{k}", [P, GS, 6]) for k in range(2)]
        stats2, mv2, veps2, nmean2 = ([sb(f"{name}{k}", [P, GS] + w) for k in range(2)]
                                      for name, w in (("stats2_", [6]), ("mv2_", [2]), ("veps2_", []), ("nmean2_", [])))
        xn = sb("xn", [P, GS, D])
        inner, uu = (xn[:, i, :].rearrange("p (c n) -> p c n", c=DC) for i in range(2))
        xth, xtl = sb("xth", [P, DC, GS * P], F32R), sb("xtl", [P, DC, GS * P], F32R)
        c1 = sb("c1", [P, GS, P])
        c2 = sb("c2", [P, GS, P])
        inverse = sb("inverse", [R, GS, P])
        factors = [sb(f"factors{i}", [P, GS, P]) for i in range(2)]
        q1_s, q2_s = sb("q1_s", [P, GS, P]), sb("q2_s", [R, GS, P])
        ones_row = sb("ones_row", [1, P], F32R)
        rows = [sb(f"rows{i}", [P, GS, ROW]) for i in range(2)]
        x2t = sb("x2t", [P, DC, GS * P])
        gate = sb("gate", [P, GS, E])
        top8 = sb("top8", [P, GS, E])
        gsub = sb("gsub", [P, GS, E])
        ex = sb("ex", [P, GS, E])
        exs = sb("exs", [P, GS, E])
        exsum, exinv = sb("exsum", [P, GS]), sb("exinv", [P, GS])
        sel = [sb(f"sel{i}", [P, GS + 1, E]) for i in range(2)]
        carry = sb("carry", [P, E])
        dest1 = sb("place1", [P, GS, E])
        rev0, rev = sb("rev_0", [P, GS, E]), sb("rev", [P, GS, E])
        seldest = sb("seldest", [P, STEPS, E])
        last1, first1 = sb("last1", [P, STEPS]), sb("first1", [P, STEPS])
        revmax = sb("revmax", [P, GS])
        dest = [sb(f"dest_{i}", [P, GS, 2], I32) for i in range(2)]
        pad = sb("pad", [P, PAD // P, ROW])
        cnt = sb("cnt", [1, 6, E + 1])
        cnti = sb("cnti", [1, 4, E], I32)
        tie_a, tie_b, tie_dest = (w[:].rearrange("p c n -> p (c n)")[:, 0:STEPS * E] for w in (pa, pqk, pb))
        tie_a, tie_b, tie_dest = (v.rearrange("p (t e) -> p t e", e=E) for v in (tie_a, tie_b, tie_dest.bitcast(I32)))
        tie_row = xn[:].rearrange("p s d -> p (s d)")[:, 0:ROW]
        tie_idx = sb("tie_idx", [P, E], I32)

        bank_w, bank_p, bank_o, bank_g = ps[0:2], ps[2:5], ps[5:7], ps[7]

        (consts_in, setup_in, tok_in, pos_in, pos_rest_in, txt_in, px_in0, px_in1, stored, zero_out) = sems(
            st, "consts_in", "setup_in", "tok_in", "pos_in", "pos_rest_in", "txt_in", "px_in0", "px_in1", "stored",
            "zero_out")
        pads_out = sems(st, "pads_out0", "pads_out1")
        tokw_high, tokw_low, px_high = sems(st, "tokw_high", "tokw_low", "px_high")
        px_low = sems(st, "px_low_vector", "px_low_gpsimd")
        px_in = [px_in0, px_in1]
        (setup_dve, setup_pe, posb_ready, pool_const, pad_ready) = sems(
            st, "setup_dve", "setup_pe", "posb_ready", "pool_const", "pad_ready")
        (tok_done, h_sum, xn_ready, t1_done, xth_ready, xtl_ready, proj_done) = sems(
            st, "tok_done", "h_sum", "xn_ready", "t1_done", "xth_ready", "xtl_ready", "proj_done")
        stat_ready = sems(st, "stat1_ready", "stat2_ready")
        mv_ready = sems(st, "mv1_ready", "mv2_ready")
        ln_half = sems(st, "ln1_half", "ln2_half")
        rstd_ready = sems(st, "rstd1_ready", "rstd2_ready")
        ln_ready = sems(st, "ln1_ready", "ln2_ready")
        (c1_sum, c2_sum, q1_scaled, q2_scaled, q1_used, q2_used, factors_ready, out_done, h2_ready) = sems(
            st, "c1_sum", "c2_sum", "q1_scaled", "q2_scaled", "q1_used", "q2_used", "factors_ready", "out_done",
            "h2_ready")
        (x2_ready, t2_done, x2t_ready, gate_done, gate_copied, top_ready, sel_ready, gsub_ready) = sems(
            st, "x2_ready", "t2_done", "x2t_ready", "gate_done", "gate_copied", "top_ready", "sel_ready",
            "gsub_ready")
        (ex_ready, exs_ready, exsum_ready, exinv_ready, weight_ready) = sems(
            st, "ex_ready", "exs_ready", "exsum_ready", "exinv_ready", "weight_ready")
        (rank_done, dest1_ready, carry_ready, seldest_ready, rev0_ready, rev_ready, revmax_ready,
         last_ready, dest_ready, id_ready) = sems(
            st, "rank_done", "dest1_ready", "carry_ready", "seldest_ready", "rev0_ready", "rev_ready",
            "revmax_ready", "last_ready", "dest_ready", "id_ready")
        scattered = sems(st, "scattered0", "scattered1")
        (cnt_step, table_ready, tie_step, tie_ready, tie_copied, tie_moved, tie_free) = sems(
            st, "cnt_step", "table_ready", "tie_step", "tie_ready", "tie_copied", "tie_moved", "tie_free")
        (pool_waited, dve_waited, act_waited) = sems(st, "pool_waited", "dve_waited", "act_waited")
        INNER_READY, COMBINED_READY = 9, 28

        block = st.enter_context(nc.Block())

        def write_pads(eng, k):
            eng.wait_ge(table_ready, 1)
            for e in range(k, E, 2):
                row = eng.value_load(table[0:1, TB_PAD + e:TB_PAD + e + 1], min_val=e * CAP,
                                     max_val=e * CAP + TOKENS)
                eng.dma_start(lists[ds(row, PAD), :].rearrange("(k p) c -> p k c", p=P),
                              pad[:]).then_inc(pads_out[k], 16)
            eng.wait_ge(pads_out[k], 16 * E // 2)

        @block.sync
        def _(sp):
            sp.dma_start(cst[:], consts).then_inc(consts_in, 16)
            sp.dma_start(pa[:], pack_a.rearrange("(c p) n -> p c n", p=P)).then_inc(setup_in, 16)
            sp.dma_start(pqk[:], pack_qk.rearrange("(c p) n -> p c n", p=P)).then_inc(setup_in, 16)
            sp.dma_start(px[0][:], xp[:, 0:GS]).then_inc(px_in[0], 16)
            sp.dma_start(tokw, tok_wt).then_inc(tok_in, 16)
            sp.dma_start(posb[:, 0:GS, :], pos[0:GS].partition_broadcast(P)).then_inc(pos_in, 16)
            sp.dma_start(tokb[:], tok_b.partition_broadcast(P)).then_inc(pos_in, 16)
            sp.dma_start(px[1][:], xp[:, GS:2 * GS]).then_inc(px_in[1], 16)
            sp.dma_start(posb[:, GS:T_IMG, :], pos[GS:T_IMG].partition_broadcast(P)).then_inc(pos_rest_in, 16)
            for g in range(2, IMG_GROUPS):
                sp.wait_ge(px_low[0], 2 * (g - 1))
                sp.dma_start(px[g % 2][:], xp[:, GS * g:GS * g + GS]).then_inc(px_in[g % 2], 16)
                if g == 2:
                    sp.dma_start(h_all[:, T_IMG:STEPS, :], txt).then_inc(txt_in, 16)
            sp.wait_ge(tokw_low, 1)
            sp.dma_start(w1raw[:], w1_v[0]).then_inc(w_raw, 16)
            sp.dma_start(w2raw[:], w2_v[0]).then_inc(w_raw, 16)
            sp.dma_start(b2_s[:, 0, :], b2[0].partition_broadcast(P)).then_inc(b2_in, 16)
            sp.dma_start(b1_s[:], b1t).then_inc(b1_in, 16)
            sp.wait_ge(pad_ready, 2)
            sp.dma_start(out[TOKENS:TOKENS + DUMP, :], pad[:, 0, 0:D]).then_inc(zero_out, 16)
            with sp.Fori(0, GROUPS) as g:
                sp.wait_ge(h2_ready, 2 * g + 2)
                sp.dma_start(out_steps[:, ds(GS * g, GS), :], h_all[:, ds(GS * g, GS), :]).then_inc(stored, 16)
            write_pads(sp, 0)
            sp.wait_ge(stored, 16 * GROUPS)
            sp.wait_ge(zero_out, 16)

        def px_low_part(eng, nc_eng, g, k):
            eng.wait_ge(px_high, 2 * g + k + 1)
            nc_eng.tensor_tensor(pxl[k], px[g % 2][:, 2 * k:2 * k + 2], pxh[k].bitcast(F32), ALU.subtract
                                 ).then_inc(px_low[g // 2], 1)

        ln1_sets = ((0,), (1,), (4, 5, 6), (2,), (7, 8, 9), (3,), (10, 11))
        ln1_in_tick = ((2, 3), (4, 5), (6,), ())

        def ln1_before(i):
            return sum(len(groups) for groups in ln1_sets[:i])

        def ln1_set(g):
            return next(i for i, groups in enumerate(ln1_sets) if g in groups)

        def pool_ln(pool, n, first, count, before, times, half, neg, var, mean):
            s = ds(GS * first, GS * count)
            pool.wait_ge(mv_ready[n], GS * (before + count))
            nc.gpsimd.tensor_tensor(half, var, eps[:, 0:GS * count], ALU.add).then_inc(ln_half[n], 1)
            nc.gpsimd.tensor_scalar(neg, mean, -1.0, None, ALU.mult).then_inc(ln_half[n], 1)
            pool.wait_ge(ln_half[n], 2 * times + 2)
            nc.gpsimd.tensor_tensor(rstd[n][:, s], half, rsq[:, 0:GS * count], ALU.pow).then_inc(rstd_ready[n], 1)
            pool.wait_ge(rstd_ready[n], times + 1)
            nc.gpsimd.tensor_tensor(shift[n][:, s], neg, rstd[n][:, s], ALU.mult).then_inc(ln_ready[n], count)

        def pool_ln1(pool, i):
            groups = ln1_sets[i]
            s = slice(GS * groups[0], GS * groups[0] + GS * len(groups))
            pool_ln(pool, 0, groups[0], len(groups), ln1_before(i), i, veps1[:, s], nmean1[:, s],
                    mv1[:, s, 1], mv1[:, s, 0])

        def pool_ln2(pool, g, par):
            pool_ln(pool, 1, g, 1, g, g, veps2[par][:], nmean2[par][:], mv2[par][:, :, 1], mv2[par][:, :, 0])

        def pool_scatter(pool, g, par):
            if not isinstance(g, int) or g >= 2:
                pool.wait_ge(scattered[par], 64 * (g - par))
            nc.gpsimd.tensor_copy(rows[par][:, :, D], cst[:, ds(C_TOK + GS * g, GS)]).then_inc(id_ready, 1)
            pool.wait_ge(weight_ready, g + 1)
            waited(pool, pool_waited)
            nc.gpsimd.tensor_copy(rows[par][:, :, D + 1:ROW], weights[:, ds(GS * g, GS), :]).then_inc(id_ready, 1)
            pool.wait_ge(id_ready, 2 * g + 2)
            pool.wait_ge(x2_ready, GS * g + GS)
            pool.wait_ge(dest_ready, g + 1)
            waited(pool, pool_waited)
            for j in range(GS):
                for c in range(2):
                    nc.gpsimd.indirect_dma_start(
                        out=lists, out_offset=bass.IndirectOffsetOnAxis(ap=dest[par][:, j, c:c + 1], axis=0),
                        in_=rows[par][:, j, :], in_offset=None, bounds_check=LIST_ROWS - 1,
                        oob_is_err=False).then_inc(scattered[par], 16)

        @block.gpsimd
        def _(pool):
            nc.gpsimd.memset(ones[:], 1.0).then_inc(pool_const, 1)
            nc.gpsimd.memset(rsq[:], -0.5).then_inc(pool_const, 1)
            nc.gpsimd.memset(eps[:], EPS).then_inc(pool_const, 1)
            nc.gpsimd.memset(sel[0][:, GS, :], 0.0).then_inc(pool_const, 1)
            nc.gpsimd.memset(sel[1][:, GS, :], 0.0).then_inc(pool_const, 1)
            nc.gpsimd.memset(pad[:], 0.0).then_inc(pad_ready, 1)
            pool.wait_ge(pad_ready, 1)
            pool.wait_ge(consts_in, 16)
            nc.gpsimd.tensor_copy(pad[:, :, D], cst[:, C_TOK + STEPS:C_TOK + STEPS + 1]
                                  .to_broadcast([P, PAD // P])).then_inc(pad_ready, 1)
            pool.wait_ge(pos_in, 32)
            pool.wait_ge(pool_const, 5)
            for k in range(4):
                if k == 1:
                    pool.wait_ge(pos_rest_in, 16)
                v = posb[:, GS * k:GS * k + GS, :]
                nc.gpsimd.tensor_tensor(v, v, tokb[:].unsqueeze(1).to_broadcast([P, GS, D]),
                                        ALU.add).then_inc(posb_ready, 1)
            for i in range(2):
                pool_ln1(pool, i)

            def tick(g, par):
                if not isinstance(g, int) or 1 <= g <= GROUPS:
                    pool_ln2(pool, g - 1, 1 - par)
                if isinstance(g, int) and g <= 1:
                    for n, k in ((2, 0), (2, 1)) if g == 0 else ((3, 1),):
                        px_low_part(pool, nc.gpsimd, n, k)
                if not isinstance(g, int) or 2 <= g:
                    pool_scatter(pool, g - 2, par)
                if isinstance(g, int) and g < IMG_GROUPS:
                    for i in ln1_in_tick[g]:
                        if g == 0 and i == ln1_set(2):
                            px_low_part(pool, nc.gpsimd, 3, 0)
                        pool_ln1(pool, i)

            for g in range(IMG_GROUPS):
                tick(g, g % 2)
            with pool.Fori(IMG_GROUPS // 2, GROUPS // 2 - 1) as i:
                tick(2 * i, 0)
                tick(2 * i + 1, 1)
            for g in range(GROUPS - 2, GROUPS + 2):
                tick(g, g % 2)
            for par in range(2):
                pool.wait_ge(scattered[par], 64 * GROUPS)
            pool.wait_ge(table_ready, 1)
            tie = pool.value_load(table[0:1, TB_TIE:TB_TIE + 1], min_val=0, max_val=1)
            with pool.If(tie > 0):
                with pool.Fori(0, STEPS) as t:
                    pool.wait_ge(tie_copied, 4 * t + 4)
                    waited(pool, pool_waited)
                    for e in range(E):
                        nc.gpsimd.indirect_dma_start(
                            out=lists, out_offset=bass.IndirectOffsetOnAxis(ap=tie_idx[:, e:e + 1], axis=0),
                            in_=tie_row, in_offset=None, bounds_check=LIST_ROWS - 1,
                            oob_is_err=False).then_inc(tie_moved, 16)
                    pool.wait_ge(tie_moved, 16 * E * t + 16 * E)
                    pool.sem_inc(tie_free, 1)

        def px_high_part(act, g, k):
            act.wait_ge(px_in[g % 2], 16 * (g // 2 + 1))
            if g >= 1:
                act.wait_ge(tok_done, 2 * (g - 1) + k + 1)
            nc.scalar.copy(pxh[k], px[g % 2][:, 2 * k:2 * k + 2]).then_inc(px_high, 1)

        def act_ln1(act, g, par):
            i = ln1_set(g) if isinstance(g, int) else len(ln1_sets) - 1
            act.wait_ge(ln_ready[0], ln1_before(i + 1))
            if not isinstance(g, int) or g >= 1:
                act.wait_ge(t1_done, 2 * g)
            for j in range(GS):
                t = ds(GS * g + j, 1)
                nc.scalar.activation(xn[:, j, :], h_all[:, t, :].squeeze(1), ACT.Identity,
                                     bias=shift[0][:, t], scale=rstd[0][:, t]).then_inc(xn_ready, 1)

        def act_xt(act, g):
            for k in range(2):
                act.wait_ge(t1_done, 2 * g + k + 1)
                nc.scalar.copy(xth[:, :, 256 * k:256 * k + 256],
                               bank_w[k][:].rearrange("p (c n) -> p c n", c=DC)).then_inc(xth_ready, 1)

        def act_query(act, g, n, bank, dst, scaled, used):
            act.wait_ge(proj_done, 4 * g + n + 1)
            if not isinstance(g, int) or g >= 1:
                act.wait_ge(used, g)
            waited(act, act_waited)
            for j in range(GS):
                m = dst.shape[0]
                nc.scalar.activation(dst[:, j, :], bank[0:m, P * j:P * j + P], ACT.Copy,
                                     scale=cst[0:m, ds(C_INV + GS * g + j, 1)]).then_inc(scaled, 1)

        def act_tail(act, g, par):
            act.wait_ge(ln_ready[1], g + 1)
            if not isinstance(g, int) or g >= 2:
                act.wait_ge(scattered[par], 64 * (g - par))
            for j in range(GS):
                t = ds(GS * g + j, 1)
                nc.scalar.activation(rows[par][:, j, 0:D], h_all[:, t, :].squeeze(1), ACT.Identity,
                                     bias=shift[1][:, t], scale=rstd[1][:, t]).then_inc(x2_ready, 1)

        def act_x2t(act, g):
            if not isinstance(g, int) or g >= 1:
                act.wait_ge(gate_done, g)
            for k in range(2):
                act.wait_ge(t2_done, 2 * g + k + 1)
                nc.scalar.copy(x2t[:, :, 256 * k:256 * k + 256],
                               bank_w[k][:].rearrange("p (c n) -> p c n", c=DC)).then_inc(x2t_ready, 1)

        @block.scalar
        def _(act):
            act.dma_start(pb[:], pack_b.rearrange("(c p) n -> p c n", p=P)).then_inc(setup_in, 16)
            act.dma_start(alpha[:], alphas.partition_broadcast(P)).then_inc(setup_in, 16)
            px_high_part(act, 0, 0)
            px_high_part(act, 0, 1)
            act.wait_ge(tok_in, 16)
            nc.scalar.copy(tokwh[:], tokw).then_inc(tokw_high, 1)
            px_high_part(act, 1, 0)
            px_high_part(act, 1, 1)
            px_high_part(act, 2, 0)
            act_ln1(act, 0, 0)
            act_xt(act, 0)
            px_high_part(act, 2, 1)
            act_ln1(act, 1, 1)

            def tick(g, par):
                if not isinstance(g, int) or g < GROUPS:
                    act_query(act, g, 1, bank_p[1], q1_s, q1_scaled, q1_used)
                if not isinstance(g, int) or g >= 2:
                    act.wait_ge(gsub_ready, g - 1)
                    if not isinstance(g, int) or g >= 3:
                        act.wait_ge(exs_ready, g - 2)
                    nc.scalar.activation(ex[:], gsub[:], ACT.Exp).then_inc(ex_ready, 1)
                if not isinstance(g, int) or 1 <= g <= GROUPS:
                    act_tail(act, g - 1, 1 - par)
                if not isinstance(g, int) or g < GROUPS:
                    act_query(act, g, 3, bank_p[0], q2_s, q2_scaled, q2_used)
                if not isinstance(g, int) or 1 <= g <= GROUPS:
                    act_x2t(act, g - 1)
                if not isinstance(g, int) or g + 1 < GROUPS:
                    act_xt(act, g + 1)
                if isinstance(g, int) and g == 0:
                    for k in range(2):
                        px_high_part(act, 3, k)
                if not isinstance(g, int) or g + 2 < GROUPS:
                    act_ln1(act, g + 2, par)

            for g in range(IMG_GROUPS):
                tick(g, g % 2)
            with act.Fori(IMG_GROUPS // 2, GROUPS // 2 - 1) as i:
                tick(2 * i, 0)
                tick(2 * i + 1, 1)
            for g in range(GROUPS - 2, GROUPS + 2):
                tick(g, g % 2)
            act.wait_ge(w_raw, 32)
            nc.scalar.copy(w1h[0][:], w1raw[:]).then_inc(w_high, 1)
            nc.scalar.copy(w2hl[0][:, :, 0:D], w2raw[:]).then_inc(w_high, 1)
            write_pads(act, 1)

        def dve_stats(dve, n, g, before, stats, mv):
            for j in range(GS):
                nc.vector.bn_stats(stats[:, j, :], h_all[:, ds(GS * g + j, 1), :].squeeze(1)
                                   ).then_inc(stat_ready[n], 1)
            dve.wait_ge(stat_ready[n], GS * before + GS)
            waited(dve, dve_waited)
            for j in range(GS):
                nc.vector.bn_aggr(mv[:, j, :], stats[:, j, :]).then_inc(mv_ready[n], 1)

        def dve_stats1(dve, i):
            for before, g in enumerate(ln1_sets[i], ln1_before(i)):
                if before >= 2:
                    dve.wait_ge(mv_ready[0], GS * (before - 1))
                dve_stats(dve, 0, g, before, stats1[before % 2], mv1[:, GS * g:GS * g + GS, :])

        def dve_tok(dve, g):
            dve.wait_ge(posb_ready, g + 1)
            for k in range(2):
                if g == 0 and k == 1:
                    px_low_part(dve, nc.vector, 1, 0)
                dve.wait_ge(tok_done, 2 * g + k + 1)
                s = slice(GS * g + 2 * k, GS * g + 2 * k + 2)
                nc.vector.tensor_tensor(h_all[:, s, :], bank_w[k][:].rearrange("p (s d) -> p s d", s=2),
                                        posb[:, s, :], ALU.add).then_inc(h_sum, 1)
            if g == 0:
                px_low_part(dve, nc.vector, 1, 1)
            dve.wait_ge(h_sum, 2 * g + 2)

        def dve_xt(dve, g):
            for k in range(2):
                dve.wait_ge(xth_ready, 2 * g + k + 1)
                s = slice(256 * k, 256 * k + 256)
                nc.vector.tensor_tensor(xtl[:, :, s], bank_w[k][:].rearrange("p (c n) -> p c n", c=DC),
                                        xth[:, :, s].bitcast(F32), ALU.subtract).then_inc(xtl_ready, 1)

        def dve_h2(dve, g, par):
            for k in range(2):
                dve.wait_ge(out_done, 2 * g + k + 1)
                v = h_all[:, ds(GS * g + 2 * k, 2), :]
                nc.vector.tensor_tensor(v, bank_o[k][:].rearrange("p (s d) -> p s d", s=2), v, ALU.add
                                        ).then_inc(h2_ready, 1)
            dve.wait_ge(h2_ready, 2 * g + 2)
            waited(dve, dve_waited)
            dve_stats(dve, 1, g, g, stats2[par], mv2[par])

        def psum(n):
            return bank_p[n][:].rearrange("p (s b) -> p s b", s=GS)

        def dve_forward(dve, g, par):
            f = factors[par]
            dve.wait_ge(proj_done, 4 * g + 1)
            for j in range(GS):
                dve.wait_ge(c1_sum, GS * g + j + 1)
                nc.vector.tensor_tensor(c1[:, j, :], psum(0)[:, j, :], c1[:, (j - 1) % GS, :],
                                        ALU.add).then_inc(c1_sum, 1)
            dve.wait_ge(q1_scaled, GS * g + GS)
            dve.wait_ge(c1_sum, GS * g + GS + 1)
            nc.vector.tensor_tensor(f[:], q1_s[:], c1[:], ALU.mult).then_inc(q1_used, 1)

        def dve_inverse_keys(dve, g):
            dve.wait_ge(proj_done, 4 * g + 3)
            for j in range(GS):
                dve.wait_ge(c2_sum, GS * g + j + 1)
                nc.vector.tensor_tensor(c2[:, j, :], psum(2)[:, j, :], c2[:, (j - 1) % GS, :],
                                        ALU.add).then_inc(c2_sum, 1)

        def dve_inverse(dve, g, par):
            f = factors[par]
            dve.wait_ge(q2_scaled, GS * g + GS)
            dve.wait_ge(c2_sum, GS * g + GS + 1)
            nc.vector.tensor_tensor(inverse[:], q2_s[:], c2[0:R, :, :], ALU.mult).then_inc(q2_used, 1)
            dve.wait_ge(q1_used, g + 1)
            nc.vector.tensor_tensor(f[R:P, :, :], c2[R:P, :, :], f[R:P, :, :], ALU.mult).then_inc(factors_ready, 1)
            dve.wait_ge(q2_used, g + 1)
            nc.vector.tensor_tensor(f[0:R, :, :], f[0:R, :, :], inverse[:], ALU.add).then_inc(factors_ready, 1)

        def dve_choose(dve, g, par):
            dve.wait_ge(gate_done, g + 1)
            nc.vector.tensor_copy(gate[:], bank_g[:, 0:GS * E].rearrange("p (s e) -> p s e", s=GS)
                                  ).then_inc(gate_copied, 1)
            dve.wait_ge(gate_copied, g + 1)
            waited(dve, dve_waited)
            for j in range(GS):
                nc.vector.max(top8[:, j, :], gate[:, j, :]).then_inc(top_ready, 1)
            dve.wait_ge(top_ready, GS * g + GS)
            nc.vector.tensor_tensor(sel[par][:, 0:GS, :], gate[:], top8[:, :, 1:2].to_broadcast([P, GS, E]),
                                    ALU.is_ge).then_inc(sel_ready, 1)
            if not isinstance(g, int) or g >= 1:
                dve.wait_ge(ex_ready, g)
            nc.vector.tensor_tensor(gsub[:], gate[:], top8[:, :, 0:1].to_broadcast([P, GS, E]),
                                    ALU.subtract).then_inc(gsub_ready, 1)

        def dve_route(dve, g, par):
            s = ds(GS * g, GS)
            dve.wait_ge(ex_ready, g + 1)
            nc.vector.tensor_tensor(exs[:], ex[:], sel[par][:, 0:GS, :], ALU.mult).then_inc(exs_ready, 1)
            dve.wait_ge(rank_done, g + 1)
            ranks = bank_g[:, 64:64 + (GS + 1) * E].rearrange("p (s e) -> p s e", s=GS + 1)
            dve.wait_ge(carry_ready, g + 1)
            nc.vector.tensor_tensor(dest1[:], ranks[:, 0:GS, :], carry[:].unsqueeze(1).to_broadcast([P, GS, E]),
                                    ALU.add).then_inc(dest1_ready, 1)
            dve.wait_ge(exs_ready, g + 1)
            nc.vector.reduce_sum(exsum[:], exs[:], AX.X).then_inc(exsum_ready, 1)
            dve.wait_ge(dest1_ready, g + 1)
            nc.vector.tensor_tensor(carry[:], ranks[:, GS, :], carry[:], ALU.add).then_inc(carry_ready, 1)
            nc.vector.tensor_tensor(seldest[:, s, :], dest1[:], sel[par][:, 0:GS, :], ALU.mult
                                    ).then_inc(seldest_ready, 1)
            nc.vector.tensor_scalar(rev0[:], dest1[:], -1.0, float(LIST_ROWS + 1), ALU.mult, ALU.add
                                    ).then_inc(rev0_ready, 1)
            dve.wait_ge(exsum_ready, g + 1)
            nc.vector.reciprocal(exinv[:], exsum[:]).then_inc(exinv_ready, 1)
            dve.wait_ge(rev0_ready, g + 1)
            nc.vector.tensor_tensor(rev[:], rev0[:], sel[par][:, 0:GS, :], ALU.mult).then_inc(rev_ready, 1)
            dve.wait_ge(seldest_ready, g + 1)
            nc.vector.reduce_max(last1[:, s], seldest[:, s, :], AX.X).then_inc(last_ready, 1)
            dve.wait_ge(exinv_ready, g + 1)
            nc.vector.scalar_tensor_tensor(weights[:, s, :], exs[:], 1.0 / E,
                                           exinv[:].unsqueeze(2).to_broadcast([P, GS, E]), ALU.mult,
                                           ALU.mult).then_inc(weight_ready, 1)
            dve.wait_ge(rev_ready, g + 1)
            nc.vector.reduce_max(revmax[:], rev[:], AX.X).then_inc(revmax_ready, 1)
            dve.wait_ge(last_ready, g + 1)
            if not isinstance(g, int) or g >= 2:
                dve.wait_ge(scattered[par], 64 * (g - par))
            nc.vector.tensor_scalar(dest[par][:, :, 1], last1[:, s], -1.0, None, ALU.add)
            dve.wait_ge(revmax_ready, g + 1)
            nc.vector.tensor_scalar(first1[:, s], revmax[:], -1.0, float(LIST_ROWS + 1), ALU.mult, ALU.add)
            nc.vector.tensor_scalar(dest[par][:, :, 0], revmax[:], -1.0, float(LIST_ROWS), ALU.mult, ALU.add
                                    ).then_inc(dest_ready, 1)

        @block.vector
        def _(dve):
            n = [0]

            def step(ins):
                n[0] += 1
                ins.then_inc(setup_dve, 1)

            nc.vector.memset(c1[:, GS - 1, :], 0.0).then_inc(c1_sum, 1)
            nc.vector.memset(c2[:, GS - 1, :], 0.0).then_inc(c2_sum, 1)
            dve.wait_ge(consts_in, 16)
            nc.vector.tensor_copy(carry[:], cst[:, C_CAP:C_CAP + E]).then_inc(carry_ready, 1)
            dve.wait_ge(setup_in, 64)
            bias_b, bias_t, xt = pb[:, :, W_BB], pb[:, :, W_BT], pb[:, :, W_XT:W_XT + R]
            step(nc.vector.tensor_copy(uu[:, :, 0:R], pb[:, :, W_UB:W_UB + R]))
            step(nc.vector.tensor_scalar(uu[:, :, R:2 * R], pb[:, :, W_UT:W_UT + R], alpha[:, 1:2], None, ALU.mult))
            step(nc.vector.tensor_scalar(bias_m[:, 0, :], bias_t, alpha[:, 1:2], None, ALU.mult))
            dve.wait_ge(setup_dve, n[0])
            step(nc.vector.tensor_tensor(bias_m[:, 1, :], bias_b, bias_m[:, 0, :], ALU.add))
            dve.wait_ge(setup_dve, n[0])
            step(nc.vector.scalar_tensor_tensor(bias_col[:], bias_b, alpha[:, 0:1],
                                                bias_m[:, 1, :], ALU.mult, ALU.add))
            step(nc.vector.tensor_copy(a_h[:, :, M_K2 + R:M_Q2], xt))
            dve.wait_ge(setup_dve, n[0])
            step(nc.vector.tensor_tensor(a_l[:, :, M_K2 + R:M_Q2], xt, a_h[:, :, M_K2 + R:M_Q2].bitcast(F32),
                                         ALU.subtract))
            dve.wait_ge(pool_const, 5)
            dve.wait_ge(setup_pe, 1)
            step(nc.vector.tensor_copy(ones_row[:], ones[0:1, :]))
            step(nc.vector.tensor_copy(inner, bank_p[0][:, 0:256].rearrange("p (c n) -> p c n", c=DC)))
            assert n[0] == INNER_READY
            for k in range(2):
                px_low_part(dve, nc.vector, 0, k)
            dve.wait_ge(tokw_high, 1)
            nc.vector.tensor_tensor(tokwl[:], tokw, tokwh[:].bitcast(F32), ALU.subtract).then_inc(tokw_low, 1)
            for m in range(DC):
                dve.wait_ge(setup_pe, 2 + m)
                q, k = bank_p[1 + m][:, 0:192], bank_p[1 + m][:, 192:384]
                for dst, src in ((M_Q1, q[:, 0:128]), (M_K1, k[:, 0:128]), (M_K2, k[:, 128:192])):
                    w = src.shape[1]
                    step(nc.vector.tensor_copy(a_h[:, m, dst:dst + w], src))
                    dve.wait_ge(setup_dve, n[0])
                    step(nc.vector.tensor_tensor(a_l[:, m, dst:dst + w], src, a_h[:, m, dst:dst + w].bitcast(F32),
                                                 ALU.subtract))
                step(nc.vector.tensor_scalar(a_h[:, m, M_Q2:M_END], q[:, 128:192], alpha[:, 0:1], None, ALU.mult))
                dve.wait_ge(setup_dve, n[0])
                step(nc.vector.scalar_tensor_tensor(a_l[:, m, M_Q2:M_END], q[:, 128:192], alpha[:, 0:1],
                                                    a_h[:, m, M_Q2:M_END].bitcast(F32), ALU.mult, ALU.subtract))
            dve.wait_ge(setup_pe, 4)
            step(nc.vector.tensor_copy(g_out[:], bank_o[0][:, 0:D]))
            step(nc.vector.tensor_copy(g_bias[:, 0, :], bank_o[1][0:1, 0:D]))
            dve.wait_ge(setup_dve, n[0])
            step(nc.vector.tensor_tensor(g_bias[:, 1, :], bank_o[1][0:1, 0:D], g_bias[:, 0, :].bitcast(F32),
                                         ALU.subtract))
            assert n[0] == COMBINED_READY
            dve_tok(dve, 0)
            dve_stats1(dve, 0)
            dve_tok(dve, 1)
            dve_stats1(dve, 1)
            dve_xt(dve, 0)

            def tick(g, par):
                if not isinstance(g, int) or 1 <= g <= GROUPS:
                    dve_h2(dve, g - 1, 1 - par)
                if not isinstance(g, int) or g >= 2:
                    dve_choose(dve, g - 2, par)
                if not isinstance(g, int) or g < GROUPS:
                    dve_forward(dve, g, par)
                    dve_inverse_keys(dve, g)
                if not isinstance(g, int) or g >= 2:
                    dve_route(dve, g - 2, par)
                if not isinstance(g, int) or g < GROUPS:
                    dve_inverse(dve, g, par)
                if not isinstance(g, int) or g + 1 < GROUPS:
                    dve_xt(dve, g + 1)
                if isinstance(g, int) and g < IMG_GROUPS:
                    for i in ln1_in_tick[g]:
                        if ln1_sets[i][0] < IMG_GROUPS:
                            dve_tok(dve, ln1_sets[i][0])
                        else:
                            dve.wait_ge(txt_in, 16)
                        dve_stats1(dve, i)

            for g in range(IMG_GROUPS):
                tick(g, g % 2)
            with dve.Fori(IMG_GROUPS // 2, GROUPS // 2 - 1) as i:
                tick(2 * i, 0)
                tick(2 * i + 1, 1)
            for g in range(GROUPS - 2, GROUPS + 2):
                tick(g, g % 2)

            m = [0]

            def count(ins):
                m[0] += 1
                ins.then_inc(cnt_step, 1)
                dve.wait_ge(cnt_step, m[0])

            dve.wait_ge(carry_ready, GROUPS + 1)
            nf, nt, tile0, n_half = cnt[:, 0, 0:E], cnt[:, 1, 0:E], cnt[:, 2, :], cnt[:, 3, 0:E]
            count(nc.vector.tensor_tensor(nf, carry[0:1, :], cst[0:1, C_CAP:C_CAP + E], ALU.subtract))
            nc.vector.tensor_scalar(cnti[:, 1, :], nf, float(P - 1), None, ALU.add)
            count(nc.vector.tensor_scalar(cnti[:, 0, :], nf, float(TILE - 1), None, ALU.add))
            nc.vector.tensor_scalar(cnti[:, 3, :], cnti[:, 1, :], P.bit_length() - 1, None, ALU.arith_shift_right)
            count(nc.vector.tensor_scalar(cnti[:, 2, :], cnti[:, 0, :], TILE.bit_length() - 1, None,
                                          ALU.arith_shift_right))
            nc.vector.tensor_copy(n_half, cnti[:, 3, :])
            nc.vector.memset(tile0[:, 0:1], 0.0)
            count(nc.vector.tensor_scalar(nt, cnti[:, 2, :], 1.0, None, ALU.max))
            for e in range(E):
                count(nc.vector.tensor_tensor(tile0[:, e + 1:e + 2], tile0[:, e:e + 1], nt[:, e:e + 1], ALU.add))
            nc.vector.tensor_copy(table[:, TB_TILE:TB_TILE + E + 1], tile0)
            nc.vector.tensor_scalar(table[:, TB_PAD:TB_PAD + E], carry[0:1, :], -1.0, None, ALU.add)
            count(nc.vector.reduce_sum(cnt[:, 4, 0:1], nf, AX.X))
            count(nc.vector.tensor_tensor(cnt[:, 5, 0:E], n_half, nt, ALU.subtract))
            count(nc.vector.tensor_tensor(cnt[:, 5, 0:E], cnt[:, 5, 0:E], tile0[:, 0:E], ALU.add))
            count(nc.vector.scalar_tensor_tensor(table[:, TB_FULL:TB_FULL + E], tile0[:, 0:E], 1.0,
                                                 cnt[:, 5, 0:E], ALU.add, ALU.max))
            nc.vector.tensor_scalar(table[:, TB_TIE:TB_TIE + 1], cnt[:, 4, 0:1], float(2 * TOKENS), None,
                                    ALU.is_gt).then_inc(table_ready, 1)
            dve.wait_ge(w_high, 2)
            split_low(nc.vector, 0)
            dve.wait_ge(table_ready, 1)
            tie = dve.value_load(table[0:1, TB_TIE:TB_TIE + 1], min_val=0, max_val=1)
            with dve.If(tie > 0):
                for a, edge in ((tie_a, first1), (tie_b, last1)):
                    nc.vector.tensor_tensor(a, seldest[:], edge[:].unsqueeze(2).to_broadcast([P, STEPS, E]),
                                            ALU.not_equal).then_inc(tie_step, 1)
                dve.wait_ge(tie_step, 2)
                nc.vector.tensor_tensor(tie_a, tie_a, tie_b, ALU.mult).then_inc(tie_step, 1)
                dve.wait_ge(tie_step, 3)
                nc.vector.tensor_tensor(tie_b, tie_a, seldest[:], ALU.mult).then_inc(tie_step, 1)
                dve.wait_ge(tie_step, 4)
                nc.vector.tensor_scalar(tie_a, tie_b, 0.0, float(LIST_ROWS + 2), ALU.is_equal,
                                        ALU.mult).then_inc(tie_step, 1)
                dve.wait_ge(tie_step, 5)
                nc.vector.scalar_tensor_tensor(tie_dest, tie_b, -1.0, tie_a, ALU.add, ALU.add
                                               ).then_inc(tie_ready, 1)
                dve.wait_ge(tie_ready, 1)
                dve.sem_inc(tie_free, 1)
                with dve.Fori(0, STEPS) as t:
                    dve.wait_ge(tie_free, t + 1)
                    waited(dve, dve_waited)
                    v = ds(t, 1)
                    nc.vector.tensor_scalar(tie_row[:, 0:D], h_all[:, v, :].squeeze(1), rstd[1][:, v], shift[1][:, v],
                                            ALU.mult, ALU.add).then_inc(tie_copied, 1)
                    nc.vector.tensor_copy(tie_row[:, D:D + 1], cst[:, ds(C_TOK + t, 1)]).then_inc(tie_copied, 1)
                    nc.vector.tensor_copy(tie_row[:, D + 1:ROW], weights[:, v, :].squeeze(1)).then_inc(tie_copied, 1)
                    nc.vector.tensor_copy(tie_idx[:], tie_dest[:, v, :].squeeze(1)).then_inc(tie_copied, 1)

        def pe_tok(pe, g):
            pe.wait_ge(tokw_low, 1)
            for k in range(2):
                pe.wait_ge(px_low[g // 2], 2 * (g % 2) + k + 1)
                if g == 1:
                    pe.wait_ge(h_sum, k + 1)
                if g >= 2:
                    pe.wait_ge(xtl_ready, 2 * (g - 1) + k + 1)
                for jj in range(2):
                    for c in range(FC):
                        for i, (x, w) in enumerate(((pxh, tokwh), (pxl, tokwh), (pxh, tokwl))):
                            last = nc.tensor.matmul(bank_w[k][:, D * jj:D * jj + D], x[k][:, jj, c, :], w[:, c, :],
                                                    start=(c == 0 and i == 0), stop=(c == FC - 1 and i == 2))
                last.then_inc(tok_done, 1)

        def pe_t1(pe, g):
            for k in range(2):
                pe.wait_ge(xn_ready, GS * g + 2 * k + 2)
                if isinstance(g, int) and g == 0:
                    pe.wait_ge(h_sum, 2 + k + 1)
                if isinstance(g, int) and g == 1:
                    pe.wait_ge(xtl_ready, k + 1)
                if not isinstance(g, int) or g >= 2:
                    pe.wait_ge(x2t_ready, 2 * (g - 2) + k + 1)
                for jj in range(2):
                    for c in range(DC):
                        last = nc.tensor.transpose(bank_w[k][:, 256 * c + P * jj:256 * c + P * jj + P],
                                                   xn[:, 2 * k + jj, P * c:P * c + P], ident)
                last.then_inc(t1_done, 1)

        def pe_t2(pe, g, par):
            for k in range(2):
                pe.wait_ge(x2_ready, GS * g + 2 * k + 2)
                pe.wait_ge(xtl_ready, 2 * (g + 1) + k + 1 if not isinstance(g, int) or g + 1 < GROUPS
                           else 2 * GROUPS)
                if isinstance(g, int) and g + 2 < IMG_GROUPS:
                    pe.wait_ge(h_sum, 2 * (g + 2) + k + 1)
                for jj in range(2):
                    for c in range(DC):
                        last = nc.tensor.transpose(bank_w[k][:, 256 * c + P * jj:256 * c + P * jj + P],
                                                   rows[par][:, 2 * k + jj, P * c:P * c + P], ident)
                last.then_inc(t2_done, 1)

        def pe_proj(pe, g, which):
            if which[0] == 0:
                pe.wait_ge(xth_ready, 2 * g + 2)
                pe.wait_ge(xtl_ready, 2 * g + 2)
            chunks = ((0, M_K1, P), (1, M_Q1, P), (2, M_K2, P), (0, M_Q2, R))
            freed = ((q2_scaled, GS * g), (q1_scaled, GS * g), (c2_sum, GS * g + 1), (c1_sum, GS * g + GS + 1))
            for n in which:
                bank, col, m = chunks[n]
                if not (isinstance(g, int) and g == 0 and n < 3):
                    pe.wait_ge(*freed[n])
                for c in range(DC):
                    for i, (a, x) in enumerate(((a_h, xth), (a_h, xtl), (a_l, xth))):
                        last = nc.tensor.matmul(bank_p[bank][0:m, :], a[:, c, col:col + m], x[:, c, :],
                                                start=(c == 0 and i == 0), stop=(c == DC - 1 and i == 2))
                last.then_inc(proj_done, 1)

        def pe_out(pe, g, par):
            pe.wait_ge(factors_ready, 2 * g + 2)
            for k in range(2):
                if not isinstance(g, int) or g >= 1:
                    pe.wait_ge(h2_ready, 2 * (g - 1) + k + 1)
                for jj in range(2):
                    o = bank_o[k][:, D * jj:D * jj + D]
                    nc.tensor.matmul(o, factors[par][:, 2 * k + jj, :], g_out[:], start=True, stop=False)
                    for part in range(2):
                        last = nc.tensor.matmul(o, ones_row[:], g_bias[:, part, :],
                                                start=False, stop=(part == 1))
                last.then_inc(out_done, 1)

        def pe_gate(pe, g):
            pe.wait_ge(x2t_ready, 2 * g + 2)
            if not isinstance(g, int) or g >= 1:
                pe.wait_ge(gate_copied, g)
                pe.wait_ge(carry_ready, g + 1)
            for j in range(GS):
                for c in range(DC):
                    last = nc.tensor.matmul(bank_g[:, E * j:E * j + E], x2t[:, c, P * j:P * j + P],
                                            pb[:, c, W_G:W_G + E], start=(c == 0), stop=(c == DC - 1))
            last.then_inc(gate_done, 1)

        def pe_rank(pe, g, par):
            pe.wait_ge(sel_ready, g + 1)
            if not isinstance(g, int) or g >= 1:
                pe.wait_ge(carry_ready, g + 1)
            nc.tensor.matmul(bank_g[:, 64:64 + (GS + 1) * E], cst[:, C_TRI:C_TRI + P],
                             sel[par][:].rearrange("p s e -> p (s e)"), start=True, stop=False)
            for j in range(GS):
                later = GS - j
                last = nc.tensor.matmul(
                    bank_g[:, 64 + (j + 1) * E:64 + (GS + 1) * E].rearrange("p (s e) -> p s e", e=E), ones[:],
                    sel[par][:, j:j + 1, :].to_broadcast([P, later, E]), start=False, stop=(j == GS - 1))
            last.then_inc(rank_done, 1)

        @block.tensor
        def _(pe):
            pe.wait_ge(consts_in, 16)
            pe.wait_ge(pool_const, 5)
            pe.wait_ge(setup_in, 64)
            v_and_w = pa[:, :, W_V:W_A_END].rearrange("p c (k n) -> p c k n", k=2)[:, :, :, 0:R]
            for m in range(DC):
                for c in range(DC):
                    last = nc.tensor.matmul(bank_p[0][:, P * m:P * m + P], pa[:, c, W_INV + P * m:W_INV + P * m + P],
                                            v_and_w[:, c], start=(c == 0), stop=(c == DC - 1))
            last.then_inc(setup_pe, 1)
            pe.wait_ge(setup_dve, INNER_READY)
            for m in range(DC):
                for o, w, own, inv in ((0, W_Q, W_V, R), (192, W_K, W_W, 0)):
                    for o2, rhs in ((o, pa[:, :, own:own + 2 * R]), (o + 2 * R, inner[:, :, inv:inv + R])):
                        for c in range(DC):
                            last = nc.tensor.matmul(bank_p[1 + m][:, o2:o2 + rhs.shape[2]],
                                                    pqk[:, c, w + P * m:w + P * m + P], rhs[:, c, :],
                                                    start=(c == 0), stop=(c == DC - 1))
                last.then_inc(setup_pe, 1)
            for c in range(DC):
                nc.tensor.matmul(bank_o[0][:, 0:D], uu[:, c, :], pb[:, c, W_O:W_O + D], start=(c == 0),
                                 stop=(c == DC - 1))
            for c in range(DC):
                last = nc.tensor.matmul(bank_o[1][0:1, 0:D], bias_col[:, c:c + 1], pb[:, c, W_O:W_O + D],
                                        start=(c == 0), stop=(c == DC - 1))
            last.then_inc(setup_pe, 1)
            pe_tok(pe, 0)
            pe_tok(pe, 1)
            pe_t1(pe, 0)
            pe.wait_ge(setup_dve, COMBINED_READY)

            def tick(g, par):
                if not isinstance(g, int) or 1 <= g <= GROUPS:
                    pe_out(pe, g - 1, 1 - par)
                if not isinstance(g, int) or g < GROUPS:
                    pe_proj(pe, g, (0,))
                if not isinstance(g, int) or g >= 2:
                    pe_gate(pe, g - 2)
                if not isinstance(g, int) or g < GROUPS:
                    pe_proj(pe, g, (1, 2))
                if not isinstance(g, int) or g >= 2:
                    pe_rank(pe, g - 2, par)
                if not isinstance(g, int) or g < GROUPS:
                    pe_proj(pe, g, (3,))
                if not isinstance(g, int) or 1 <= g <= GROUPS:
                    pe_t2(pe, g - 1, 1 - par)
                if not isinstance(g, int) or g + 1 < GROUPS:
                    pe_t1(pe, g + 1)
                if isinstance(g, int) and g + 2 < IMG_GROUPS:
                    pe_tok(pe, g + 2)

            for g in range(IMG_GROUPS):
                tick(g, g % 2)
            with pe.Fori(IMG_GROUPS // 2, GROUPS // 2 - 1) as i:
                tick(2 * i, 0)
                tick(2 * i + 1, 1)
            for g in range(GROUPS - 2, GROUPS + 2):
                tick(g, g % 2)


def experts(nc, sb_, sems, ps, ident, table, lists, out, w1_v, w2_v, b2, w1h, w1l, w2hl,
            w1raw, w2raw, b1_s, b2_s, w_raw, w_high, w_low, b1_in, b2_in, split_low):
    with ExitStack() as st:
        def sb(name, shape, dt=F32):
            return sb_(name, shape, dt, st)

        w1h.append(sb("w1h1", [P, DC, H], F32R))
        w1l.append(sb("w1l1", [P, DC, H], F32R))
        w2hl.append(sb("w2hl1", [P, HC, 2 * D], F32R))
        xe = sb("xe", [P, SUB, ROW])
        xh, xl = sb("xh", [P, DC, TILE], F32R), sb("xl", [P, DC, TILE], F32R)
        hid = sb("hid", [P, HC, TILE])
        hh, hl = sb("hh", [P, HC, TILE], F32R), sb("hl", [P, HC, TILE], F32R)
        meta_n = sb("meta_n", [P, SUB, 1 + E])
        meta_w = sb("meta_w", [P, SUB, 1 + E])
        meta_i = sb("meta_i", [P, SUB], I32)
        y1 = sb("y1", [P, SUB, D])
        y2 = sb("y2", [P, SUB, D])
        y = sb("y", [P, SUB, D])
        bank_s, bank_y, bank_x = ps[0:4], ps[4:6], ps[6]

        (xe_in, transposed, xh_ready, xl_ready, s1_done, hh_ready, hid_ready, hl_ready) = sems(
            st, "xe_in", "transposed", "xh_ready", "xl_ready", "s1_done", "hh_ready", "hid_ready",
            "hl_ready")
        (y_done, y1_ready, y2_ready, y_ready, added, y_free, meta_next, meta_ready, ids_ready) = sems(
            st, "y_done", "y1_ready", "y2_ready", "y_ready", "added", "y_free", "meta_next", "meta_ready", "ids_ready")

        (sp_waited, pool_waited, pe_waited, act_waited, dve_waited) = sems(
            st, "sp_waited", "pool_waited_2", "pe_waited", "act_waited_2", "dve_waited_2")
        block = st.enter_context(nc.Block())
        MAX_TILES = E * (TOKENS // TILE) + E

        def tile_of(eng, e):
            return eng.value_load(table[0:1, ds(TB_TILE + e, 1)], min_val=0, max_val=MAX_TILES)

        def each_expert(eng, tile, head=None, behind_first=None, behind_all=None, halves=False):
            with eng.Fori(0, E // 2) as i:
                for k in range(2):
                    e = 2 * i + k
                    t0 = tile_of(eng, e)
                    t1 = tile_of(eng, e + 1)
                    if head is not None:
                        head(e, k)
                    tile(t0, e, k, t0)
                    if behind_first is not None:
                        behind_first(e, k, t0)
                    full = t1
                    if halves:
                        full = eng.value_load(table[0:1, ds(TB_FULL + e, 1)], min_val=1, max_val=MAX_TILES)
                    with eng.If(full > t0 + 1):
                        with eng.Fori(t0 + 1, full) as t:
                            tile(t, e, k, t0)
                    if halves:
                        with eng.If(t1 > full):
                            tile(full, e, k, t0, subs=1)
                    if behind_all is not None:
                        behind_all(e, k, t0)

        def following(i2):
            return (i2 + 1) % E

        @block.sync
        def _(sp):
            def weights_of_next(e, k, t0):
                sp.wait_ge(w_low, 2 * e + 2)
                n = following(e)
                sp.dma_start(w1raw[:], w1_v[ds(n, 1)].squeeze(0)).then_inc(w_raw, 16)
                sp.dma_start(w2raw[:], w2_v[ds(n, 1)].squeeze(0)).then_inc(w_raw, 16)

            def bias_of_next(e, k, t0):
                sp.wait_ge(b2_in, 16 * e + 16)
                sp.wait_ge(y_free, SUB * t0 + SUB)
                sp.dma_start(b2_s[:, 1 - k, :], b2[ds(following(e), 1)].squeeze(0).partition_broadcast(P)
                             ).then_inc(b2_in, 16)

            def tile(t, e, k, t0):
                sp.wait_ge(transposed, t + 1)
                sp.wait_ge(meta_next, t + 1)
                row = nc.s_assert_within(
                    e * CAP + (t - t0) * TILE, 0, LIST_ROWS - TILE,
                    skip_runtime_bounds_check_because="an expert has at most CAP // TILE tiles")
                sp.dma_start(xe[:], lists[ds(row, TILE), :].rearrange("(s p) c -> p s c", p=P)
                             ).then_inc(xe_in, 16)

            each_expert(sp, tile, behind_first=weights_of_next, behind_all=bias_of_next)
            total = tile_of(sp, E)
            sp.wait_ge(transposed, total + 1)
            sp.wait_ge(meta_next, total + 1)
            sp.dma_start(xe[:], lists[0:TILE, :].rearrange("(s p) c -> p s c", p=P)).then_inc(xe_in, 16)
            sp.wait_ge(xe_in, 16 * total + 16)
            sp.wait_ge(w_raw, 32 * E + 32)
            sp.wait_ge(b2_in, 16 * E + 16)
            waited(sp, sp_waited)

        @block.gpsimd
        def _(pool):
            def use_next(t1):
                pool.wait_ge(meta_next, t1 + 1)
                waited(pool, pool_waited)
                nc.gpsimd.tensor_copy(meta_w[:], meta_n[:]).then_inc(meta_ready, 1)

            def scatter_ids(t1):
                pool.wait_ge(meta_ready, t1)
                waited(pool, pool_waited)
                nc.gpsimd.tensor_copy(meta_i[:], meta_w[:, :, 0]).then_inc(ids_ready, 1)

            pool.sem_inc(y_free, SUB)
            use_next(1)
            scatter_ids(1)

            def split_next(e, k, t0):
                pool.wait_ge(w_high, 2 * e + 4)
                split_low(nc.gpsimd, 1 - k)

            def tile(t, e, k, t0):
                pool.wait_ge(y_ready, SUB * t + SUB)
                pool.wait_ge(ids_ready, t + 1)
                use_next(t + 2)
                for s in range(SUB):
                    nc.gpsimd.indirect_dma_start(
                        out=out, out_offset=bass.IndirectOffsetOnAxis(ap=meta_i[:, s:s + 1], axis=0),
                        in_=y[:, s, :], in_offset=None, bounds_check=TOKENS + DUMP - 1, oob_is_err=True,
                        compute_op=ALU.add).then_inc(added, 16)
                    pool.wait_ge(added, 16 * (SUB * t + s + 1))
                    pool.sem_inc(y_free, 1)
                scatter_ids(t + 2)

            each_expert(pool, tile, behind_first=split_next)

        @block.scalar
        def _(act):
            act.sem_inc(hid_ready, HC)
            def high_x(t1):
                act.wait_ge(transposed, t1 + 1)
                nc.scalar.copy(xh[:], bank_x[:].rearrange("p (c n) -> p c n", c=DC)).then_inc(xh_ready, 1)

            def take_next(t1):
                nc.scalar.copy(meta_n[:], xe[:, :, D:ROW]).then_inc(meta_next, 1)

            act.sem_inc(meta_next, 1)
            high_x(1)
            act.wait_ge(xe_in, 16)
            take_next(1)
            act.wait_ge(b1_in, 16)

            def tile(t, e, k, t0, subs=SUB):
                n = P * subs
                for c in range(HC):
                    if c % 2 == 0:
                        act.wait_ge(s1_done, HC // 2 * t + c // 2 + 1)
                        act.wait_ge(hl_ready, HC // 2 * t + c // 2 + 1)
                        waited(act, act_waited)
                    nc.scalar.activation(hid[:, c, 0:n], bank_s[c // 2][:, TILE * (c % 2):TILE * (c % 2) + n],
                                         ACT.Relu, bias=b1_s[:, ds(e * HC + c, 1)]).then_inc(hid_ready, 1)
                high_x(t + 2)
                act.wait_ge(meta_ready, t + 1)
                act.wait_ge(xe_in, 16 * (t + 2))
                take_next(t + 2)
                for s in range(subs):
                    act.wait_ge(y_done, SUB * t + s + 1)
                    waited(act, act_waited)
                    nc.scalar.activation(y1[:, s, :], bank_y[s][:, D:2 * D], ACT.Copy,
                                         scale=meta_w[:, s, ds(1 + e, 1)]).then_inc(y1_ready, SUB // subs)

            def raise_next(e, k, t0):
                act.wait_ge(w_raw, 32 * e + 64)
                waited(act, act_waited)
                nc.scalar.copy(w2hl[1 - k][:, :, 0:D], w2raw[:]).then_inc(w_high, 1)

            each_expert(act, tile, behind_first=raise_next, halves=True)

        @block.vector
        def _(dve):
            dve.sem_inc(hl_ready, HC // 2)
            dve.sem_inc(y2_ready, SUB)

            def low_x(t1):
                dve.wait_ge(xh_ready, t1)
                nc.vector.tensor_tensor(xl[:], bank_x[:].rearrange("p (c n) -> p c n", c=DC),
                                        xh[:].bitcast(F32), ALU.subtract).then_inc(xl_ready, 1)

            low_x(1)

            def head(e, k):
                dve.wait_ge(b2_in, 16 * e + 16)
                waited(dve, dve_waited)

            def tile(t, e, k, t0, subs=SUB):
                n = P * subs

                def high_hidden(q):
                    v = slice(2 * q, 2 * q + 2)
                    dve.wait_ge(hid_ready, HC * (t + 1) + 2 * q + 2)
                    nc.vector.tensor_copy(hh[:, v, 0:n], hid[:, v, 0:n]).then_inc(hh_ready, 1)

                def low_hidden(q):
                    v = slice(2 * q, 2 * q + 2)
                    dve.wait_ge(hh_ready, HC // 2 * t + q + 1)
                    nc.vector.tensor_tensor(hl[:, v, 0:n], hid[:, v, 0:n], hh[:, v, 0:n].bitcast(F32),
                                            ALU.subtract).then_inc(hl_ready, 1)

                for q in range(HC // 2):
                    high_hidden(q)
                    low_hidden(q)
                low_x(t + 2)
                for s in range(subs):
                    w = meta_w[:, s, ds(1 + e, 1)]
                    dve.wait_ge(y1_ready, SUB * t + s + 1)
                    nc.vector.scalar_tensor_tensor(y2[:, s, :], bank_y[s][:, 0:D], w, y1[:, s, :], ALU.mult,
                                                   ALU.add).then_inc(y2_ready, SUB // subs)
                for s in range(subs):
                    w = meta_w[:, s, ds(1 + e, 1)]
                    dve.wait_ge(y2_ready, SUB * (t + 1) + s + 1)
                    dve.wait_ge(y_free, SUB * t + s + 1)
                    nc.vector.scalar_tensor_tensor(y[:, s, :], b2_s[:, k, :], w, y2[:, s, :], ALU.mult,
                                                   ALU.add).then_inc(y_ready, SUB // subs)

            def raise_next(e, k, t0):
                dve.wait_ge(w_raw, 32 * e + 64)
                nc.vector.tensor_copy(w1h[1 - k][:], w1raw[:]).then_inc(w_high, 1)

            each_expert(dve, tile, head=head, behind_first=raise_next, halves=True)

        @block.tensor
        def _(pe):
            pe.sem_inc(transposed, 1)

            def transpose(t1):
                pe.wait_ge(xe_in, 16 * t1)
                for c in range(DC):
                    for s in range(SUB):
                        last = nc.tensor.transpose(bank_x[:, TILE * c + P * s:TILE * c + P * s + P],
                                                   xe[:, s, P * c:P * c + P], ident)
                last.then_inc(transposed, 1)

            transpose(1)

            def head(e, k):
                pe.wait_ge(w_low, 2 * e + 2)
                waited(pe, pe_waited)

            def tile(t, e, k, t0, subs=SUB):
                n = P * subs
                pe.wait_ge(xh_ready, t + 1)
                pe.wait_ge(xl_ready, t + 1)
                for c in range(HC):
                    if c % 2 == 0:
                        pe.wait_ge(hid_ready, HC * t + c + 2)
                    for d in range(DC):
                        for i, (w, x) in enumerate(((w1h[k], xh), (w1h[k], xl), (w1l[k], xh))):
                            last = nc.tensor.matmul(bank_s[c // 2][:, TILE * (c % 2):TILE * (c % 2) + n],
                                                    w[:, d, P * c:P * c + P], x[:, d, 0:n],
                                                    start=(d == 0 and i == 0), stop=(d == DC - 1 and i == 2))
                    if c % 2 == 1:
                        last.then_inc(s1_done, 1)
                transpose(t + 2)
                for s in range(subs):
                    pe.wait_ge(y2_ready, SUB * t + s + 1)
                    for c in range(HC):
                        if s == 0 and c % 2 == 0:
                            pe.wait_ge(hl_ready, HC // 2 * (t + 1) + c // 2 + 1)
                        nc.tensor.matmul(bank_y[s][:], hh[:, c, P * s:P * s + P], w2hl[k][:, c, :],
                                         start=(c == 0), stop=False)
                        last = nc.tensor.matmul(bank_y[s][:, 0:D], hl[:, c, P * s:P * s + P], w2hl[k][:, c, 0:D],
                                                start=False, stop=(c == HC - 1))
                    last.then_inc(y_done, SUB // subs)

            each_expert(pe, tile, head=head, halves=True)


def kernel(**inputs):
    import numpy as np
    import concourse.bacc as bacc
    from concourse.bass_utils import run_bass_kernel_spmd

    def a(name):
        return np.ascontiguousarray(inputs[name])

    def side_by_side(arrays):
        return np.concatenate([w.reshape(D, -1) for w in arrays], axis=1)

    x = a("x").reshape(P, 3, 4, 16, 4, 16).transpose(2, 4, 1, 3, 5, 0)
    x = x.reshape(T_IMG, FC, P, P).transpose(2, 0, 1, 3)
    consts = np.zeros((P, C_END), np.float32)
    consts[:, C_ID:C_ID + P] = np.eye(P)
    consts[:, C_TRI:C_TRI + P] = np.triu(np.ones((P, P)), 1)
    consts[:R, C_INV:C_INV + STEPS] = 1.0 / np.arange(1, STEPS + 1)
    consts[R:, C_INV:C_INV + STEPS] = 1.0 / np.arange(1, STEPS + 1) ** 2
    consts[:, C_TOK:C_TOK + STEPS] = np.arange(TOKENS).reshape(P, STEPS)
    consts[:, C_TOK + STEPS] = TOKENS + np.arange(P)
    consts[:, C_CAP:C_CAP + E] = np.arange(E) * CAP + 1
    L, A, M = "L0_tok_", "L0_attn_", "L0_ffn_"
    data = {
        "xp": x, "txt": a("txt"),
        "tok_wt": a(L + "W").T.reshape(FC, P, D).transpose(1, 0, 2),
        "tok_b": a(L + "b"), "pos": a(L + "pos_emb"),
        "pack_a": side_by_side(a(A + n) for n in ("Winv", "V_b", "V_t", "W_b", "W_t")),
        "pack_qk": side_by_side(a(A + n) for n in ("WQ", "WK")),
        "pack_b": side_by_side((a(A + "WO").T, a(A + "X_t"), a(A + "U_b"), a(A + "U_t"), a(M + "W_gate"),
                                a(A + "bias_b"), a(A + "bias_t"))),
        "alphas": np.concatenate([a(A + "alpha_bi").reshape(1), a(A + "alpha_tri").reshape(1)]),
        "w1": a(M + "W1"),
        "b1t": a(M + "b1").reshape(E, HC, P).transpose(2, 0, 1).reshape(P, E * HC),
        "w2": a(M + "W2"), "b2": a(M + "b2"), "consts": consts,
    }
    data = {k: np.ascontiguousarray(v) for k, v in data.items()}
    nc = bacc.Bacc("TRN2", target_bir_lowering=False, num_devices=1)
    args = [nc.dram_tensor(f"in_{k}", v.shape, mybir.dt.from_np(v.dtype), kind="ExternalInput").ap()
            for k, v in data.items()]
    out = nc.dram_tensor("out", (TOKENS + DUMP, D), F32, kind="ExternalOutput").ap()
    build(nc, *args, out)
    got = run_bass_kernel_spmd(nc, [{f"in_{k}": v for k, v in data.items()}], core_ids=[0])
    return got.results[0]["out"][0:TOKENS].reshape(P, STEPS, D)
```
